# Optimizing a Trainium2 kernel written in Bass

```python
import numpy as np
import jax
import jax.numpy as jnp

def _softmax(x, axis=-1):
    return jax.nn.softmax(x, axis=axis)

def _gelu(x):
    return jax.nn.gelu(x, approximate=True)

def _silu(x):
    return jax.nn.silu(x)

def _sigmoid(x):
    return jax.nn.sigmoid(x)

def _layernorm(x, axis=-1, eps=1e-05):
    m = jnp.mean(x, axis=axis, keepdims=True)
    v = jnp.var(x, axis=axis, keepdims=True)
    return (x - m) / jnp.sqrt(v + eps)

def _scatter_add(tgt, idx, src, axis=0):
    return tgt.at[idx].add(src)

def _segment_sum(src, seg, n):
    return jax.ops.segment_sum(src, seg, n)
kernel_name = 'mk_decoder_preln_d2_seqx_r8_8f69b0'

def setup_inputs(seed: int=0):
    np.random.seed(seed)
    _w = jnp.asarray

    def _rec_inputs():
        import jax
        import jax.numpy as jnp
        _rk = jax.random.key(seed)
        x = -0.0002928 + 1 * jax.random.normal(jax.random.fold_in(_rk, 1), (32, 128, 128), jnp.float32)
        _lenS = 128 - jax.random.randint(jax.random.fold_in(_rk, 7), (32,), 0, max(1, 128 // 4) + 1, jnp.int32)
        _lenS2 = 128 - jax.random.randint(jax.random.fold_in(_rk, 8), (32,), 0, max(1, 128 // 4) + 1, jnp.int32)
        _ctx_1024P = jax.random.normal(jax.random.fold_in(_rk, 11), (32, 16, 128), jnp.float32)
        _ctx_1024c = jax.random.dirichlet(jax.random.fold_in(_rk, 511), 0.3 * jnp.ones((16,), jnp.float32), (32, 128))
        _ctx_1024t = jnp.einsum('bsk,bkd->bsd', _ctx_1024c, _ctx_1024P)
        _ctx_1024t = _ctx_1024t * jax.lax.rsqrt(jnp.mean(jnp.square(_ctx_1024t)) + 1e-12) * 0.953939
        ctx_1024 = -1.39393e-06 + 0.999914 * (_ctx_1024t + 0.3 * jax.random.normal(jax.random.fold_in(_rk, 611), (32, 128, 128), jnp.float32))
        _validS = jnp.arange(128)[None, :] < _lenS[:, None]
        _validS2 = jnp.arange(128)[None, :] < _lenS2[:, None]
        _causal = jnp.tril(jnp.ones((128, 128), dtype=bool))
        mask_Bx1xSxS2_ff0 = jnp.where(jnp.ones((32, 1, 128, 128), dtype=bool), 0.0, -1000000000.0).astype(jnp.float32)
        mask_Bx1x1xS2_ff0 = jnp.where(jnp.ones((32, 1, 1, 128), dtype=bool), 0.0, -1000000000.0).astype(jnp.float32)
        return (x, ctx_1024, mask_Bx1xSxS2_ff0, mask_Bx1x1xS2_ff0)
    x, ctx_1024, mask_Bx1xSxS2_ff0, mask_Bx1x1xS2_ff0 = _rec_inputs()

    def _L0_attn_setup():
        import jax, jax.numpy as jnp
        import numpy as np
        D_MODEL = 128
        N_HEADS = 16
        D_HIDDEN = 512
        BATCH = 2
        N_CTX = 256

        def _split_heads(t, n_heads):
            B, S, D = t.shape
            return t.reshape(B, S, n_heads, D // n_heads).transpose(0, 2, 1, 3)
        key = jax.random.key(seed)
        ks = jax.random.split(key, 4)
        scale = 0.02
        x = jax.random.normal(ks[0], (BATCH, N_CTX, D_MODEL), dtype=jnp.float32)
        Wk = jax.random.normal(ks[1], (D_MODEL, D_MODEL), dtype=jnp.float32) * scale
        bk = jnp.zeros((D_MODEL,), dtype=jnp.float32)
        Wv = jax.random.normal(ks[2], (D_MODEL, D_HIDDEN), dtype=jnp.float32) * scale
        bv = jnp.zeros((D_HIDDEN,), dtype=jnp.float32)
        Wf = jax.random.normal(ks[3], (D_HIDDEN, D_MODEL), dtype=jnp.float32) * scale
        bf = jnp.zeros((D_MODEL,), dtype=jnp.float32)
        return {'x': x, 'Wk': Wk, 'bk': bk, 'Wv': Wv, 'bv': bv, 'Wf': Wf, 'bf': bf}
    _L0_attn_all = _L0_attn_setup()
    _L0_attn_in = {k: v for k, v in _L0_attn_all.items() if k in ('Wk', 'bk', 'Wv', 'bv', 'Wf', 'bf')}
    del _L0_attn_all

    def _L0_xattn_setup():
        import jax, jax.numpy as jnp
        import numpy as np
        HIDDEN = 128
        NUM_HEADS = 16
        HEAD_DIM = HIDDEN // NUM_HEADS
        B, F, T = (2, 256, 256)
        key = jax.random.key(seed)
        ks = jax.random.split(key, 6)
        return {'query_input': jax.random.normal(ks[0], (B, F, HIDDEN), dtype=jnp.float32), 'source_input': jax.random.normal(ks[1], (B, T, HIDDEN), dtype=jnp.float32), 'bias': jnp.zeros((B, 1, F, T), dtype=jnp.float32), 'wq': jax.random.normal(ks[2], (HIDDEN, NUM_HEADS, HEAD_DIM), dtype=jnp.float32) * (1.0 / np.sqrt(HIDDEN)), 'wk': jax.random.normal(ks[3], (HIDDEN, NUM_HEADS, HEAD_DIM), dtype=jnp.float32) * (1.0 / np.sqrt(HIDDEN)), 'wv': jax.random.normal(ks[4], (HIDDEN, NUM_HEADS, HEAD_DIM), dtype=jnp.float32) * (1.0 / np.sqrt(HIDDEN)), 'wo': jax.random.normal(ks[5], (NUM_HEADS, HEAD_DIM, HIDDEN), dtype=jnp.float32) * (1.0 / np.sqrt(HIDDEN))}
    _L0_xattn_all = _L0_xattn_setup()
    _L0_xattn_in = {k: v for k, v in _L0_xattn_all.items() if k in ('wq', 'wk', 'wv', 'wo')}
    del _L0_xattn_all

    def _L0_ffn_setup():
        import jax, jax.numpy as jnp
        import numpy as np
        D_MODEL = 128
        EXPANSION = 4
        D_HIDDEN = D_MODEL * EXPANSION
        NUM_STAGES = int(np.log2(D_HIDDEN))

        def butterfly(y, weights, dim):
            lead = y.shape[:-1]
            for stage in range(weights.shape[0]):
                s = 2 ** stage
                nb = dim // (2 * s)
                yr = y.reshape(*lead, nb, 2, s)
                a = yr[..., 0, :]
                b = yr[..., 1, :]
                w = weights[stage].reshape(nb, s, 2, 2)
                na = w[..., 0, 0] * a + w[..., 0, 1] * b
                nb2 = w[..., 1, 0] * a + w[..., 1, 1] * b
                y = jnp.stack([na, nb2], axis=-2).reshape(*lead, dim)
            return y
        key = jax.random.key(seed)
        ks = jax.random.split(key, 6)
        B, S = (4, 256)
        x = jax.random.normal(ks[0], (B, S, D_MODEL), jnp.float32)
        W_exp = jax.random.normal(ks[1], (D_MODEL, D_HIDDEN), jnp.float32) * 0.02
        b_exp = jnp.zeros((D_HIDDEN,), jnp.float32)
        up_weights = jax.random.normal(ks[2], (NUM_STAGES, D_HIDDEN // 2, 2, 2), jnp.float32) * 0.02
        up_bias = jnp.zeros((D_HIDDEN,), jnp.float32)
        down_weights = jax.random.normal(ks[3], (NUM_STAGES, D_HIDDEN // 2, 2, 2), jnp.float32) * 0.02
        W_con = jax.random.normal(ks[4], (D_HIDDEN, D_MODEL), jnp.float32) * 0.02
        b_con = jnp.zeros((D_MODEL,), jnp.float32)
        down_bias = jnp.zeros((D_MODEL,), jnp.float32)
        return dict(x=x, W_exp=W_exp, b_exp=b_exp, up_weights=up_weights, up_bias=up_bias, down_weights=down_weights, W_con=W_con, b_con=b_con, down_bias=down_bias)
    _L0_ffn_all = _L0_ffn_setup()
    _L0_ffn_in = {k: v for k, v in _L0_ffn_all.items() if k in ('W_exp', 'b_exp', 'up_weights', 'up_bias', 'down_weights', 'W_con', 'b_con', 'down_bias')}
    del _L0_ffn_all

    def _L1_attn_setup():
        import jax, jax.numpy as jnp
        import numpy as np
        import math
        B, S, E = (2, 256, 128)
        H, DK, DV = (16, 64, 64)

        def _rope(q, k):
            D = q.shape[-1]
            theta = 10000.0 ** (jnp.arange(0, D, 2, dtype=jnp.float32) / D)
            pos = jnp.arange(q.shape[-2], dtype=jnp.float32)
            freqs = pos[:, None] * (1.0 / theta)[None, :]
            emb = jnp.concatenate([freqs, freqs], axis=-1)
            cos = jnp.cos(emb)[None, None]
            sin = jnp.sin(emb)[None, None]

            def rotate(x):
                x1 = x[..., ::2]
                x2 = x[..., 1::2]
                return jnp.stack([-x2, x1], axis=-1).reshape(x.shape)
            return (q * cos + rotate(q) * sin, k * cos + rotate(k) * sin)
        key = jax.random.key(seed)
        ks = jax.random.split(key, 9)
        sE = 1.0 / math.sqrt(E)
        sV = 1.0 / math.sqrt(H * DV)
        return {'x': jax.random.normal(ks[0], (B, S, E), dtype=jnp.float32), 'wq': jax.random.uniform(ks[1], (H * DK, E), jnp.float32, -sE, sE), 'bq': jax.random.uniform(ks[2], (H * DK,), jnp.float32, -sE, sE), 'wk': jax.random.uniform(ks[3], (H * DK, E), jnp.float32, -sE, sE), 'bk': jax.random.uniform(ks[4], (H * DK,), jnp.float32, -sE, sE), 'wv': jax.random.uniform(ks[5], (H * DV, E), jnp.float32, -sE, sE), 'bv': jax.random.uniform(ks[6], (H * DV,), jnp.float32, -sE, sE), 'wo': jax.random.uniform(ks[7], (E, H * DV), jnp.float32, -sV, sV), 'bo': jax.random.uniform(ks[8], (E,), jnp.float32, -sV, sV)}
    _L1_attn_all = _L1_attn_setup()
    _L1_attn_in = {k: v for k, v in _L1_attn_all.items() if k in ('wq', 'bq', 'wk', 'bk', 'wv', 'bv', 'wo', 'bo')}
    del _L1_attn_all

    def _L1_xattn_setup():
        import jax, jax.numpy as jnp
        import numpy as np
        B, T, D, H = (2, 256, 128, 16)
        DH = D // H

        def _heads(x):
            b, t, _ = x.shape
            return x.reshape(b, t, H, DH).transpose(0, 2, 1, 3)
        key = jax.random.key(seed)
        ks = jax.random.split(key, 8)
        s = 0.02
        return {'query_states': jax.random.normal(ks[0], (B, T, D), jnp.float32), 'key_states': jax.random.normal(ks[1], (B, T, D), jnp.float32), 'attention_mask': jnp.zeros((B, 1, 1, T), jnp.float32), 'Wq': jax.random.normal(ks[2], (D, D), jnp.float32) * s, 'bq': jnp.zeros((D,), jnp.float32), 'Wk': jax.random.normal(ks[3], (D, D), jnp.float32) * s, 'bk': jnp.zeros((D,), jnp.float32), 'Wv': jax.random.normal(ks[4], (D, D), jnp.float32) * s, 'bv': jnp.zeros((D,), jnp.float32), 'mask_future': 0}
    _L1_xattn_all = _L1_xattn_setup()
    _L1_xattn_in = {k: v for k, v in _L1_xattn_all.items() if k in ('Wq', 'bq', 'Wk', 'bk', 'Wv', 'bv')}
    del _L1_xattn_all

    def _L1_ffn_setup():
        import jax, jax.numpy as jnp
        import numpy as np
        D_MODEL = 128
        H_SHARED = 256
        H_ROUTED = 128
        N_EXPERTS = 8
        TOP_K = 2
        key = jax.random.key(seed)
        ks = jax.random.split(key, 8)
        B, T = (2, 256)
        sc_d = 1.0 / np.sqrt(D_MODEL)
        sc_hs = 1.0 / np.sqrt(H_SHARED)
        sc_hr = 1.0 / np.sqrt(H_ROUTED)
        return {'x': jax.random.normal(ks[0], (B, T, D_MODEL), dtype=jnp.float32), 'router_w': jax.random.normal(ks[1], (N_EXPERTS, D_MODEL), dtype=jnp.float32) * sc_d, 'router_bias': jnp.zeros((N_EXPERTS,), dtype=jnp.float32), 'sw1': jax.random.normal(ks[2], (D_MODEL, H_SHARED), dtype=jnp.float32) * sc_d, 'sw3': jax.random.normal(ks[3], (D_MODEL, H_SHARED), dtype=jnp.float32) * sc_d, 'sw2': jax.random.normal(ks[4], (H_SHARED, D_MODEL), dtype=jnp.float32) * sc_hs, 'ew1': jax.random.normal(ks[5], (N_EXPERTS, D_MODEL, H_ROUTED), dtype=jnp.float32) * sc_d, 'ew2': jax.random.normal(ks[6], (N_EXPERTS, H_ROUTED, D_MODEL), dtype=jnp.float32) * sc_hr}
    _L1_ffn_all = _L1_ffn_setup()
    _L1_ffn_in = {k: v for k, v in _L1_ffn_all.items() if k in ('router_w', 'router_bias', 'sw1', 'sw3', 'sw2', 'ew1', 'ew2')}
    del _L1_ffn_all
    return {'x': x, 'ctx_1024': ctx_1024, 'mask_Bx1xSxS2_ff0': mask_Bx1xSxS2_ff0, 'mask_Bx1x1xS2_ff0': mask_Bx1x1xS2_ff0, 'L0_attn_Wk': _L0_attn_in['Wk'], 'L0_attn_bk': _L0_attn_in['bk'], 'L0_attn_Wv': _L0_attn_in['Wv'], 'L0_attn_bv': _L0_attn_in['bv'], 'L0_attn_Wf': _L0_attn_in['Wf'], 'L0_attn_bf': _L0_attn_in['bf'], 'L0_xattn_wq': _L0_xattn_in['wq'], 'L0_xattn_wk': _L0_xattn_in['wk'], 'L0_xattn_wv': _L0_xattn_in['wv'], 'L0_xattn_wo': _L0_xattn_in['wo'], 'L0_ffn_W_exp': _L0_ffn_in['W_exp'], 'L0_ffn_b_exp': _L0_ffn_in['b_exp'], 'L0_ffn_up_weights': _L0_ffn_in['up_weights'], 'L0_ffn_up_bias': _L0_ffn_in['up_bias'], 'L0_ffn_down_weights': _L0_ffn_in['down_weights'], 'L0_ffn_W_con': _L0_ffn_in['W_con'], 'L0_ffn_b_con': _L0_ffn_in['b_con'], 'L0_ffn_down_bias': _L0_ffn_in['down_bias'], 'L1_attn_wq': _L1_attn_in['wq'], 'L1_attn_bq': _L1_attn_in['bq'], 'L1_attn_wk': _L1_attn_in['wk'], 'L1_attn_bk': _L1_attn_in['bk'], 'L1_attn_wv': _L1_attn_in['wv'], 'L1_attn_bv': _L1_attn_in['bv'], 'L1_attn_wo': _L1_attn_in['wo'], 'L1_attn_bo': _L1_attn_in['bo'], 'L1_xattn_Wq': _L1_xattn_in['Wq'], 'L1_xattn_bq': _L1_xattn_in['bq'], 'L1_xattn_Wk': _L1_xattn_in['Wk'], 'L1_xattn_bk': _L1_xattn_in['bk'], 'L1_xattn_Wv': _L1_xattn_in['Wv'], 'L1_xattn_bv': _L1_xattn_in['bv'], 'L1_ffn_router_w': _L1_ffn_in['router_w'], 'L1_ffn_router_bias': _L1_ffn_in['router_bias'], 'L1_ffn_sw1': _L1_ffn_in['sw1'], 'L1_ffn_sw3': _L1_ffn_in['sw3'], 'L1_ffn_sw2': _L1_ffn_in['sw2'], 'L1_ffn_ew1': _L1_ffn_in['ew1'], 'L1_ffn_ew2': _L1_ffn_in['ew2']}

def reference(x, ctx_1024, mask_Bx1xSxS2_ff0, mask_Bx1x1xS2_ff0, L0_attn_Wk, L0_attn_bk, L0_attn_Wv, L0_attn_bv, L0_attn_Wf, L0_attn_bf, L0_xattn_wq, L0_xattn_wk, L0_xattn_wv, L0_xattn_wo, L0_ffn_W_exp, L0_ffn_b_exp, L0_ffn_up_weights, L0_ffn_up_bias, L0_ffn_down_weights, L0_ffn_W_con, L0_ffn_b_con, L0_ffn_down_bias, L1_attn_wq, L1_attn_bq, L1_attn_wk, L1_attn_bk, L1_attn_wv, L1_attn_bv, L1_attn_wo, L1_attn_bo, L1_xattn_Wq, L1_xattn_bq, L1_xattn_Wk, L1_xattn_bk, L1_xattn_Wv, L1_xattn_bv, L1_ffn_router_w, L1_ffn_router_bias, L1_ffn_sw1, L1_ffn_sw3, L1_ffn_sw2, L1_ffn_ew1, L1_ffn_ew2):
    import jax
    import jax.numpy as jnp

    def _L0_attn_ref(x, Wk, bk, Wv, bv, Wf, bf):
        import jax, jax.numpy as jnp
        import numpy as np
        D_MODEL = 128
        N_HEADS = 16
        D_HIDDEN = 512
        BATCH = 2
        N_CTX = 256

        def _split_heads(t, n_heads):
            B, S, D = t.shape
            return t.reshape(B, S, n_heads, D // n_heads).transpose(0, 2, 1, 3)
        B, S, D = x.shape
        H = N_HEADS
        Q = _split_heads(x, H)
        K = _split_heads(x @ Wk + bk, H)
        V = _split_heads(x @ Wv + bv, H)
        causal = jnp.tril(jnp.ones((S, S), dtype=bool))
        mask = jnp.where(causal, 0.0, -jnp.inf).astype(x.dtype)
        scores = jnp.einsum('bhqd,bhkd->bhqk', Q, K) + mask
        attn = jax.nn.softmax(scores, axis=-1)
        o = jnp.einsum('bhqk,bhkd->bhqd', attn, V)
        o = o.transpose(0, 2, 1, 3).reshape(B, S, -1)
        return x + jax.nn.gelu(o, approximate=False) @ Wf + bf

    def _L0_xattn_ref(query_input, source_input, bias, wq, wk, wv, wo):
        import jax, jax.numpy as jnp
        import numpy as np
        HIDDEN = 128
        NUM_HEADS = 16
        HEAD_DIM = HIDDEN // NUM_HEADS
        B, F, T = (2, 256, 256)
        q = jnp.einsum('bfd,dnh->bfnh', query_input, wq)
        k = jnp.einsum('btd,dnh->btnh', source_input, wk)
        v = jnp.einsum('btd,dnh->btnh', source_input, wv)
        q = q * HEAD_DIM ** (-0.5)
        logits = jnp.einsum('btnh,bfnh->bnft', k, q) + bias
        weights = jax.nn.softmax(logits, axis=-1)
        attn = jnp.einsum('bnft,btnh->bfnh', weights, v)
        return jnp.einsum('bfnh,nhd->bfd', attn, wo)

    def _L0_ffn_ref(x, W_exp, b_exp, up_weights, up_bias, down_weights, W_con, b_con, down_bias):
        import jax, jax.numpy as jnp
        import numpy as np
        D_MODEL = 128
        EXPANSION = 4
        D_HIDDEN = D_MODEL * EXPANSION
        NUM_STAGES = int(np.log2(D_HIDDEN))

        def butterfly(y, weights, dim):
            lead = y.shape[:-1]
            for stage in range(weights.shape[0]):
                s = 2 ** stage
                nb = dim // (2 * s)
                yr = y.reshape(*lead, nb, 2, s)
                a = yr[..., 0, :]
                b = yr[..., 1, :]
                w = weights[stage].reshape(nb, s, 2, 2)
                na = w[..., 0, 0] * a + w[..., 0, 1] * b
                nb2 = w[..., 1, 0] * a + w[..., 1, 1] * b
                y = jnp.stack([na, nb2], axis=-2).reshape(*lead, dim)
            return y
        h = jnp.einsum('bsd,dh->bsh', x, W_exp) + b_exp
        h = butterfly(h, up_weights, D_HIDDEN)
        h = jax.nn.gelu(h + up_bias, approximate=False)
        h = butterfly(h, down_weights, D_HIDDEN)
        y = jnp.einsum('bsh,hd->bsd', h, W_con) + b_con
        return y + down_bias

    def _L1_attn_ref(x, wq, bq, wk, bk, wv, bv, wo, bo):
        import jax, jax.numpy as jnp
        import numpy as np
        import math
        B, S, E = (2, 256, 128)
        H, DK, DV = (16, 64, 64)

        def _rope(q, k):
            D = q.shape[-1]
            theta = 10000.0 ** (jnp.arange(0, D, 2, dtype=jnp.float32) / D)
            pos = jnp.arange(q.shape[-2], dtype=jnp.float32)
            freqs = pos[:, None] * (1.0 / theta)[None, :]
            emb = jnp.concatenate([freqs, freqs], axis=-1)
            cos = jnp.cos(emb)[None, None]
            sin = jnp.sin(emb)[None, None]

            def rotate(x):
                x1 = x[..., ::2]
                x2 = x[..., 1::2]
                return jnp.stack([-x2, x1], axis=-1).reshape(x.shape)
            return (q * cos + rotate(q) * sin, k * cos + rotate(k) * sin)
        Bx, Sx, Ex = x.shape
        q = (x @ wq.T + bq).reshape(Bx, Sx, H, DK).transpose(0, 2, 1, 3)
        k = (x @ wk.T + bk).reshape(Bx, Sx, H, DK).transpose(0, 2, 1, 3)
        v = (x @ wv.T + bv).reshape(Bx, Sx, H, DV).transpose(0, 2, 1, 3)
        q, k = _rope(q, k)
        scores = jnp.einsum('bhqd,bhkd->bhqk', q, k)
        causal = jnp.triu(jnp.ones((Sx, Sx), dtype=bool), k=1)
        scores = jnp.where(causal[None, None], -jnp.inf, scores)
        attn = jax.nn.softmax(scores / math.sqrt(DK), axis=-1)
        out = jnp.einsum('bhqk,bhkd->bhqd', attn, v)
        out = out.transpose(0, 2, 1, 3).reshape(Bx, Sx, H * DV)
        return out @ wo.T + bo

    def _L1_xattn_ref(query_states, key_states, attention_mask, Wq, bq, Wk, bk, Wv, bv, mask_future):
        import jax, jax.numpy as jnp
        import numpy as np
        B, T, D, H = (2, 256, 128, 16)
        DH = D // H

        def _heads(x):
            b, t, _ = x.shape
            return x.reshape(b, t, H, DH).transpose(0, 2, 1, 3)
        q = _heads(query_states @ Wq + bq)
        k = _heads(key_states @ Wk + bk)
        v = _heads(key_states @ Wv + bv)
        scale = 1.0 / jnp.sqrt(jnp.asarray(DH, jnp.float32))
        scores = jnp.einsum('bhqd,bhkd->bhqk', q, k) * scale + attention_mask
        if mask_future:
            t = scores.shape[-1]
            triu = jnp.triu(jnp.ones((t, t), bool))
            scores = jnp.where(triu, -jnp.inf, scores)
        probs = jax.nn.softmax(scores, axis=-1)
        ctx = jnp.einsum('bhqk,bhkd->bhqd', probs, v)
        b, _, t, _ = ctx.shape
        return ctx.transpose(0, 2, 1, 3).reshape(b, t, H * DH)

    def _L1_ffn_ref(x, router_w, router_bias, sw1, sw3, sw2, ew1, ew2):
        import jax, jax.numpy as jnp
        import numpy as np
        D_MODEL = 128
        H_SHARED = 256
        H_ROUTED = 128
        N_EXPERTS = 8
        TOP_K = 2
        B, T, C = x.shape
        xf = x.reshape(-1, C)
        shared_out = jax.nn.silu(xf @ sw1) * (xf @ sw3) @ sw2
        s = jax.nn.sigmoid((xf @ router_w.T).astype(jnp.float32))
        sel_scores = s + router_bias.astype(jnp.float32)
        _, topk_idx = jax.lax.top_k(sel_scores, TOP_K)
        s_sel = jnp.take_along_axis(s, topk_idx, axis=1)
        denom = s_sel.sum(axis=1, keepdims=True)
        gates = jnp.where(denom > 1e-09, s_sel / (denom + 1e-09), 1.0 / TOP_K).astype(x.dtype)
        one_hot = jax.nn.one_hot(topk_idx, N_EXPERTS, dtype=x.dtype)
        comb = jnp.einsum('nke,nk->ne', one_hot, gates)
        h = jax.nn.gelu(jnp.einsum('nd,edh->neh', xf, ew1), approximate=False)
        y = jnp.einsum('neh,ehd->ned', h, ew2)
        routed_out = jnp.einsum('ned,ne->nd', y, comb)
        return (shared_out + routed_out).reshape(B, T, C)
    x = x + _L0_attn_ref(_layernorm(x, axis=-1), L0_attn_Wk, L0_attn_bk, L0_attn_Wv, L0_attn_bv, L0_attn_Wf, L0_attn_bf)
    x = x + _L0_xattn_ref(_layernorm(x, axis=-1), ctx_1024, mask_Bx1xSxS2_ff0, L0_xattn_wq, L0_xattn_wk, L0_xattn_wv, L0_xattn_wo)
    x = x + _L0_ffn_ref(_layernorm(x, axis=-1), L0_ffn_W_exp, L0_ffn_b_exp, L0_ffn_up_weights, L0_ffn_up_bias, L0_ffn_down_weights, L0_ffn_W_con, L0_ffn_b_con, L0_ffn_down_bias)
    x = x + _L1_attn_ref(_layernorm(x, axis=-1), L1_attn_wq, L1_attn_bq, L1_attn_wk, L1_attn_bk, L1_attn_wv, L1_attn_bv, L1_attn_wo, L1_attn_bo)
    x = x + _L1_xattn_ref(_layernorm(x, axis=-1), ctx_1024, mask_Bx1x1xS2_ff0, L1_xattn_Wq, L1_xattn_bq, L1_xattn_Wk, L1_xattn_bk, L1_xattn_Wv, L1_xattn_bv, 0)
    x = x + _L1_ffn_ref(_layernorm(x, axis=-1), L1_ffn_router_w, L1_ffn_router_bias, L1_ffn_sw1, L1_ffn_sw3, L1_ffn_sw2, L1_ffn_ew1, L1_ffn_ew2)
    return x

_drawn_inputs = setup_inputs


def setup_inputs(seed=0):
    import zlib

    import numpy as np

    out = dict(_drawn_inputs(seed))
    spreads = {'L0_attn_bk': (0.0, 0.8),
     'L0_attn_bv': (0.0, 0.342),
     'L0_attn_bf': (0.0, 0.1),
     'L0_ffn_b_exp': (0.0, 0.1),
     'L0_ffn_up_bias': (0.0, 0.1),
     'L0_ffn_b_con': (0.0, 0.1),
     'L0_ffn_down_bias': (0.0, 0.1),
     'L1_xattn_bq': (0.0, 0.8),
     'L1_xattn_bk': (0.0, 0.8),
     'L1_xattn_bv': (0.0, 0.1),
     'L1_ffn_router_bias': (0.0, 0.1)}
    factors = {'L0_attn_Wk': 5.56,
     'L0_attn_Wv': 4.232,
     'L0_attn_Wf': 2.804,
     'L1_attn_wq': 3.033,
     'L1_attn_bq': 8.0,
     'L1_attn_wk': 3.013,
     'L1_attn_bk': 8.0,
     'L1_attn_bo': 3.123,
     'L1_xattn_Wq': 8.0,
     'L1_xattn_Wk': 8.0}
    for name, (base, spread) in spreads.items():
        noise = np.random.default_rng([zlib.crc32(name.encode()), seed]).standard_normal(out[name].shape)
        drawn = base * np.exp(spread * noise) if base else spread * noise
        out[name] = jnp.asarray(drawn.astype(out[name].dtype))
    for name, factor in factors.items():
        out[name] = (out[name] * factor).astype(out[name].dtype)
    return out
```

```python
from contextlib import ExitStack, contextmanager

import numpy as np

import concourse.bass as bass
from concourse import mybir

ALU = mybir.AluOpType
ACT = mybir.ActivationFunctionType
AX = mybir.AxisListType
F32 = mybir.dt.float32
BF16 = mybir.dt.bfloat16

P = 128
B = 32
S = 128
D = 128
H = 16
DH = D // H
NP = B // 2
W2 = 2 * S
G = 4
NG = H // G
FH = 512
NJ = FH // P
HD1 = 64
J1 = H * HD1 // P
NE = 8
SH = 256
SLOT = 32
MAIN = 96
MASKED = -1e30
PEEL = 4
EPS = 1e-5


@contextmanager
def phase_semaphores(nc, prefix):
    taken = []

    def sem(name):
        taken.append(nc.alloc_semaphore(name=prefix + name))
        return taken[-1]
    yield sem
    nc.clear_and_free_semaphores(taken)
    nc.all_engine_barrier()


def wait(eng, sem, value):
    if isinstance(value, int) and value <= 0:
        return
    eng.wait_ge(sem, value)


def wait_alone(eng, passed, sem, value):
    wait(eng, sem, value)
    eng.sem_inc(passed, 1)


def of_parity(n, parity, each):
    return (n - parity) * (each // 2) + each


def run_steps(eng, step, depth):
    def exists(n):
        return 0 <= n < NP
    for t in range(PEEL):
        step(t, t % 2, exists)
    with eng.Fori(PEEL // 2, NP // 2) as i:
        step(i * 2, 0, lambda n: True)
        step(i * 2 + 1, 1, lambda n: True)
    for t in range(NP, NP + depth):
        step(t, t % 2, exists)


def ln_scale_dve(dve, v, ln):
    var = v["moments"][:, :, 1]
    dve.tensor_scalar(v["vareps"][:], var, EPS, None, ALU.add).then_inc(ln["var_ready"], 1)
    dve.wait_ge(ln["root_ready"], 1)
    dve.reciprocal(v["rstd0"][:], v["root"][:]).then_inc(ln["chain"], 1)
    dve.wait_ge(ln["chain"], 1)
    dve.tensor_tensor(v["newton"][:], v["rstd0"][:], v["rstd0"][:], ALU.mult).then_inc(ln["chain"], 1)
    dve.wait_ge(ln["chain"], 2)
    dve.tensor_tensor(v["newton"][:], v["newton"][:], v["vareps"][:], ALU.mult).then_inc(ln["chain"], 1)
    dve.wait_ge(ln["chain"], 3)
    dve.tensor_scalar(v["newton"][:], v["newton"][:], -0.5, 1.5, ALU.mult, ALU.add).then_inc(ln["chain"], 1)
    dve.wait_ge(ln["chain"], 4)
    dve.tensor_tensor(v["rstd"][:], v["rstd0"][:], v["newton"][:], ALU.mult).then_inc(ln["chain"], 1)
    dve.wait_ge(ln["chain"], 5)
    dve.scalar_tensor_tensor(v["shift"][:], v["moments"][:, :, 0], -1.0, v["rstd"][:], ALU.mult,
                             ALU.mult).then_inc(ln["chain"], 1)
    dve.wait_ge(ln["chain"], 6)


def ln_scale_act(act, v, ln):
    act.wait_ge(ln["var_ready"], 1)
    act.activation(v["root"][:], v["vareps"][:], ACT.Sqrt).then_inc(ln["root_ready"], 1)


def apply_ln(dve, v, out, b, sem):
    dve.tensor_scalar(out, v["x"][:, bass.ds(b, 1), :], v["rstd"][:, bass.ds(b, 1)],
                      v["shift"][:, bass.ds(b, 1)], ALU.mult, ALU.add).then_inc(sem, 1)


UPDATES = 6


def update_x(dve, v, n, add, passed, upd):
    base = UPDATES * n
    wait(dve, upd, base)
    xs = v["x"][:, bass.ds(n * 2, 2), :]
    dve.tensor_tensor(xs, xs, add, ALU.add).then_inc(upd, 1)
    for b in range(2):
        wait_alone(dve, passed, upd, base + 1)
        dve.bn_stats(v["stats"][:, b, :], v["x"][:, bass.ds(n * 2 + b, 1), :]).then_inc(upd, 1)
    for b in range(2):
        wait_alone(dve, passed, upd, base + 2 + b)
        dve.bn_aggr(v["aggr"][:, b, :], v["stats"][:, b, :]).then_inc(upd, 1)
    dve.wait_ge(upd, base + 5)
    dve.tensor_copy(v["moments"][:, bass.ds(n * 2, 2), :], v["aggr"][:]).then_inc(upd, 1)


def setup_phase(nc, a, v):
    with ExitStack() as c:
        sem = c.enter_context(phase_semaphores(nc, "setup_"))
        passed = {eng: sem("passed_" + eng) for eng in ("dve", "pool", "sp")}
        rw = c.enter_context(nc.sbuf_tensor("rw", [NE, D], F32))
        stats = c.enter_context(nc.sbuf_tensor("xstats", [P, B, 6], F32))
        maskrow = c.enter_context(nc.sbuf_tensor("maskrow", [B, 4, S], F32))
        maskpart = c.enter_context(nc.sbuf_tensor("maskpart", [B, 3, S], BF16))
        bank = c.enter_context(nc.psum_tensor("router_bank", [P, 512], F32))
        x_loaded = [sem(f"x_loaded{i}") for i in range(4)]
        small_loaded = sem("small_loaded")
        ident_zero, ident_ready, masks_zero, masks_ready = (sem("ident_zero"), sem("ident_ready"),
                                                            sem("masks_zero"), sem("masks_ready"))
        consts_ready = sem("consts_ready")
        turned = sem("turned")
        stat_ready, mask_chain, mask_stored = sem("stat_ready"), sem("mask_chain"), sem("mask_stored")
        small = []
        for name in ["L0_attn_Wk", "L0_attn_Wv", "L1_xattn_Wq", "L1_xattn_Wk", "L1_xattn_Wv",
                     "L1_ffn_sw1", "L1_ffn_sw3", "L0_ffn_W_exp"]:
            small.append((v[name][:], a[name]))
        for name in ["L0_xattn_wq", "L0_xattn_wk", "L0_xattn_wv"]:
            small.append((v[name][:], a[name].rearrange("d n h -> d (n h)")))
        small.append((v["L0_xattn_wo"][:], a["L0_xattn_wo"].rearrange("n h d -> (n h) d")))
        small.append((v["L0_attn_Wf"][:], a["L0_attn_Wf"].rearrange("(j p) d -> p j d", p=P)))
        small.append((v["L1_ffn_sw2"][:], a["L1_ffn_sw2"].rearrange("(j p) d -> p j d", p=P)))
        small.append((rw[:], a["L1_ffn_router_w"]))
        small.append((v["rope_cos"][:], a["rope_cos"]))
        small.append((v["rope_sin"][:], a["rope_sin"]))
        small.append((maskrow[:, 0, :], a["mask_Bx1x1xS2_ff0"].rearrange("b o t k -> b (o t k)")))
        for name in ["L0_attn_bk", "L1_xattn_bq", "L1_xattn_bk"]:
            small.append((v[name][:], a[name].rearrange("(p o) -> p o", o=1)))
        for name in ["L0_attn_bv", "L0_ffn_up_bias"]:
            small.append((v[name][:], a[name].rearrange("(j p) -> p j", p=P)))
        for name in ["L0_attn_bf", "L1_xattn_bv", "L1_attn_bo", "L0_ffn_b_con", "L0_ffn_down_bias"]:
            small.append((v[name][:], a[name].rearrange("(o d) -> o d", o=1).to_broadcast([P, D])))
        small.append((v["L1_ffn_router_bias"][:],
                      a["L1_ffn_router_bias"].rearrange("(o d) -> o d", o=1).to_broadcast([P, NE])))

        block = c.enter_context(nc.Block())

        @block.sync
        def _(sp):
            xt = a["x"].rearrange("b t d -> t b d")
            for i in range(4):
                sp.dma_start(v["x"][:, 8 * i:8 * i + 8, :], xt[:, 8 * i:8 * i + 8, :]).then_inc(x_loaded[i], 16)
            with nc.allow_non_contiguous_dma(reason="biases by partition"):
                for dst, src in small:
                    sp.dma_start(dst, src).then_inc(small_loaded, 16)
            sp.wait_ge(small_loaded, 16 * len(small))
            sp.wait_ge(mask_chain, 6)
            sp.dma_start(a["mask_scratch"].rearrange("c b k -> b c k"), maskpart[:]).then_inc(mask_stored, 16)
            sp.wait_ge(mask_stored, 16)

        @block.gpsimd
        def _(pool):
            pool.memset(v["ident"][:], 0.0).then_inc(ident_zero, 1)
            pool.wait_ge(ident_zero, 1)
            pool.affine_select(out=v["ident"][:], in_=v["ident"][:], compare_op=ALU.not_equal, fill=1.0,
                               base=0, pattern=[[-1, P]], channel_multiplier=1).then_inc(ident_ready, 1)
            pool.memset(v["causal"][:], 0.0).then_inc(masks_zero, 1)
            pool.memset(v["causal_t"][:], 0.0).then_inc(masks_zero, 1)
            pool.wait_ge(masks_zero, 2)
            pool.affine_select(out=v["causal"][:], in_=v["causal"][:], compare_op=ALU.is_ge, fill=MASKED,
                               base=0, pattern=[[-1, S]], channel_multiplier=1).then_inc(masks_ready, 1)
            pool.affine_select(out=v["causal_t"][:], in_=v["causal_t"][:], compare_op=ALU.is_ge, fill=MASKED,
                               base=0, pattern=[[1, S]], channel_multiplier=-1).then_inc(masks_ready, 1)
            pool.memset(v["ones"][:], 1.0)
            pool.memset(v["ones_bf"][:], 1.0).then_inc(consts_ready, 1)
            pool.wait_ge(ident_ready, 1)
            pool.tensor_copy(v["ident_bf"][:], v["ident"][:]).then_inc(consts_ready, 1)

        @block.tensor
        def _(pe):
            pe.wait_ge(ident_ready, 1)
            pe.wait_ge(small_loaded, 16 * len(small))
            pe.transpose(bank[:, 0:NE], rw[:], v["ident"][0:NE, 0:NE]).then_inc(turned, 1)

        @block.scalar
        def _(act):
            act.wait_ge(turned, 1)
            act.copy(v["router_t"][:], bank[:, 0:NE])

        @block.vector
        def _(dve):
            for b in range(B):
                if b % 8 == 0:
                    dve.wait_ge(x_loaded[b // 8], 16)
                dve.bn_stats(stats[:, b, :], v["x"][:, b, :]).then_inc(stat_ready, 1)
            for b in range(B):
                dve.wait_ge(stat_ready, b + 1)
                dve.bn_aggr(v["moments"][:, b, :], stats[:, b, :]).then_inc(stat_ready, 1)
            dve.wait_ge(small_loaded, 16 * len(small))
            row = maskrow[:]
            dve.tensor_copy(maskpart[:, 0, :], row[:, 0, :]).then_inc(mask_chain, 1)
            dve.wait_ge(mask_chain, 1)
            dve.tensor_tensor(row[:, 1, :], row[:, 0, :], maskpart[:, 0, :], ALU.subtract).then_inc(mask_chain, 1)
            dve.wait_ge(mask_chain, 2)
            dve.tensor_copy(maskpart[:, 1, :], row[:, 1, :]).then_inc(mask_chain, 1)
            dve.wait_ge(mask_chain, 3)
            dve.tensor_tensor(row[:, 2, :], row[:, 1, :], maskpart[:, 1, :], ALU.subtract).then_inc(mask_chain, 1)
            dve.wait_ge(mask_chain, 4)
            dve.tensor_copy(maskpart[:, 2, :], row[:, 2, :]).then_inc(mask_chain, 2)
            for name in ["L0_xattn_wq", "L1_xattn_Wq", "L1_xattn_bq"]:
                dve.tensor_scalar(v[name][:], v[name][:], DH ** -0.5, None, ALU.mult)
            dve.tensor_tensor(v["ffn_bias"][:], v["L0_ffn_b_con"][:], v["L0_ffn_down_bias"][:], ALU.add)


def narrow_attention(nc, a, v, kind):
    own, cross = kind == "self", kind != "self"
    pre = {"self": "L0_attn", "cross0": "L0_xattn", "cross1": "L1_xattn"}[kind]
    wq = None if own else v[pre + ("_wq" if kind == "cross0" else "_Wq")]
    wk = v[{"self": "L0_attn_Wk", "cross0": "L0_xattn_wk", "cross1": "L1_xattn_Wk"}[kind]]
    wv = v[{"self": "L0_attn_Wv", "cross0": "L0_xattn_wv", "cross1": "L1_xattn_Wv"}[kind]]
    VW = FH // H if own else SLOT
    with ExitStack() as c:
        sem = c.enter_context(phase_semaphores(nc, kind + "_"))
        passed = {eng: sem("passed_" + eng) for eng in ("dve", "pool", "sp")}
        sb = lambda name, shape, dt=F32: c.enter_context(nc.sbuf_tensor(f"{kind}_{name}", shape, dt))
        bank = lambda name: c.enter_context(nc.psum_tensor(f"{kind}_{name}", [P, 512], F32))
        xn = sb("xn", [P, 2, 2, D])
        ctx = sb("ctx", [P, 2, 2, D]) if cross else None
        hT = sb("hT", [P, 2, 2, W2])
        qk = sb("qk", [P, 2, 2, W2])
        rest = sb("rest", [P, 2 * W2])
        part = sb("part", [P, 2, 3, 2, W2], BF16)
        qs = sb("qs", [P, 2, H, W2], BF16)
        ks = sb("ks", [P, 2, H, W2], BF16)
        vals = sb("vals", [P, 2, 2, H, VW])
        negmax = sb("negmax", [P, 2, 2, H])
        m0 = sb("m0", [H, 2, W2])
        mrest = sb("mrest", [H, W2])
        mpart = sb("mpart", [H, 2, 3, W2], BF16)
        expT = sb("expT", [P, NG, G * S])
        recip = sb("recip", [P, 512])
        if kind == "cross0":
            mraw = sb("mraw", [P, 2, 2, S])
            mask2 = sb("mask2", [P, 2, 2, 2, S])
            mask_part = sb("mask_part", [P, 2, 3, 2, 2, S], BF16)
            mask_rest = sb("mask_rest", [P, 2 * W2])
        if cross:
            oS = sb("oS", [P, 2, 512])
            on = sb("on", [P, 2, 2, D])
            onT = sb("onT", [P, 2, S])
            stats = sb("stats", [P, 2, 6])
            v = dict(v, stats=stats)
        scoreA = [bank("scoreA0"), bank("scoreA1")]
        scoreB = [bank("scoreB0"), bank("scoreB1")]
        turnb, projb, outb, endb = bank("turnb"), bank("projb"), bank("outb"), bank("endb")
        ln = {k: sem(k) for k in ["var_ready", "root_ready", "chain"]}
        rows_set, ones_rows = sem("rows_set"), sem("ones_rows")
        ctx_loaded, mask_loaded, stacked, mask_rows, m_rows = [
            [sem(f"{name}{i}") for i in range(2)] for name in ("ctx_loaded", "mask_loaded", "stacked", "mask_rows", "m_rows")]
        ln_done, x_pre, x_mid = sem("ln_done"), sem("x_pre"), sem("x_mid")
        xT_ready, hT_ready, qk_psum, qk_ready = sem("xT_ready"), sem("hT_ready"), sem("qk_psum"), sem("qk_ready")
        part1, pool_split, part3 = sem("part1"), sem("pool_split"), sem("part3")
        scr_written = sem("scr_written")
        v_psum, v_ready = sem("v_psum"), sem("v_ready")
        a_ready, max_done, mT_ready, m0_ready, m1_ready = (sem("a_ready"), sem("max_done"), sem("mT_ready"),
                                                           sem("m0_ready"), sem("m1_ready"))
        pool_msplit, m3_ready = sem("pool_msplit"), sem("m3_ready")
        b_ready, exp_done, pv_done = sem("b_ready"), sem("exp_done"), sem("pv_done")
        recip_done, norm_done = sem("recip_done"), sem("norm_done")
        o_copied, nat_ready, on_ready, onT_psum, onT_ready, y_ready, upd = (
            sem("o_copied"), sem("nat_ready"), sem("on_ready"), sem("onT_psum"), sem("onT_ready"),
            sem("y_ready"), sem("upd"))
        mask_turned, mask_copied, mask_p1, mask_p3, pool_mask = (
            sem("mask_turned"), sem("mask_copied"), sem("mask_p1"), sem("mask_p3"), sem("pool_mask"))
        scr = a["part_scratch"]
        KROWS = [0, 24, 40, 48]

        block = c.enter_context(nc.Block())

        @block.sync
        def _(sp):
            if cross:
                xt = a["ctx_1024"].rearrange("b t d -> t b d")
                mt = a["mask_Bx1xSxS2_ff0"].rearrange("b o q k -> q (b o) k")
            sp.wait_ge(rows_set, 6)
            for p in range(2):
                sp.dma_start(ks[MAIN:MAIN + 3, p, :, :], v["ones_bf"][0:3, :].unsqueeze(1).to_broadcast([3, H, W2])).then_inc(ones_rows, 16)
                if kind == "cross1":
                    sp.dma_start(qs[48:51, p, :, :], v["ones_bf"][0:3, :].unsqueeze(1).to_broadcast([3, H, W2])).then_inc(ones_rows, 16)
            sp.wait_ge(ones_rows, 16 * (4 if kind == "cross1" else 2))

            def step(t, p, has):
                q = 1 - p
                if cross and has(t):
                    wait(sp, xT_ready, t - 1)
                    sp.dma_start(ctx[:, p, :, :], xt[:, bass.ds(t * 2, 2), :]).then_inc(ctx_loaded[p], 16)
                    if kind == "cross0":
                        wait(sp, mask_copied, 2 * (t - 1))
                        sp.dma_start(mraw[:, p, :, :], mt[:, bass.ds(t * 2, 2), :]).then_inc(mask_loaded[p], 16)
                n = t - 1
                if has(n):
                    sp.wait_ge(part3, n + 1)
                    wait(sp, stacked[q], of_parity(n - 2, q, 96))
                    for k in range(3):
                        for s in range(2):
                            sp.dma_start(scr[q, s, k].rearrange("d h t -> h d t"),
                                         part[:, q, k, s, :]).then_inc(scr_written, 16)
                    wait_alone(sp, passed["sp"], scr_written, 96 * (n + 1))
                    wait(sp, b_ready, 8 * (n - 1))
                    for k in range(3):
                        m = 3 - k
                        r = KROWS[k]
                        sp.dma_start(qs[r:r + 8 * m, q, :, :].rearrange("p h t -> p (h t)"),
                                     scr[q, 0, k:k + 1].to_broadcast([m, DH, H, W2]).rearrange(
                                         "m d h t -> m d (h t)")).then_inc(stacked[q], 16)
                        sp.dma_start(ks[r:r + 8 * m, q, :, :].rearrange("p h t -> p (h t)"),
                                     scr[q, 1, 0:m].rearrange("m d h t -> (m d) (h t)")).then_inc(stacked[q], 16)
                    if kind == "cross1":
                        sp.dma_start(ks[48:51, q, :, :], a["mask_scratch"][:, bass.ds(n * 2, 2), :].rearrange(
                            "c b k -> c (b k)").unsqueeze(1).to_broadcast([3, H, W2])).then_inc(mask_rows[q], 16)
                n = t - 2
                if has(n):
                    sp.wait_ge(m3_ready, n + 1)
                    for k in range(3):
                        sp.dma_start(qs[MAIN + k:MAIN + k + 1, p, :, :], mpart[:, p, k, :]).then_inc(m_rows[p], 16)
            run_steps(sp, step, 4)

        @block.gpsimd
        def _(pool):
            for tile in (qs, ks):
                for lo in (32, 64, 96):
                    pool.memset(tile[lo:lo + 32, :, :, :], 0.0).then_inc(rows_set, 1)
            pool.wait_ge(rows_set, 6)
            if cross:
                pool.memset(vals[:], 0.0).then_inc(rows_set, 1)
                pool.wait_ge(rows_set, 7)
                pool.memset(vals[:, :, :, :, DH:DH + 1], 1.0).then_inc(rows_set, 1)

            def step(t, p, has):
                q = 1 - p
                n = t - 1
                if has(n):
                    pool.wait_ge(part1, n + 1)
                    wait(pool, part3, n)
                    pool.tensor_tensor(rest[:], qk[:, q, :, :].rearrange("p a t -> p (a t)"),
                                       part[:, q, 0, :, :].rearrange("p a t -> p (a t)"), ALU.subtract).then_inc(pool_split, 1)
                    wait_alone(pool, passed["pool"], pool_split, 2 * n + 1)
                    pool.tensor_scalar(part[:, q, 1, :, :].rearrange("p a t -> p (a t)"), rest[:], 1.0, 0.0,
                                       ALU.mult, ALU.add).then_inc(pool_split, 1)
                    pool.wait_ge(pool_split, 2 * n + 2)
                    pool.tensor_tensor(part[:, q, 2, :, :].rearrange("p a t -> p (a t)"), rest[:],
                                       part[:, q, 1, :, :].rearrange("p a t -> p (a t)"), ALU.subtract).then_inc(part3, 1)
                if kind in ("self", "cross1") and has(t):
                    wait_alone(pool, passed["pool"], ln_done, 2 * (t + 1))
                    bias = v["L0_attn_bf" if own else "L1_xattn_bv"][:].unsqueeze(1).to_broadcast([P, 2, D])
                    xs = v["x"][:, bass.ds(t * 2, 2), :]
                    if own:
                        pool.tensor_tensor(xs, xs, xn[:, p, :, :], ALU.add).then_inc(x_mid, 1)
                        wait_alone(pool, passed["pool"], x_mid, t + 1)
                    pool.tensor_tensor(xs, xs, bias, ALU.add).then_inc(x_pre, 1)
                n = t - 1
                if kind == "cross0" and has(n):
                    flat = lambda tile: tile.rearrange("p a b k -> p (a b k)")
                    pool.wait_ge(mask_p1, n + 1)
                    wait(pool, mask_p3, n)
                    pool.tensor_tensor(mask_rest[:], flat(mask2[:, q, :, :, :]), flat(mask_part[:, q, 0, :, :, :]),
                                       ALU.subtract).then_inc(pool_mask, 1)
                    wait_alone(pool, passed["pool"], pool_mask, 2 * n + 1)
                    pool.tensor_scalar(flat(mask_part[:, q, 1, :, :, :]), mask_rest[:], 1.0, 0.0,
                                       ALU.mult, ALU.add).then_inc(pool_mask, 1)
                    pool.wait_ge(pool_mask, 2 * n + 2)
                    pool.tensor_tensor(flat(mask_part[:, q, 2, :, :, :]), mask_rest[:],
                                       flat(mask_part[:, q, 1, :, :, :]), ALU.subtract).then_inc(mask_p3, 1)
                n = t - 2
                if has(n):
                    pool.wait_ge(m1_ready, n + 1)
                    wait(pool, m3_ready, n)
                    pool.tensor_tensor(mrest[:], m0[:, p, :], mpart[:, p, 0, :], ALU.subtract).then_inc(pool_msplit, 1)
                    wait_alone(pool, passed["pool"], pool_msplit, 2 * n + 1)
                    pool.tensor_scalar(mpart[:, p, 1, :], mrest[:], 1.0, 0.0, ALU.mult, ALU.add).then_inc(pool_msplit, 1)
                    pool.wait_ge(pool_msplit, 2 * n + 2)
                    pool.tensor_tensor(mpart[:, p, 2, :], mrest[:], mpart[:, p, 1, :], ALU.subtract).then_inc(m3_ready, 1)
            run_steps(pool, step, 4)

        @block.scalar
        def _(act):
            ln_scale_act(act, v, ln)

            def step(t, p, has):
                q = 1 - p
                n = t - 1
                if has(n):
                    act.wait_ge(qk_psum, n + 1)
                    wait(act, part3, n - 1)
                    if own:
                        act.copy(qk[:, q, 0, :], hT[:, q, 0, :])
                        act.activation(qk[:, q, 1, :], projb[:, W2:2 * W2], ACT.Identity,
                                       bias=v["L0_attn_bk"][:, 0:1]).then_inc(qk_ready, 1)
                    elif kind == "cross0":
                        act.copy(qk[:, q, :, :].rearrange("p a t -> p (a t)"), projb[:]).then_inc(qk_ready, 1)
                    else:
                        act.activation(qk[:, q, 0, :], projb[:, 0:W2], ACT.Identity, bias=v["L1_xattn_bq"][:, 0:1])
                        act.activation(qk[:, q, 1, :], projb[:, W2:2 * W2], ACT.Identity,
                                       bias=v["L1_xattn_bk"][:, 0:1]).then_inc(qk_ready, 1)
                    act.wait_ge(qk_ready, n + 1)
                    wait(act, scr_written, 96 * (n - 1))
                    act.copy(part[:, q, 0, :, :].rearrange("p a t -> p (a t)"),
                             qk[:, q, :, :].rearrange("p a t -> p (a t)")).then_inc(part1, 1)
                n = t - 3
                if has(n):
                    for b in range(2):
                        for g in range(NG):
                            u = 8 * n + 4 * b + g
                            act.wait_ge(b_ready, u + 1)
                            wait(act, pv_done, u - 3)
                            act.activation(expT[:, g, :], scoreB[g % 2][:], ACT.Exp).then_inc(exp_done, 1)
                        if cross:
                            act.wait_ge(pv_done, 8 * n + 4 * b + 4)
                            wait(act, nat_ready, 2 * n + b - 1)
                            act.copy(oS[:, b, :], outb[:]).then_inc(o_copied, 1)
                    if kind == "cross0":
                        for b in range(2):
                            act.wait_ge(onT_psum, 2 * n + b + 1)
                            wait(act, y_ready, n)
                            act.copy(onT[:, b, :], endb[:, 0:S]).then_inc(onT_ready, 1)
                if has(t):
                    act.wait_ge(xT_ready, t + 1)
                    wait(act, v_psum, (2 if own else 1) * (t - 1))
                    if cross:
                        act.copy(hT[:, p, :, :].rearrange("p a t -> p (a t)"), turnb[:]).then_inc(hT_ready, 1)
                    else:
                        act.copy(hT[:, p, 0, :], turnb[:, 0:W2]).then_inc(hT_ready, 1)
                n = t - 1
                if kind == "cross0" and has(n):
                    act.wait_ge(mask_turned, n + 1)
                    wait(act, mask_p3, n - 1)
                    act.copy(mask2[:, q, 1, :, :].rearrange("p b k -> p (b k)"), turnb[:, 0:W2]).then_inc(mask_copied, 1)
                    act.copy(mask2[:, q, 0, :, :], mraw[:, q, :, :]).then_inc(mask_copied, 1)
                    act.wait_ge(mask_copied, 2 * n + 2)
                    wait(act, b_ready, 8 * (n - 1))
                    act.copy(mask_part[:, q, 0, :, :, :].rearrange("p a b k -> p (a b k)"),
                             mask2[:, q, :, :, :].rearrange("p a b k -> p (a b k)")).then_inc(mask_p1, 1)
                if has(n):
                    if own:
                        for b in range(2):
                            act.wait_ge(v_psum, 2 * n + b + 1)
                            act.copy(vals[:, q, b, :, :].rearrange("p h w -> p (h w)"), projb[:]).then_inc(v_ready, 1)
                    else:
                        act.wait_ge(v_psum, n + 1)
                        act.copy(vals[:, q, :, :, 0:DH], projb[:, 0:W2].rearrange("p (b h w) -> p b h w", b=2, h=H)).then_inc(v_ready, 1)
                n = t - 2
                if has(n):
                    act.wait_ge(mT_ready, n + 1)
                    wait(act, m3_ready, n - 1)
                    act.copy(m0[:, p, :], turnb[0:H, 0:W2]).then_inc(m0_ready, 1)
                    act.wait_ge(m0_ready, n + 1)
                    wait(act, m_rows[p], of_parity(n - 2, p, 48))
                    act.copy(mpart[:, p, 0, :], m0[:, p, :]).then_inc(m1_ready, 1)
            if cross:
                act.wait_ge(rows_set, 8)
            run_steps(act, step, 4)

        @block.vector
        def _(dve):
            ln_scale_dve(dve, v, ln)

            def natural(n, b):
                o = endb[:].rearrange("p (h w) -> p h w", w=SLOT)
                k = 2 * n + b
                dve.wait_ge(nat_ready, k + 1)
                wait(dve, norm_done, k)
                if kind == "cross0":
                    wait(dve, onT_psum, k - 1)
                else:
                    wait(dve, upd, UPDATES * n)
                dve.reciprocal(recip[:, 0:H], o[:, :, DH]).then_inc(recip_done, 1)
                dve.wait_ge(recip_done, k + 1)
                dve.tensor_tensor(on[:, 0, b, :].rearrange("p (h w) -> p h w", h=H), o[:, :, 0:DH],
                                  recip[:, 0:H].unsqueeze(2).to_broadcast([P, H, DH]), ALU.mult).then_inc(norm_done, 1)

            def step(t, p, has):
                n = t - 3
                if own and has(n):
                    for b in range(2):
                        k = 2 * n + b
                        dve.wait_ge(pv_done, 8 * n + 4 * b + 4)
                        wait(dve, norm_done, k)
                        dve.reciprocal(recip[:], endb[:]).then_inc(recip_done, 1)
                        dve.wait_ge(recip_done, k + 1)
                        dve.tensor_tensor(v["o_all"][:, bass.ds(n, 1), :, b * S:(b + 1) * S],
                                          outb[:].rearrange("p (o j t) -> p o j t", o=1, j=NJ),
                                          recip[:].rearrange("p (o j t) -> p o j t", o=1, j=NJ),
                                          ALU.mult).then_inc(norm_done, 1)
                if cross and has(n):
                    natural(n, 0)
                if has(t):
                    wait(dve, xT_ready, t - 1)
                    if own:
                        wait(dve, x_mid, t - 1)
                    for b in range(2):
                        apply_ln(dve, v, xn[:, p, b:b + 1, :], t * 2 + b, ln_done)
                m = t - 2
                if has(m):
                    wait(dve, mT_ready, m - 1)
                for b in range(2):
                    if has(m):
                        for g in range(NG):
                            u = 8 * m + 4 * b + g
                            dve.wait_ge(a_ready, u + 1)
                            dve.tensor_reduce(negmax[:, p, b, G * g:G * g + G],
                                              scoreA[g % 2][:].rearrange("p (h k) -> p h k", h=G),
                                              AX.X, ALU.max, negate=True).then_inc(max_done, 1)
                    if cross and has(n) and b == 0:
                        natural(n, 1)
                if cross and has(n):
                    if kind == "cross0":
                        dve.wait_ge(y_ready, n + 1)
                        add = endb[:, S:S + W2].rearrange("p (b d) -> p b d", b=2)
                    else:
                        dve.wait_ge(norm_done, 2 * n + 2)
                        dve.wait_ge(x_pre, n + 1)
                        add = on[:, 0, :, :]
                    update_x(dve, v, n, add, passed["dve"], upd)
            run_steps(dve, step, 4)

        @block.tensor
        def _(pe):
            pe.wait_ge(ones_rows, 16 * (4 if kind == "cross1" else 2))
            ident, identb = v["ident"], v["ident_bf"]

            def mask_product(out, p, b, turned):
                if kind == "self":
                    m = v["causal_t" if turned else "causal"][:].unsqueeze(1).to_broadcast([P, G, S])
                    pe.matmul(out[:].rearrange("p (h k) -> p h k", h=G), identb[:], m, start=True, stop=False)
                elif kind == "cross0":
                    for k in range(3):
                        m = mask_part[:, p, k, 1 if turned else 0, b:b + 1, :].to_broadcast([P, G, S])
                        pe.matmul(out[:].rearrange("p (h k) -> p h k", h=G), identb[:], m, start=(k == 0), stop=False)

            def score_a(n, p, b, g):
                u = 8 * n + 4 * b + g
                wait(pe, max_done, u - 1)
                out = scoreA[g % 2]
                mask_product(out, p, b, False)
                for i in range(G):
                    h = G * g + i
                    mm = pe.matmul(out[:, i * S:(i + 1) * S], qs[0:MAIN, p, h, b * S:(b + 1) * S],
                                   ks[0:MAIN, p, h, b * S:(b + 1) * S], start=(kind == "cross1"), stop=(kind == "cross1" or i == G - 1))
                mm.then_inc(a_ready, 1)

            def score_b(n, p, b, g):
                u = 8 * n + 4 * b + g
                wait(pe, exp_done, u - 1)
                out = scoreB[g % 2]
                mask_product(out, p, b, True)
                for i in range(G):
                    h = G * g + i
                    mm = pe.matmul(out[:, i * S:(i + 1) * S], ks[:, p, h, b * S:(b + 1) * S],
                                   qs[:, p, h, b * S:(b + 1) * S], start=(kind == "cross1"), stop=(kind == "cross1" or i == G - 1))
                mm.then_inc(b_ready, 1)

            def weigh(n, p, b, g):
                u = 8 * n + 4 * b + g
                pe.wait_ge(exp_done, u + 1)
                if g == 0:
                    if own:
                        wait(pe, norm_done, 2 * n + b)
                    else:
                        wait(pe, o_copied, 2 * n + b)
                for i in range(G):
                    h = G * g + i
                    pT = expT[:, g, i * S:(i + 1) * S]
                    mm = pe.matmul(outb[SLOT * i:SLOT * i + SLOT, g * S:(g + 1) * S], vals[:, p, b, h, :], pT,
                                   start=True, stop=True)
                if own:
                    for i in range(G):
                        pT = expT[:, g, i * S:(i + 1) * S]
                        mm = pe.matmul(endb[SLOT * i:SLOT * i + SLOT, g * S:(g + 1) * S], v["ones"][:, 0:SLOT], pT,
                                       start=True, stop=True)
                mm.then_inc(pv_done, 1)

            def turn_out(n, b):
                k = 2 * n + b
                pe.wait_ge(o_copied, k + 1)
                for j in range(NG):
                    mm = pe.transpose(endb[:, j * S:(j + 1) * S], oS[:, b, j * S:(j + 1) * S], ident[:])
                mm.then_inc(nat_ready, 1)

            def turn_normed(n, b):
                pe.wait_ge(norm_done, 2 * n + b + 1)
                pe.transpose(endb[:, 0:S], on[:, 0, b, :], ident[:]).then_inc(onT_psum, 1)
                pe.wait_ge(onT_ready, 2 * n + b + 1)

            def step(t, p, has):
                q = 1 - p
                n = t - 1
                if has(n):
                    pe.wait_ge(hT_ready, n + 1)
                    wait(pe, v_ready, (2 if own else 1) * n)
                    if own:
                        pe.matmul(projb[:, W2:2 * W2], wk[:], hT[:, q, 0, :], start=True, stop=True).then_inc(qk_psum, 1)
                    else:
                        pe.matmul(projb[:, 0:W2], wq[:], hT[:, q, 0, :], start=True, stop=True)
                        pe.matmul(projb[:, W2:2 * W2], wk[:], hT[:, q, 1, :], start=True, stop=True).then_inc(qk_psum, 1)
                m = t - 3
                if has(m):
                    pe.wait_ge(m_rows[q], of_parity(m, q, 48))
                    pe.wait_ge(v_ready, (2 if own else 1) * (m + 1))
                    for b in range(2):
                        score_b(m, q, b, 0)
                        for g in range(NG):
                            if g < NG - 1:
                                score_b(m, q, b, g + 1)
                            weigh(m, q, b, g)
                k = t - 2
                if has(k):
                    pe.wait_ge(stacked[p], of_parity(k, p, 96))
                    if kind == "cross0":
                        pe.wait_ge(mask_p3, k + 1)
                    if kind == "cross1":
                        pe.wait_ge(mask_rows[p], of_parity(k, p, 16))
                for b in range(2):
                    if cross and has(m):
                        if b == 0:
                            wait(pe, upd, UPDATES * m)
                        else:
                            pe.wait_ge(norm_done, 2 * m + 1)
                        turn_out(m, b)
                    if has(k):
                        for g in range(NG):
                            score_a(k, p, b, g)
                    if kind == "cross0" and has(m):
                        turn_normed(m, b)
                if kind == "cross0" and has(m):
                    for b in range(2):
                        mm = pe.matmul(endb[:, S + b * S:2 * S + b * S], onT[:, b, :], v["L0_xattn_wo"][:], start=True, stop=True)
                    mm.then_inc(y_ready, 1)
                if has(t):
                    pe.wait_ge(ln_done, 2 * (t + 1))
                    wait(pe, m0_ready, t - 2)
                    if cross:
                        pe.wait_ge(ctx_loaded[p], of_parity(t, p, 16))
                    for b in range(2):
                        mm = pe.transpose(turnb[:, b * S:(b + 1) * S], xn[:, p, b, :], ident[:])
                    if cross:
                        for b in range(2):
                            mm = pe.transpose(turnb[:, W2 + b * S:W2 + (b + 1) * S], ctx[:, p, b, :], ident[:])
                    mm.then_inc(xT_ready, 1)
                n = t - 1
                if kind == "cross0" and has(n):
                    pe.wait_ge(mask_loaded[q], of_parity(n, q, 16))
                    if has(t):
                        pe.wait_ge(hT_ready, t + 1)
                    else:
                        wait(pe, m0_ready, t - 2)
                    for b in range(2):
                        mm = pe.transpose(turnb[:, b * S:(b + 1) * S], mraw[:, q, b, :], ident[:])
                    mm.then_inc(mask_turned, 1)
                if has(n):
                    pe.wait_ge(qk_ready, n + 1)
                    for b in range(2):
                        if own:
                            if b == 1:
                                pe.wait_ge(v_ready, 2 * n + 1)
                            pe.matmul(projb[:], hT[:, q, 0, b * S:(b + 1) * S], wv[:], start=True, stop=True).then_inc(v_psum, 1)
                        else:
                            mm = pe.matmul(projb[:, b * S:(b + 1) * S], hT[:, q, 1, b * S:(b + 1) * S], wv[:], start=True, stop=True)
                    if cross:
                        mm.then_inc(v_psum, 1)
                if has(k):
                    pe.wait_ge(max_done, 8 * (k + 1))
                    if kind == "cross0" and has(t - 1):
                        pe.wait_ge(mask_copied, 2 * t - 1)
                    elif has(t):
                        pe.wait_ge(hT_ready, t + 1)
                    else:
                        wait(pe, m0_ready, k)
                    for b in range(2):
                        mm = pe.transpose(turnb[0:H, b * S:(b + 1) * S], negmax[:, p, b, :], ident[:])
                    mm.then_inc(mT_ready, 1)
            run_steps(pe, step, 4)


def gelu_projection(nc, a, v):
    with ExitStack() as c:
        sem = c.enter_context(phase_semaphores(nc, "wf_"))
        passed = {eng: sem("passed_" + eng) for eng in ("dve", "pool", "sp")}
        sb = lambda name, shape, dt=F32: c.enter_context(nc.sbuf_tensor("wf_" + name, shape, dt))
        g = sb("g", [P, 2, NJ, W2])
        stats = sb("stats", [P, 2, 6])
        v = dict(v, stats=stats)
        yb = [c.enter_context(nc.psum_tensor(f"wf_y{i}", [P, 512], F32)) for i in range(2)]
        g_ready, y_ready, upd = sem("g_ready"), sem("y_ready"), sem("upd")
        block = c.enter_context(nc.Block())

        @block.scalar
        def _(act):
            def step(t, p, has):
                if has(t):
                    wait(act, y_ready, t - 1)
                    for j in range(NJ):
                        act.activation(g[:, p, j:j + 1, :], v["o_all"][:, bass.ds(t, 1), j, :], ACT.Gelu,
                                       bias=v["L0_attn_bv"][:, j:j + 1]).then_inc(g_ready, 1)
            run_steps(act, step, 0)

        @block.tensor
        def _(pe):
            def step(t, p, has):
                if has(t):
                    wait(pe, upd, UPDATES * (t - 1))
                    pe.wait_ge(g_ready, NJ * (t + 1))
                    for b in range(2):
                        for j in range(NJ):
                            mm = pe.matmul(yb[p][:, b * D:(b + 1) * D], g[:, p, j, b * S:(b + 1) * S],
                                           v["L0_attn_Wf"][:, j, :], start=(j == 0), stop=(j == NJ - 1))
                    mm.then_inc(y_ready, 1)
            run_steps(pe, step, 0)

        @block.vector
        def _(dve):
            def step(t, p, has):
                if has(t):
                    dve.wait_ge(y_ready, t + 1)
                    update_x(dve, v, t, yb[p][:, 0:W2].rearrange("p (b d) -> p b d", b=2), passed["dve"], upd)
            run_steps(dve, step, 0)


def butterfly(eng, tile, tmp, w, rows, loaded, chain, down):
    for k in range(9):
        st = 8 - k if down else k
        s = 2 ** st
        src = tile[0:rows, k % 2, :].rearrange("p (n two s) -> p n two s", two=2, s=s)
        dst = tile[0:rows, (k + 1) % 2, :].rearrange("p (n two s) -> p n two s", two=2, s=s)
        ws = w[0:rows, k % 2, :].rearrange("p (n s f) -> p n s f", s=s, f=4)
        eng.wait_ge(loaded[k % 2], 16 * (k // 2 + 1))
        for o in range(2):
            first, second = (o, 2 + o) if down else (2 * o, 2 * o + 1)
            if k:
                eng.wait_ge(chain, 6 * k)
            shape = lambda t: t.rearrange("p (n s) -> p n s", s=s)
            eng.tensor_tensor(shape(tmp[0:rows, 2 * o, :]), src[:, :, 0, :], ws[:, :, :, first], ALU.mult).then_inc(chain, 1)
            eng.tensor_tensor(shape(tmp[0:rows, 2 * o + 1, :]), src[:, :, 1, :], ws[:, :, :, second], ALU.mult).then_inc(chain, 1)
        for o in range(2):
            eng.wait_ge(chain, 6 * k + 2 * o + 2)
            eng.tensor_tensor(dst[:, :, o, :], shape(tmp[0:rows, 2 * o, :]), shape(tmp[0:rows, 2 * o + 1, :]), ALU.add).then_inc(chain, 1)
    eng.wait_ge(chain, 54)


def weights_phase(nc, a, v):
    with ExitStack() as c:
        sem = c.enter_context(phase_semaphores(nc, "bf_"))
        passed = {eng: sem("passed_" + eng) for eng in ("dve", "pool", "sp")}
        sb = lambda name, shape, dt=F32: c.enter_context(nc.sbuf_tensor("bf_" + name, shape, dt))
        up, down, row = sb("up", [P, 2, FH]), sb("down", [P, 2, FH]), sb("row", [1, 2, FH])
        w_up, w_down = sb("w_up", [P, 2, 2 * FH]), sb("w_down", [P, 2, 2 * FH])
        w_row = sb("w_row", [1, 2, 2 * FH])
        tmp, tmp_row = sb("tmp", [P, 4, FH // 2]), sb("tmp_row", [1, 4, FH // 2])
        bank = c.enter_context(nc.psum_tensor("bf_bank", [P, 512], F32))
        bias_bank = c.enter_context(nc.psum_tensor("bf_bias", [P, 512], F32))
        con_bank = c.enter_context(nc.psum_tensor("bf_con_turned", [P, 512], F32))
        wt = c.enter_context(nc.psum_tensor("bf_wt", [P, 2, 512], F32))
        con = sb("con", [P, NJ, D])
        stage_w = sb("stage_w", [P, 4, J1, P])
        up_loaded, down_loaded, row_loaded = [[sem(f"{n}_loaded{i}") for i in range(2)] for n in ("up", "down", "row")]
        up_chain, down_chain, row_chain = sem("up_chain"), sem("down_chain"), sem("row_chain")
        begun, b_loaded, turned, copied = sem("begun"), sem("b_loaded"), sem("turned"), sem("copied")
        con_loaded, con_turned, stage_loaded, w_turned, w_copied, bias_loaded, late_loaded = (
            sem("con_loaded"), sem("con_turned"), sem("stage_loaded"), sem("w_turned"), sem("w_copied"),
            sem("bias_loaded"), sem("late_loaded"))
        block = c.enter_context(nc.Block())

        def stage(name, st, rows):
            return a[name][st:st + 1].rearrange("o k i j -> o (k i j)").to_broadcast([rows, 2 * FH])

        @block.sync
        def _(sp):
            sp.dma_start(con[:], a["L0_ffn_W_con"].rearrange("(j p) d -> p j d", p=P)).then_inc(con_loaded, 16)
            sp.dma_start(row[:, 0, :], a["L0_ffn_b_exp"].rearrange("(o d) -> o d", o=1)).then_inc(b_loaded, 16)
            for i, name in enumerate(["L1_attn_wq", "L1_attn_wk", "L1_attn_wv"]):
                sp.dma_start(stage_w[:, i, :, :], a[name].rearrange("(j p) e -> p j e", p=P)).then_inc(stage_loaded, 16)
            sp.dma_start(stage_w[:, 3, :, :].rearrange("p j e -> p (j e)"), a["L1_attn_wo"]).then_inc(stage_loaded, 16)
            with nc.allow_non_contiguous_dma(reason="biases by partition"):
                for name in ["L1_attn_bq", "L1_attn_bk", "L1_attn_bv"]:
                    sp.dma_start(v[name][:], a[name].rearrange("(j p) -> p j", p=P)).then_inc(bias_loaded, 16)
                for name in ["L1_attn_bq", "L1_attn_bk"]:
                    pairs = a[name].rearrange("(j p two) -> two p j", p=P // 2, two=2)
                    for k in range(2):
                        sp.dma_start(v[name + "_swapped"][k::2, :], pairs[1 - k]).then_inc(bias_loaded, 16)
            for k in range(9):
                if k >= 2:
                    sp.wait_ge(up_chain, 6 * (k - 1))
                sp.dma_start(w_up[:, k % 2, :], stage("L0_ffn_up_weights", k, P)).then_inc(up_loaded[k % 2], 16)
                if k >= 2:
                    sp.wait_ge(row_chain, 6 * (k - 1))
                sp.dma_start(w_row[:, k % 2, :], stage("L0_ffn_up_weights", k, 1)).then_inc(row_loaded[k % 2], 16)
            sp.dma_start(v["L1_ffn_ew1"][:], a["L1_ffn_ew1"].rearrange("e d h -> d e h")).then_inc(late_loaded, 16)
            sp.dma_start(v["L1_ffn_ew2"][:], a["L1_ffn_ew2"].rearrange("e h d -> h e d")).then_inc(late_loaded, 16)
            sp.wait_ge(late_loaded, 32)

        @block.scalar
        def _(act):
            def load_down(k):
                if k >= 2:
                    act.wait_ge(down_chain, 6 * (k - 1))
                act.dma_start(w_down[:, k % 2, :], stage("L0_ffn_down_weights", 8 - k, P)).then_inc(down_loaded[k % 2], 16)
            load_down(0)
            load_down(1)
            act.wait_ge(con_turned, 1)
            act.copy(down[:, 0, :], con_bank[:]).then_inc(begun, 1)
            for g in range(8):
                act.wait_ge(w_turned, g + 1)
                name = ["wqT", "wkT", "wvT", "woT"][g // 2]
                src = wt[:, g % 2, :].rearrange("p (j e) -> p j e", j=4)
                tiles = slice(4 * (g % 2), 4 * (g % 2) + 4)
                scale = HD1 ** -0.5 if g < 2 else 1.0
                if g < 4:
                    for k in range(2):
                        act.activation(v[name + "_swapped"][:, tiles, k::2], src[:, :, 1 - k::2], ACT.Copy, scale=scale)
                act.activation(v[name][:, tiles, :], src, ACT.Copy, scale=scale).then_inc(w_copied, 1)
            act.wait_ge(bias_loaded, 16 * 7)
            for name in ["L1_attn_bq", "L1_attn_bq_swapped"]:
                act.activation(v[name][:], v[name][:], ACT.Copy, scale=HD1 ** -0.5)
            for k in range(2, 9):
                load_down(k)
            act.wait_ge(turned, 1)
            act.copy(v["up_bias_row"][:], bias_bank[:, 0:NJ]).then_inc(copied, 1)
            act.wait_ge(turned, 2)
            act.copy(v["W_down"][:], bank[:].rearrange("p (j d) -> p j d", j=NJ)).then_inc(copied, 1)

        @block.vector
        def _(dve):
            dve.tensor_copy(up[:, 0, :], v["L0_ffn_W_exp"][:]).then_inc(begun, 1)
            dve.wait_ge(begun, 2)
            butterfly(dve, up, tmp, w_up, P, up_loaded, up_chain, False)
            dve.tensor_copy(v["W_up"][:], up[:, 1, :])
            butterfly(dve, down, tmp, w_down, P, down_loaded, down_chain, True)
            dve.wait_ge(copied, 1)
            dve.tensor_tensor(v["up_bias"][:], v["up_bias_row"][:], v["L0_ffn_up_bias"][:], ALU.add)

        @block.gpsimd
        def _(pool):
            pool.wait_ge(b_loaded, 16)
            butterfly(pool, row, tmp_row, w_row, 1, row_loaded, row_chain, False)

        @block.tensor
        def _(pe):
            pe.wait_ge(con_loaded, 16)
            for j in range(NJ):
                mm = pe.transpose(con_bank[:, j * P:(j + 1) * P], con[:, j, :], v["ident"][:])
            mm.then_inc(con_turned, 1)
            pe.wait_ge(stage_loaded, 64)
            for g in range(8):
                if g >= 2:
                    pe.wait_ge(w_copied, g - 1)
                for j in range(4):
                    mm = pe.transpose(wt[:, g % 2, 128 * j:128 * j + 128], stage_w[:, g // 2, 4 * (g % 2) + j, :], v["ident"][:])
                mm.then_inc(w_turned, 1)
            pe.wait_ge(row_chain, 54)
            for j in range(NJ):
                mm = pe.matmul(bias_bank[:, j:j + 1], row[:, 1, j * P:(j + 1) * P], v["ones"][0:1, 0:1], start=True, stop=True)
            mm.then_inc(turned, 1)
            pe.wait_ge(down_chain, 54)
            for j in range(NJ):
                mm = pe.transpose(bank[:, j * P:(j + 1) * P], down[:, 1, j * P:(j + 1) * P], v["ident"][:])
            mm.then_inc(turned, 1)


def ffn_phase(nc, a, v):
    with ExitStack() as c:
        sem = c.enter_context(phase_semaphores(nc, "ffn_"))
        passed = {eng: sem("passed_" + eng) for eng in ("dve", "pool", "sp")}
        sb = lambda name, shape, dt=F32: c.enter_context(nc.sbuf_tensor("ffn_" + name, shape, dt))
        bank = lambda name: c.enter_context(nc.psum_tensor("ffn_" + name, [P, 512], F32))
        xn, hT, g = sb("xn", [P, 2, 2, D]), sb("hT", [P, 2, W2]), sb("g", [P, 2, NJ, W2])
        v = dict(v, stats=sb("stats", [P, 2, 6]))
        turnb, hidb, yb = [bank("turn0"), bank("turn1")], [bank("hid0"), bank("hid1")], [bank("y0"), bank("y1")]
        ln = {k: sem(k) for k in ["var_ready", "root_ready", "chain"]}
        ln_done, x_pre, xT_ready, hT_ready = sem("ln_done"), sem("x_pre"), sem("xT_ready"), sem("hT_ready")
        hid_ready, g_ready, y_ready, upd = sem("hid_ready"), sem("g_ready"), sem("y_ready"), sem("upd")
        block = c.enter_context(nc.Block())

        @block.gpsimd
        def _(pool):
            def step(t, p, has):
                if has(t):
                    wait_alone(pool, passed["pool"], ln_done, 2 * (t + 1))
                    xs = v["x"][:, bass.ds(t * 2, 2), :]
                    pool.tensor_tensor(xs, xs, v["ffn_bias"][:].unsqueeze(1).to_broadcast([P, 2, D]),
                                       ALU.add).then_inc(x_pre, 1)
            run_steps(pool, step, 0)

        @block.scalar
        def _(act):
            ln_scale_act(act, v, ln)

            def step(t, p, has):
                q = 1 - p
                if has(t):
                    act.wait_ge(xT_ready, t + 1)
                    wait(act, hid_ready, 2 * (t - 1))
                    act.copy(hT[:, p, :], turnb[p][:, 0:W2]).then_inc(hT_ready, 1)
                n = t - 1
                if has(n):
                    wait(act, y_ready, n - 1)
                    for j in range(NJ):
                        act.wait_ge(hid_ready, 2 * n + j // 2 + 1)
                        act.activation(g[:, q, j, :], hidb[j // 2][:, (j % 2) * W2:(j % 2 + 1) * W2], ACT.Gelu,
                                       bias=v["up_bias"][:, j:j + 1]).then_inc(g_ready, 1)
            run_steps(act, step, 2)

        @block.vector
        def _(dve):
            ln_scale_dve(dve, v, ln)

            def step(t, p, has):
                if has(t):
                    wait(dve, xT_ready, t - 1)
                    for b in range(2):
                        apply_ln(dve, v, xn[:, p, b:b + 1, :], t * 2 + b, ln_done)
                n = t - 2
                if has(n):
                    dve.wait_ge(y_ready, n + 1)
                    dve.wait_ge(x_pre, n + 1)
                    update_x(dve, v, n, yb[p][:, 0:W2].rearrange("p (b d) -> p b d", b=2), passed["dve"], upd)
            run_steps(dve, step, 2)

        @block.tensor
        def _(pe):
            def step(t, p, has):
                q = 1 - p
                if has(t):
                    pe.wait_ge(ln_done, 2 * (t + 1))
                    wait(pe, hT_ready, t - 1)
                    for b in range(2):
                        mm = pe.transpose(turnb[p][:, b * S:(b + 1) * S], xn[:, p, b, :], v["ident"][:])
                    mm.then_inc(xT_ready, 1)
                n = t - 2
                if has(n):
                    pe.wait_ge(g_ready, NJ * (n + 1))
                    wait(pe, upd, UPDATES * (n - 1))
                    for b in range(2):
                        for j in range(NJ):
                            mm = pe.matmul(yb[p][:, b * D:(b + 1) * D], g[:, p, j, b * S:(b + 1) * S],
                                           v["W_down"][:, j, :], start=(j == 0), stop=(j == NJ - 1))
                    mm.then_inc(y_ready, 1)
                n = t - 1
                if has(n):
                    pe.wait_ge(hT_ready, n + 1)
                    for j in range(NJ):
                        if j % 2 == 0:
                            wait(pe, g_ready, NJ * (n - 1) + j + 2)
                        mm = pe.matmul(hidb[j // 2][:, (j % 2) * W2:(j % 2 + 1) * W2], v["W_up"][:, j * P:(j + 1) * P],
                                       hT[:, q, :], start=True, stop=True)
                        if j % 2:
                            mm.then_inc(hid_ready, 1)
            run_steps(pe, step, 2)


def rotary_attention(nc, a, v):
    with ExitStack() as c:
        sem = c.enter_context(phase_semaphores(nc, "rot_"))
        passed = {eng: sem("passed_" + eng) for eng in ("dve", "pool", "sp")}
        sb = lambda name, shape, dt=F32: c.enter_context(nc.sbuf_tensor("rot_" + name, shape, dt))
        bank = lambda name: c.enter_context(nc.psum_tensor("rot_" + name, [P, 512], F32))
        xn, hT = sb("xn", [P, 2, 2, D]), sb("hT", [P, 2, W2])
        qT = sb("qT", [P, 2, J1, W2])
        kz = sb("kz", [P, 2, J1, 2, 2, S])
        cosp, sinp = sb("cosp", [P, 2, 2, W2]), sb("sinp", [P, 2, 2, W2])
        vals = sb("vals", [P, 2, 2, H * HD1])
        negmax, sums, inv = sb("negmax", [P, 4, G]), sb("sums", [P, 4, G]), sb("inv", [P, 4, G])
        probs, pT = sb("probs", [P, 4, G * S]), sb("pT", [P, 2, G * S])
        oT = sb("oT", [P, 2, J1, S])
        stats = sb("stats", [P, 6])
        qb, kb = bank("q"), bank("k")
        scoreb, turnb = [bank("score0"), bank("score1")], [bank("turn0"), bank("turn1")]
        outb, mixb = bank("out"), bank("mix")
        ln = {k: sem(k) for k in ["var_ready", "root_ready", "chain"]}
        kz_zero, ln_done, x_pre, xT_ready, hT_ready = (sem("kz_zero"), sem("ln_done"), sem("x_pre"),
                                                       sem("xT_ready"), sem("hT_ready"))
        projected, mixed, q_rotated, k_rotated = sem("projected"), sem("mixed"), sem("q_rotated"), sem("k_rotated")
        v_psum, v_ready, a_ready, max_done, exp_done = (sem("v_psum"), sem("v_ready"), sem("a_ready"),
                                                        sem("max_done"), sem("exp_done"))
        inv_done, normed, turned, pT_ready, pv_done, o_ready, y_ready, upd = (
            sem("inv_done"), sem("normed"), sem("turned"), sem("pT_ready"), sem("pv_done"), sem("o_ready"),
            sem("y_ready"), sem("upd"))
        block = c.enter_context(nc.Block())

        def unit(t, k, lag):
            return (t - 2, k - lag) if k >= lag else (t - 3, k - lag + 8)

        @block.gpsimd
        def _(pool):
            pool.memset(kz[:], 0.0).then_inc(kz_zero, 1)
            pool.wait_ge(kz_zero, 1)

            def step(t, p, has):
                q = 1 - p
                for k in range(8):
                    n = t - 1
                    if has(n):
                        cn = 8 * n + k
                        pool.wait_ge(mixed, 4 * cn + 4)
                        if k == 0:
                            wait(pool, a_ready, 8 * (n - 1))
                        for i in range(2):
                            r = slice(64 * i, 64 * i + 64)
                            if i == 1:
                                if k == 0:
                                    pool.wait_ge(x_pre, n + 1)
                                m, u = unit(t, k - 1, 1) if k else unit(t - 1, 7, 1)
                                if has(m):
                                    pool.wait_ge(normed, 8 * m + u + 1)
                            pool.tensor_tensor(kz[r, q, k, :, i, :], cosp[r, k % 2, 1, :].rearrange("p (b t) -> p b t", b=2),
                                               sinp[r, k % 2, 1, :].rearrange("p (b t) -> p b t", b=2),
                                               ALU.add).then_inc(k_rotated, 1)
                    m, u = unit(t, k, 1)
                    if has(m):
                        un = 8 * m + u
                        pool.wait_ge(inv_done, un + 1)
                        if has(n):
                            pool.wait_ge(k_rotated, 2 * cn + 2)
                        pr = probs[:, u % 4, :].rearrange("p (h k) -> p h k", h=G)
                        pool.tensor_tensor(pr, pr, inv[:, u % 4, :].unsqueeze(2).to_broadcast([P, G, S]),
                                           ALU.mult).then_inc(normed, 1)
                if has(t):
                    wait_alone(pool, passed["pool"], ln_done, 2 * (t + 1))
                    if has(t - 1):
                        pool.wait_ge(k_rotated, 16 * t)
                    xs = v["x"][:, bass.ds(t * 2, 2), :]
                    pool.tensor_tensor(xs, xs, v["L1_attn_bo"][:].unsqueeze(1).to_broadcast([P, 2, D]),
                                       ALU.add).then_inc(x_pre, 1)
            run_steps(pool, step, 3)

        @block.scalar
        def _(act):
            ln_scale_act(act, v, ln)

            def step(t, p, has):
                q = 1 - p
                for k in range(8):
                    m, u = unit(t, k, 2)
                    if has(m):
                        un = 8 * m + u
                        act.wait_ge(turned, un + 1)
                        wait(act, pv_done, un - 1)
                        act.copy(pT[:, u % 2, :], turnb[u % 2][:]).then_inc(pT_ready, 1)
                    n = t - 2
                    if has(n):
                        un = 8 * n + k
                        act.wait_ge(max_done, un + 1)
                        wait(act, turned, un - 3)
                        wait(act, inv_done, un - 3)
                        for i in range(G):
                            act.activation(probs[:, k % 4, i * S:(i + 1) * S], scoreb[k % 2][:, i * S:(i + 1) * S],
                                           ACT.Exp, bias=negmax[:, k % 4, i:i + 1],
                                           accum_out=sums[:, k % 4, i:i + 1]).then_inc(exp_done, 1)
                    m, u = unit(t, k, 3)
                    if has(m) and u % 2:
                        act.wait_ge(pv_done, 8 * m + u + 1)
                        b, j0 = u // 4, (u % 4 - 1) * 2
                        if u % 4 == 1:
                            wait(act, y_ready, 2 * m + b - 1)
                        for i in range(4):
                            act.activation(oT[:, b, j0 + i, :], outb[:, i * S:(i + 1) * S], ACT.Identity,
                                           bias=v["L1_attn_bv"][:, j0 + i:j0 + i + 1]).then_inc(o_ready, 1)
                    n = t - 1
                    if has(n) and 3 <= k < 7:
                        i = k - 3
                        act.wait_ge(v_psum, 4 * n + i + 1)
                        act.copy(vals[:, q, i // 2, (i % 2) * 512:(i % 2 + 1) * 512], mixb[:]).then_inc(v_ready, 1)
                    if has(t) and k == 6:
                        act.wait_ge(xT_ready, t + 1)
                        act.copy(hT[:, p, :], mixb[:, 0:W2]).then_inc(hT_ready, 1)
            run_steps(act, step, 3)

        @block.vector
        def _(dve):
            ln_scale_dve(dve, v, ln)

            def add_y(n, b):
                k = 2 * n + b
                dve.wait_ge(y_ready, k + 1)
                dve.wait_ge(x_pre, n + 1)
                wait(dve, upd, 4 * k)
                xs = v["x"][:, bass.ds(n * 2 + b, 1), :]
                dve.tensor_tensor(xs, xs, mixb[:, 0:D].unsqueeze(1), ALU.add).then_inc(upd, 1)
                wait_alone(dve, passed["dve"], upd, 4 * k + 1)
                dve.bn_stats(stats[:], xs).then_inc(upd, 1)
                wait_alone(dve, passed["dve"], upd, 4 * k + 2)
                dve.bn_aggr(v["aggr"][:, 0, :], stats[:]).then_inc(upd, 1)
                dve.wait_ge(upd, 4 * k + 3)
                dve.tensor_copy(v["moments"][:, bass.ds(n * 2 + b, 1), :], v["aggr"][:, 0:1, :]).then_inc(upd, 1)

            def step(t, p, has):
                q = 1 - p
                for k in range(8):
                    n = t - 2
                    if has(n):
                        un = 8 * n + k
                        dve.wait_ge(a_ready, un + 1)
                        dve.tensor_reduce(negmax[:, k % 4, :], scoreb[k % 2][:].rearrange("p (h k) -> p h k", h=G),
                                          AX.X, ALU.max, negate=True).then_inc(max_done, 1)
                    n = t - 1
                    if has(n):
                        cn = 8 * n + k
                        dve.wait_ge(projected, cn + 1)
                        wait(dve, q_rotated, cn - 1)
                        wait(dve, k_rotated, 2 * (cn - 1))
                        for s, bk, bias in ((0, qb, "L1_attn_bq"), (1, kb, "L1_attn_bk")):
                            for dst, o, name, table in ((cosp, 0, bias, "rope_cos"), (sinp, W2, bias + "_swapped", "rope_sin")):
                                dve.scalar_tensor_tensor(
                                    dst[:, k % 2, s, :].rearrange("p (b t) -> p b t", b=2),
                                    bk[:, o:o + W2].rearrange("p (b t) -> p b t", b=2), v[name][:, k:k + 1],
                                    v[table][:].unsqueeze(1).to_broadcast([P, 2, S]), ALU.add, ALU.mult).then_inc(mixed, 1)
                        if k == 0:
                            wait(dve, a_ready, 8 * (n - 1))
                        dve.wait_ge(mixed, 4 * cn + 2)
                        dve.tensor_tensor(qT[:, q, k, :], cosp[:, k % 2, 0, :], sinp[:, k % 2, 0, :],
                                          ALU.add).then_inc(q_rotated, 1)
                    m, u = unit(t, k, 1)
                    if has(m):
                        un = 8 * m + u
                        dve.wait_ge(exp_done, 4 * un + 4)
                        wait(dve, normed, un - 3)
                        dve.reciprocal(inv[:, u % 4, :], sums[:, u % 4, :]).then_inc(inv_done, 1)
                    if k == 4 and has(t - 3):
                        add_y(t - 3, 1)
                    if k == 5 and has(t):
                        wait(dve, xT_ready, t - 1)
                        for b in range(2):
                            apply_ln(dve, v, xn[:, p, b:b + 1, :], t * 2 + b, ln_done)
                    if k == 7 and has(t - 2):
                        add_y(t - 2, 0)
            run_steps(dve, step, 3)

        @block.tensor
        def _(pe):
            ident, identb = v["ident"], v["ident_bf"]
            pe.wait_ge(kz_zero, 1)

            def out_projection(n, b):
                k = 2 * n + b
                pe.wait_ge(o_ready, 8 * (k + 1))
                for j in range(J1):
                    mm = pe.matmul(mixb[:, 0:D], oT[:, b, j, :], v["woT"][:, j, :], start=(j == 0), stop=(j == J1 - 1))
                mm.then_inc(y_ready, 1)

            def step(t, p, has):
                q = 1 - p
                m = t - 3
                n = t - 1
                for k in range(8):
                    if has(n):
                        cn = 8 * n + k
                        if k == 0:
                            pe.wait_ge(hT_ready, n + 1)
                        wait(pe, mixed, 4 * cn)
                        for bk, w in ((qb, "wqT"), (kb, "wkT")):
                            pe.matmul(bk[:, 0:W2], v[w][:, k, :], hT[:, q, :], start=True, stop=True)
                            mm = pe.matmul(bk[:, W2:2 * W2], v[w + "_swapped"][:, k, :], hT[:, q, :], start=True, stop=True)
                        mm.then_inc(projected, 1)
                    if has(t - 2):
                        un = 8 * (t - 2) + k
                        b, g = k // 4, k % 4
                        if k == 0:
                            pe.wait_ge(q_rotated, 8 * (t - 1))
                            pe.wait_ge(k_rotated, 16 * (t - 1))
                        wait(pe, exp_done, 4 * (un - 1))
                        out = scoreb[k % 2]
                        pe.matmul(out[:].rearrange("p (h k) -> p h k", h=G), identb[:],
                                  v["causal"][:].unsqueeze(1).to_broadcast([P, G, S]), start=True, stop=False)
                        for i in range(2):
                            j = 2 * g + i
                            mm = pe.matmul(out[:, i * W2:(i + 1) * W2], qT[:, p, j, b * S:(b + 1) * S],
                                           kz[:, p, j, b, :, :].rearrange("p h t -> p (h t)"), start=False, stop=(i == 1))
                        mm.then_inc(a_ready, 1)
                    l, u = unit(t, k, 2)
                    if has(l):
                        un = 8 * l + u
                        pe.wait_ge(normed, un + 1)
                        wait(pe, pT_ready, un - 1)
                        for i in range(G):
                            mm = pe.transpose(turnb[u % 2][:, i * S:(i + 1) * S], probs[:, u % 4, i * S:(i + 1) * S], ident[:])
                        mm.then_inc(turned, 1)
                    l, u = unit(t, k, 3)
                    if has(l):
                        un = 8 * l + u
                        r = p if k >= 3 else q
                        b, g = u // 4, u % 4
                        pe.wait_ge(pT_ready, un + 1)
                        if u == 0:
                            pe.wait_ge(v_ready, 4 * (l + 1))
                        if u % 2 == 0:
                            wait(pe, o_ready, 2 * un)
                        for i in range(G):
                            h = G * g + i
                            col = ((u % 2) * 2 + i // 2) * S
                            mm = pe.matmul(outb[64 * (i % 2):64 * (i % 2) + 64, col:col + S],
                                           vals[:, r, b, h * HD1:(h + 1) * HD1], pT[:, u % 2, i * S:(i + 1) * S],
                                           start=True, stop=True)
                        mm.then_inc(pv_done, 1)
                    if has(n) and 3 <= k < 7:
                        i = k - 3
                        if i == 0 and has(m):
                            pe.wait_ge(upd, 4 * (2 * m + 1))
                        if i in (1, 3):
                            pe.wait_ge(v_ready, 4 * n + i)
                        if i == 2:
                            pe.wait_ge(v_ready, 4 * n + 2)
                            if has(m):
                                pe.wait_ge(upd, 4 * (2 * m + 2))
                        pe.matmul(mixb[:], hT[:, q, (i // 2) * S:(i // 2 + 1) * S],
                                  v["wvT"][:, (i % 2) * 4:(i % 2) * 4 + 4, :].rearrange("p j e -> p (j e)"),
                                  start=True, stop=True).then_inc(v_psum, 1)
                    if k == 4 and has(m):
                        if has(n):
                            pe.wait_ge(v_ready, 4 * n + 2)
                        pe.wait_ge(upd, 4 * (2 * m + 1))
                        out_projection(m, 1)
                    if k == 6 and has(t):
                        if has(n):
                            pe.wait_ge(v_ready, 4 * n + 4)
                        pe.wait_ge(ln_done, 2 * (t + 1))
                        for b in range(2):
                            mm = pe.transpose(mixb[:, b * S:(b + 1) * S], xn[:, p, b, :], ident[:])
                        mm.then_inc(xT_ready, 1)
                    if k == 7 and has(t - 2):
                        if has(t):
                            pe.wait_ge(hT_ready, t + 1)
                        elif has(n):
                            pe.wait_ge(v_ready, 4 * n + 4)
                        if has(m):
                            pe.wait_ge(upd, 4 * (2 * m + 2))
                        out_projection(t - 2, 0)
            run_steps(pe, step, 3)


def router_phase(nc, a, v):
    E3 = [P, B, NE]
    with ExitStack() as c:
        sem = c.enter_context(phase_semaphores(nc, "rt_"))
        sb = lambda name, shape, dt=F32: c.enter_context(nc.sbuf_tensor("rt_" + name, shape, dt))
        bank = lambda name: c.enter_context(nc.psum_tensor("rt_" + name, [P, 512], F32))
        xn = sb("xn", [P, 2, 2, D])
        logits, score, sel = sb("logits", E3), sb("score", E3), sb("sel", E3)
        hit, key, rank, tmp = sb("hit", E3), sb("key", E3), sb("rank", E3), sb("tmp", E3)
        chosen = [sb("chosen0", E3), sb("chosen1", E3)]
        best, denom, big, inv = [sb(n, [P, B]) for n in ("best", "denom", "big", "inv")]
        turnb, logitb = [bank("turn0"), bank("turn1")], [bank("logit0"), bank("logit1")]
        ln = {k: sem(k) for k in ["var_ready", "root_ready", "chain"]}
        ln_done, xT_ready, hT_ready, logit_psum, logit_ready = (sem("ln_done"), sem("xT_ready"), sem("hT_ready"),
                                                                sem("logit_psum"), sem("logit_ready"))
        rank_ready, e_ready, g = sem("rank_ready"), sem("e_ready"), sem("gate")
        block = c.enter_context(nc.Block())

        @block.gpsimd
        def _(pool):
            for e in range(NE):
                last = pool.memset(rank[:, :, e:e + 1], float(NE - e))
                last.then_inc(rank_ready, 1)

        @block.scalar
        def _(act):
            ln_scale_act(act, v, ln)

            def step(t, p, has):
                if has(t):
                    act.wait_ge(xT_ready, t + 1)
                    act.copy(v["hT_all"][:, t, :] if isinstance(t, int) else v["hT_all"][:, bass.ds(t, 1), :],
                             turnb[p][:, 0:W2] if isinstance(t, int) else turnb[p][:, 0:W2].unsqueeze(1)).then_inc(hT_ready, 1)
                    act.copy(v["hT_two"][:, p, :], turnb[p][:, 0:W2]).then_inc(hT_ready, 1)
            run_steps(act, step, 0)
            act.wait_ge(logit_ready, NP)
            act.activation(score[:], logits[:], ACT.Exp, scale=-1.0).then_inc(e_ready, 1)

        @block.tensor
        def _(pe):
            def step(t, p, has):
                q = 1 - p
                if has(t):
                    pe.wait_ge(ln_done, 2 * (t + 1))
                    wait(pe, hT_ready, 2 * (t - 1))
                    for b in range(2):
                        mm = pe.transpose(turnb[p][:, b * S:(b + 1) * S], xn[:, p, b, :], v["ident"][:])
                    mm.then_inc(xT_ready, 1)
                n = t - 1
                if has(n):
                    pe.wait_ge(hT_ready, 2 * (n + 1))
                    wait(pe, logit_ready, n - 1)
                    for b in range(2):
                        mm = pe.matmul(logitb[q][:, b * NE:(b + 1) * NE], v["hT_two"][:, q, b * S:(b + 1) * S],
                                       v["router_t"][:], start=True, stop=True)
                    mm.then_inc(logit_psum, 1)
            run_steps(pe, step, 1)

        @block.vector
        def _(dve):
            ln_scale_dve(dve, v, ln)

            def step(t, p, has):
                q = 1 - p
                if has(t):
                    wait(dve, xT_ready, t - 1)
                    for b in range(2):
                        apply_ln(dve, v, xn[:, p, b:b + 1, :], t * 2 + b, ln_done)
                n = t - 1
                if has(n):
                    dve.wait_ge(logit_psum, n + 1)
                    dve.tensor_copy(logits[:, bass.ds(n * 2, 2), :],
                                    logitb[q][:, 0:2 * NE].rearrange("p (b e) -> p b e", b=2)).then_inc(logit_ready, 1)
            run_steps(dve, step, 1)
            dve.wait_ge(rank_ready, NE)
            dve.wait_ge(e_ready, 1)
            wide = lambda t: t[:].unsqueeze(2).to_broadcast(E3)
            dve.tensor_scalar(tmp[:], score[:], 1.0, None, ALU.add).then_inc(g, 1)
            dve.wait_ge(g, 1)
            dve.reciprocal(score[:], tmp[:]).then_inc(g, 1)
            dve.wait_ge(g, 2)
            dve.tensor_tensor(sel[:], score[:], v["L1_ffn_router_bias"][:].unsqueeze(1).to_broadcast(E3), ALU.add).then_inc(g, 1)
            n = 3
            for i in range(2):
                dve.wait_ge(g, n)
                dve.tensor_reduce(best[:], sel[:], AX.X, ALU.max).then_inc(g, 1)
                dve.wait_ge(g, n + 1)
                dve.tensor_tensor(hit[:], sel[:], wide(best), ALU.is_equal).then_inc(g, 1)
                dve.wait_ge(g, n + 2)
                dve.tensor_tensor(key[:], hit[:], rank[:], ALU.mult).then_inc(g, 1)
                dve.wait_ge(g, n + 3)
                dve.tensor_reduce(best[:], key[:], AX.X, ALU.max).then_inc(g, 1)
                dve.wait_ge(g, n + 4)
                dve.tensor_tensor(chosen[i][:], key[:], wide(best), ALU.is_equal).then_inc(g, 1)
                dve.wait_ge(g, n + 5)
                n += 5
                if i == 0:
                    dve.scalar_tensor_tensor(sel[:], chosen[0][:], MASKED, sel[:], ALU.mult, ALU.add).then_inc(g, 1)
                    n += 1
            dve.tensor_tensor(chosen[0][:], chosen[0][:], chosen[1][:], ALU.add).then_inc(g, 1)
            dve.wait_ge(g, n + 1)
            dve.tensor_tensor(tmp[:], score[:], chosen[0][:], ALU.mult).then_inc(g, 1)
            dve.wait_ge(g, n + 2)
            dve.tensor_reduce(denom[:], tmp[:], AX.X, ALU.add).then_inc(g, 1)
            dve.wait_ge(g, n + 3)
            dve.tensor_scalar(big[:], denom[:], 1e-9, None, ALU.is_gt).then_inc(g, 1)
            dve.tensor_scalar(denom[:], denom[:], 1e-9, None, ALU.add).then_inc(g, 1)
            dve.wait_ge(g, n + 5)
            dve.reciprocal(inv[:], denom[:]).then_inc(g, 1)
            dve.wait_ge(g, n + 6)
            dve.tensor_tensor(inv[:], inv[:], big[:], ALU.mult).then_inc(g, 1)
            dve.tensor_scalar(big[:], big[:], -0.5, 0.5, ALU.mult, ALU.add).then_inc(g, 1)
            dve.wait_ge(g, n + 8)
            dve.tensor_tensor(tmp[:], tmp[:], wide(inv), ALU.mult).then_inc(g, 1)
            dve.tensor_tensor(chosen[0][:], chosen[0][:], wide(big), ALU.mult).then_inc(g, 1)
            dve.wait_ge(g, n + 10)
            dve.tensor_tensor(v["gates"][:], tmp[:], chosen[0][:], ALU.add)


def experts_phase(nc, a, v):
    with ExitStack() as c:
        sem = c.enter_context(phase_semaphores(nc, "ex_"))
        passed = {eng: sem("passed_" + eng) for eng in ("dve", "pool", "sp")}
        sb = lambda name, shape, dt=F32: c.enter_context(nc.sbuf_tensor("ex_" + name, shape, dt))
        bank = lambda name: c.enter_context(nc.psum_tensor("ex_" + name, [P, 512], F32))
        th, up, act_in = sb("th", [P, 512]), sb("up", [P, 512]), sb("act_in", [P, 2, 512])
        g = sb("g", [P, 2, NE, W2])
        gateb, linb, hidb = bank("gate"), bank("lin"), [bank("hid0"), bank("hid1")]
        yb, sharedb = [bank("y0"), bank("y1")], bank("shared")
        shared_psum, tanh_done, silu_mid, act_ready = sem("shared_psum"), sem("tanh_done"), sem("silu_mid"), sem("act_ready")
        hid_psum, g_ready, y_psum, shared_y, upd, stored = (sem("hid_psum"), sem("g_ready"), sem("y_psum"),
                                                            sem("shared_y"), sem("upd"), sem("stored"))
        out = a["out"].rearrange("b t d -> t b d")
        UP = NE * 2 + 1
        block = c.enter_context(nc.Block())

        @block.sync
        def _(sp):
            def step(t, p, has):
                n = t - 1
                if has(n):
                    sp.wait_ge(upd, UP * (n + 1))
                    sp.dma_start(out[:, bass.ds(n * 2, 2), :], v["x"][:, bass.ds(n * 2, 2), :]).then_inc(stored, 16)
            run_steps(sp, step, 1)
            sp.wait_ge(stored, 16 * NP)

        @block.scalar
        def _(act):
            def step(t, p, has):
                if has(t):
                    act.wait_ge(shared_psum, t + 1)
                    wait(act, silu_mid, t)
                    act.activation(th[:], gateb[:], ACT.Tanh, scale=0.5).then_inc(tanh_done, 1)
                    wait(act, y_psum, 4 * (t - 1))
                    for i in range(NE // 2):
                        act.wait_ge(hid_psum, 4 * t + i + 1)
                        act.activation(g[:, p, 2 * i:2 * i + 2, :].rearrange("p e t -> p (e t)"), hidb[i % 2][:],
                                       ACT.Gelu).then_inc(g_ready, 1)
            run_steps(act, step, 0)

        @block.vector
        def _(dve):
            def step(t, p, has):
                q = 1 - p
                if has(t):
                    dve.wait_ge(tanh_done, t + 1)
                    wait(dve, act_ready, t)
                    dve.scalar_tensor_tensor(up[:], th[:], 1.0, gateb[:], ALU.add, ALU.mult).then_inc(silu_mid, 1)
                    dve.wait_ge(silu_mid, t + 1)
                    wait(dve, shared_y, t - 1)
                    dve.scalar_tensor_tensor(act_in[:, p, :], up[:], 0.5, linb[:], ALU.mult, ALU.mult).then_inc(act_ready, 1)
                n = t - 1
                if has(n):
                    k = UP * n
                    xs = v["x"][:, bass.ds(n * 2, 2), :]
                    dve.wait_ge(shared_y, n + 1)
                    wait(dve, upd, k)
                    dve.tensor_tensor(xs, xs, sharedb[:, 0:W2].rearrange("p (b d) -> p b d", b=2), ALU.add).then_inc(upd, 1)
                    for i in range(4):
                        dve.wait_ge(y_psum, 4 * n + i + 1)
                        for e in range(2):
                            for b in range(2):
                                if b == 0:
                                    dve.wait_ge(upd, k + 1 + 4 * i + 2 * e)
                                x1 = v["x"][:, bass.ds(n * 2 + b, 1), :]
                                gate = v["gates"][:, bass.ds(n * 2 + b, 1), 2 * i + e:2 * i + e + 1]
                                dve.scalar_tensor_tensor(
                                    x1, yb[i % 2][:, (2 * e + b) * D:(2 * e + b + 1) * D].unsqueeze(1),
                                    gate.rearrange("p a b -> p (a b)"), x1, ALU.mult, ALU.add).then_inc(upd, 1)
            run_steps(dve, step, 1)

        @block.tensor
        def _(pe):
            def step(t, p, has):
                q = 1 - p
                n = t - 1
                if has(t):
                    h = v["hT_all"][:, t, :] if isinstance(t, int) else v["hT_all"][:, bass.ds(t, 1), :].rearrange("p a t -> p (a t)")
                    wait(pe, act_ready, t)
                    for j in range(2):
                        pe.matmul(gateb[:, j * W2:(j + 1) * W2], v["L1_ffn_sw1"][:, j * P:(j + 1) * P], h, start=True, stop=True)
                    for j in range(2):
                        mm = pe.matmul(linb[:, j * W2:(j + 1) * W2], v["L1_ffn_sw3"][:, j * P:(j + 1) * P], h, start=True, stop=True)
                    mm.then_inc(shared_psum, 1)
                for i in range(4):
                    if has(t):
                        wait(pe, g_ready, 4 * t + i - 1)
                        for e in range(2):
                            mm = pe.matmul(hidb[i % 2][:, e * W2:(e + 1) * W2], v["L1_ffn_ew1"][:, 2 * i + e, :], h, start=True, stop=True)
                        mm.then_inc(hid_psum, 1)
                    if has(n):
                        if i == 0:
                            pe.wait_ge(act_ready, n + 1)
                            wait(pe, upd, UP * (n - 1) + 1)
                            for b in range(2):
                                for j in range(2):
                                    mm = pe.matmul(sharedb[:, b * D:(b + 1) * D], act_in[:, q, j * W2 + b * S:j * W2 + (b + 1) * S],
                                                   v["L1_ffn_sw2"][:, j, :], start=(j == 0), stop=(j == 1))
                            mm.then_inc(shared_y, 1)
                        pe.wait_ge(g_ready, 4 * n + i + 1)
                        wait(pe, upd, UP * n + 1 + 4 * (i - 1) if i >= 2 else UP * (n - 1) + 1 + 4 * (i + 3))
                        for e in range(2):
                            for b in range(2):
                                mm = pe.matmul(yb[i % 2][:, (2 * e + b) * D:(2 * e + b + 1) * D],
                                               g[:, q, 2 * i + e, b * S:(b + 1) * S], v["L1_ffn_ew2"][:, 2 * i + e, :],
                                               start=True, stop=True)
                        mm.then_inc(y_psum, 1)
            run_steps(pe, step, 1)


INPUTS = ["x", "ctx_1024", "mask_Bx1xSxS2_ff0", "mask_Bx1x1xS2_ff0",
          "L0_attn_Wk", "L0_attn_bk", "L0_attn_Wv", "L0_attn_bv", "L0_attn_Wf", "L0_attn_bf",
          "L0_xattn_wq", "L0_xattn_wk", "L0_xattn_wv", "L0_xattn_wo",
          "L0_ffn_W_exp", "L0_ffn_b_exp", "L0_ffn_up_weights", "L0_ffn_up_bias", "L0_ffn_down_weights",
          "L0_ffn_W_con", "L0_ffn_b_con", "L0_ffn_down_bias",
          "L1_attn_wq", "L1_attn_bq", "L1_attn_wk", "L1_attn_bk", "L1_attn_wv", "L1_attn_bv", "L1_attn_wo",
          "L1_attn_bo", "L1_xattn_Wq", "L1_xattn_bq", "L1_xattn_Wk", "L1_xattn_bk", "L1_xattn_Wv", "L1_xattn_bv",
          "L1_ffn_router_w", "L1_ffn_router_bias", "L1_ffn_sw1", "L1_ffn_sw3", "L1_ffn_sw2", "L1_ffn_ew1",
          "L1_ffn_ew2"]


def rope_tables():
    theta = np.float32(10000.0) ** (np.arange(0, HD1, 2, dtype=np.float32) / np.float32(HD1))
    freqs = np.arange(S, dtype=np.float32)[:, None] * (np.float32(1.0) / theta)[None, :]
    emb = np.concatenate([freqs, freqs], axis=-1).astype(np.float64).T
    sign = np.where(np.arange(HD1) % 2 == 0, -1.0, 1.0)[:, None]
    return (np.tile(np.cos(emb), (2, 1)).astype(np.float32), np.tile(np.sin(emb) * sign, (2, 1)).astype(np.float32))


def build_program(nc, a):
    a = dict(a)
    a["part_scratch"] = nc.dram_tensor("part_scratch", [2, 2, 3, DH, H, W2], BF16, kind="Internal").ap()
    a["mask_scratch"] = nc.dram_tensor("mask_scratch", [3, B, S], BF16, kind="Internal").ap()
    with ExitStack() as c:
        v = {}

        def keep(name, shape, dt=F32):
            v[name] = c.enter_context(nc.sbuf_tensor("v_" + name, shape, dt))
        keep("x", [P, B, D])
        for name in ["vareps", "root", "rstd0", "newton", "rstd", "shift"]:
            keep(name, [P, B])
        keep("moments", [P, B, 2])
        keep("aggr", [P, 2, 2])
        keep("ident", [P, P])
        keep("ident_bf", [P, P], BF16)
        keep("causal", [P, S], BF16)
        keep("causal_t", [P, S], BF16)
        keep("ones", [P, SLOT])
        keep("ones_bf", [P, W2], BF16)
        for name in ["L0_attn_Wk", "L1_xattn_Wq", "L1_xattn_Wk", "L1_xattn_Wv", "L0_xattn_wq", "L0_xattn_wk",
                     "L0_xattn_wv", "L0_xattn_wo", "L0_attn_bf", "L1_xattn_bv", "L1_attn_bo", "L0_ffn_b_con",
                     "L0_ffn_down_bias", "ffn_bias", "rope_cos", "rope_sin"]:
            keep(name, [P, D])
        for name in ["L0_attn_Wv", "L0_ffn_W_exp", "W_up"]:
            keep(name, [P, FH])
        for name in ["L0_attn_Wf", "W_down"]:
            keep(name, [P, NJ, D])
        keep("L1_ffn_sw1", [P, SH])
        keep("L1_ffn_sw3", [P, SH])
        keep("L1_ffn_sw2", [P, SH // P, D])
        keep("router_t", [P, NE])
        keep("L1_ffn_router_bias", [P, NE])
        keep("gates", [P, B, NE])
        for name in ["L0_attn_bk", "L1_xattn_bq", "L1_xattn_bk"]:
            keep(name, [P, 1])
        for name in ["L0_attn_bv", "L0_ffn_up_bias", "up_bias", "up_bias_row"]:
            keep(name, [P, NJ])
        setup_phase(nc, a, v)
        with ExitStack() as own:
            v["o_all"] = own.enter_context(nc.sbuf_tensor("v_o_all", [P, NP, NJ, W2], F32))
            narrow_attention(nc, a, v, "self")
            gelu_projection(nc, a, v)
        narrow_attention(nc, a, v, "cross0")
        keep("L1_ffn_ew1", [P, NE, P])
        keep("L1_ffn_ew2", [P, NE, D])
        for name in ["wqT", "wkT", "wvT", "woT", "wqT_swapped", "wkT_swapped"]:
            keep(name, [P, J1, P])
        for name in ["L1_attn_bq", "L1_attn_bk", "L1_attn_bv", "L1_attn_bq_swapped", "L1_attn_bk_swapped"]:
            keep(name, [P, J1])
        weights_phase(nc, a, v)
        ffn_phase(nc, a, v)
        rotary_attention(nc, a, v)
        narrow_attention(nc, a, v, "cross1")
        v["hT_all"] = c.enter_context(nc.sbuf_tensor("v_hT_all", [P, NP, W2], F32))
        v["hT_two"] = c.enter_context(nc.sbuf_tensor("v_hT_two", [P, 2, W2], F32))
        router_phase(nc, a, v)
        experts_phase(nc, a, v)


def kernel(**inputs):
    import concourse.bacc as bacc
    from concourse.bass_utils import run_bass_kernel_spmd

    nc = bacc.Bacc("TRN2", target_bir_lowering=False, num_devices=1)
    cos, sin = rope_tables()
    given = {name: np.ascontiguousarray(inputs[name]) for name in INPUTS}
    given["rope_cos"], given["rope_sin"] = cos, sin
    arrays, aps = {}, {}
    for name, value in given.items():
        arrays["in_" + name] = value
        aps[name] = nc.dram_tensor("in_" + name, value.shape, mybir.dt.from_np(value.dtype), kind="ExternalInput").ap()
    aps["out"] = nc.dram_tensor("out_x", [B, S, D], F32, kind="ExternalOutput").ap()
    build_program(nc, aps)
    result = run_bass_kernel_spmd(nc, [arrays], core_ids=[0])
    return result.results[0]["out_x"]
```

```python
from contextlib import ExitStack, contextmanager

import numpy as np

import concourse.bass as bass
from concourse import mybir

ALU = mybir.AluOpType
ACT = mybir.ActivationFunctionType
AX = mybir.AxisListType
F32 = mybir.dt.float32
BF16 = mybir.dt.bfloat16

P = 128
B = 32
S = 128
D = 128
H = 16
DH = D // H
NP = B // 2
W2 = 2 * S
G = 4
NG = H // G
FH = 512
NJ = FH // P
HD1 = 64
J1 = H * HD1 // P
NE = 8
SH = 256
SLOT = 32
MAIN = 96
MASKED = -1e30
PEEL = 4
EPS = 1e-5


@contextmanager
def phase_semaphores(nc, prefix):
    taken = []

    def sem(name):
        taken.append(nc.alloc_semaphore(name=prefix + name))
        return taken[-1]
    yield sem
    nc.clear_and_free_semaphores(taken)
    nc.all_engine_barrier()


def wait(eng, sem, value):
    if isinstance(value, int) and value <= 0:
        return
    eng.wait_ge(sem, value)


def wait_alone(eng, passed, sem, value):
    wait(eng, sem, value)
    eng.sem_inc(passed, 1)


def of_parity(n, parity, each):
    return (n - parity) * (each // 2) + each


def run_steps(eng, step, depth, peel=PEEL):
    def exists(n):
        return 0 <= n < NP
    for t in range(peel):
        step(t, t % 2, exists)
    with eng.Fori(peel // 2, NP // 2) as i:
        step(i * 2, 0, lambda n: True)
        step(i * 2 + 1, 1, lambda n: True)
    for t in range(NP, NP + depth):
        step(t, t % 2, exists)


def ln_scale_dve(dve, v, ln):
    var = v["moments"][:, :, 1]
    dve.tensor_scalar(v["vareps"][:], var, EPS, None, ALU.add).then_inc(ln["var_ready"], 1)
    dve.wait_ge(ln["root_ready"], 1)
    dve.reciprocal(v["rstd0"][:], v["root"][:]).then_inc(ln["chain"], 1)
    dve.wait_ge(ln["chain"], 1)
    dve.tensor_tensor(v["newton"][:], v["rstd0"][:], v["rstd0"][:], ALU.mult).then_inc(ln["chain"], 1)
    dve.wait_ge(ln["chain"], 2)
    dve.tensor_tensor(v["newton"][:], v["newton"][:], v["vareps"][:], ALU.mult).then_inc(ln["chain"], 1)
    dve.wait_ge(ln["chain"], 3)
    dve.tensor_scalar(v["newton"][:], v["newton"][:], -0.5, 1.5, ALU.mult, ALU.add).then_inc(ln["chain"], 1)
    dve.wait_ge(ln["chain"], 4)
    dve.tensor_tensor(v["rstd"][:], v["rstd0"][:], v["newton"][:], ALU.mult).then_inc(ln["chain"], 1)
    dve.wait_ge(ln["chain"], 5)
    dve.scalar_tensor_tensor(v["shift"][:], v["moments"][:, :, 0], -1.0, v["rstd"][:], ALU.mult,
                             ALU.mult).then_inc(ln["chain"], 1)
    dve.wait_ge(ln["chain"], 6)


def ln_scale_act(act, v, ln):
    act.wait_ge(ln["var_ready"], 1)
    act.activation(v["root"][:], v["vareps"][:], ACT.Sqrt).then_inc(ln["root_ready"], 1)


def apply_ln(dve, v, out, b, sem, by_place=False):
    src = v["x"][:, bass.ds(b, 1), :]
    if by_place:
        src = src.rearrange("p o (h d) -> p (o h) d", h=H)
        out = out.rearrange("p o (d h) -> p (o h) d", h=H)
    dve.tensor_scalar(out, src, v["rstd"][:, bass.ds(b, 1)], v["shift"][:, bass.ds(b, 1)],
                      ALU.mult, ALU.add).then_inc(sem, 1)


UPDATES = 6


def update_x(dve, v, n, add, passed, upd):
    base = UPDATES * n
    wait(dve, upd, base)
    xs = v["x"][:, bass.ds(n * 2, 2), :]
    dve.tensor_tensor(xs, xs, add, ALU.add).then_inc(upd, 1)
    for b in range(2):
        wait_alone(dve, passed, upd, base + 1)
        dve.bn_stats(v["stats"][:, b, :], v["x"][:, bass.ds(n * 2 + b, 1), :]).then_inc(upd, 1)
    for b in range(2):
        wait_alone(dve, passed, upd, base + 2 + b)
        dve.bn_aggr(v["aggr"][:, b, :], v["stats"][:, b, :]).then_inc(upd, 1)
    dve.wait_ge(upd, base + 5)
    dve.tensor_copy(v["moments"][:, bass.ds(n * 2, 2), :], v["aggr"][:]).then_inc(upd, 1)


def setup_phase(nc, a, v):
    with ExitStack() as c:
        sem = c.enter_context(phase_semaphores(nc, "setup_"))
        passed = {eng: sem("passed_" + eng) for eng in ("dve", "pool", "sp")}
        stats = c.enter_context(nc.sbuf_tensor("xstats", [P, B, 6], F32))
        maskrow = c.enter_context(nc.sbuf_tensor("maskrow", [B, 4, S], F32))
        maskpart = c.enter_context(nc.sbuf_tensor("maskpart", [B, 3, S], BF16))
        x_loaded = [sem(f"x_loaded{i}") for i in range(4)]
        small_loaded = sem("small_loaded")
        ident_zero, ident_ready, masks_zero, masks_ready = (sem("ident_zero"), sem("ident_ready"),
                                                            sem("masks_zero"), sem("masks_ready"))
        consts_ready = sem("consts_ready")
        stat_ready, mask_chain, mask_stored = sem("stat_ready"), sem("mask_chain"), sem("mask_stored")
        small = []
        for name in ["L0_attn_Wk", "L0_attn_Wv", "L1_xattn_Wq", "L1_xattn_Wk", "L1_xattn_Wv", "L0_xattn_wq",
                     "L0_xattn_wk", "L0_xattn_wv", "L0_xattn_wo", "L1_ffn_sw1", "L1_ffn_sw3", "L0_ffn_W_exp",
                     "router_t", "rope_cos", "rope_sin", "L0_attn_bk", "L1_xattn_bq", "L1_xattn_bk",
                     "L0_attn_bv", "L0_ffn_up_bias"]:
            small.append((v[name][:], a[name]))
        small.append((v["L0_attn_Wf"][:], a["L0_attn_Wf"].rearrange("(j p) d -> p j d", p=P)))
        small.append((v["L1_ffn_sw2"][:], a["L1_ffn_sw2"].rearrange("(j p) d -> p j d", p=P)))
        small.append((maskrow[:, 0, :], a["mask_Bx1x1xS2_ff0"].rearrange("b o t k -> b (o t k)")))
        for name in ["L0_attn_bf", "L1_xattn_bv", "L1_attn_bo", "L0_ffn_b_con", "L0_ffn_down_bias"]:
            small.append((v[name][:], a[name].rearrange("(o d) -> o d", o=1).to_broadcast([P, D])))
        small.append((v["L1_ffn_router_bias"][:],
                      a["L1_ffn_router_bias"].rearrange("(o d) -> o d", o=1).to_broadcast([P, NE])))

        block = c.enter_context(nc.Block())

        @block.sync
        def _(sp):
            xt = a["x"].rearrange("b t d -> t b d")
            for i in range(4):
                sp.dma_start(v["x"][:, 8 * i:8 * i + 8, :], xt[:, 8 * i:8 * i + 8, :]).then_inc(x_loaded[i], 16)
            for dst, src in small:
                sp.dma_start(dst, src).then_inc(small_loaded, 16)
            sp.wait_ge(small_loaded, 16 * len(small))
            sp.wait_ge(mask_chain, 6)
            sp.dma_start(a["mask_scratch"].rearrange("c b k -> b c k"), maskpart[:]).then_inc(mask_stored, 16)
            sp.wait_ge(mask_stored, 16)

        @block.gpsimd
        def _(pool):
            pool.memset(v["ident"][:], 0.0).then_inc(ident_zero, 1)
            pool.wait_ge(ident_zero, 1)
            pool.affine_select(out=v["ident"][:], in_=v["ident"][:], compare_op=ALU.not_equal, fill=1.0,
                               base=0, pattern=[[-1, P]], channel_multiplier=1).then_inc(ident_ready, 1)
            pool.memset(v["causal"][:], 0.0).then_inc(masks_zero, 1)
            pool.memset(v["causal_t"][:], 0.0).then_inc(masks_zero, 1)
            pool.wait_ge(masks_zero, 2)
            pool.affine_select(out=v["causal"][:], in_=v["causal"][:], compare_op=ALU.is_ge, fill=MASKED,
                               base=0, pattern=[[-1, S]], channel_multiplier=1).then_inc(masks_ready, 1)
            pool.affine_select(out=v["causal_t"][:], in_=v["causal_t"][:], compare_op=ALU.is_ge, fill=MASKED,
                               base=0, pattern=[[1, S]], channel_multiplier=-1).then_inc(masks_ready, 1)
            pool.memset(v["ones"][:], 1.0)
            pool.memset(v["ones_bf"][:], 1.0).then_inc(consts_ready, 1)
            pool.wait_ge(ident_ready, 1)
            pool.tensor_copy(v["ident_bf"][:], v["ident"][:]).then_inc(consts_ready, 1)

        @block.vector
        def _(dve):
            for b in range(B):
                if b % 8 == 0:
                    dve.wait_ge(x_loaded[b // 8], 16)
                dve.bn_stats(stats[:, b, :], v["x"][:, b, :]).then_inc(stat_ready, 1)
            for b in range(B):
                dve.wait_ge(stat_ready, b + 1)
                dve.bn_aggr(v["moments"][:, b, :], stats[:, b, :]).then_inc(stat_ready, 1)
            dve.wait_ge(small_loaded, 16 * len(small))
            row = maskrow[:]
            dve.tensor_copy(maskpart[:, 0, :], row[:, 0, :]).then_inc(mask_chain, 1)
            dve.wait_ge(mask_chain, 1)
            dve.tensor_tensor(row[:, 1, :], row[:, 0, :], maskpart[:, 0, :], ALU.subtract).then_inc(mask_chain, 1)
            dve.wait_ge(mask_chain, 2)
            dve.tensor_copy(maskpart[:, 1, :], row[:, 1, :]).then_inc(mask_chain, 1)
            dve.wait_ge(mask_chain, 3)
            dve.tensor_tensor(row[:, 2, :], row[:, 1, :], maskpart[:, 1, :], ALU.subtract).then_inc(mask_chain, 1)
            dve.wait_ge(mask_chain, 4)
            dve.tensor_copy(maskpart[:, 2, :], row[:, 2, :]).then_inc(mask_chain, 2)
            for name in ["L0_xattn_wq", "L1_xattn_Wq", "L1_xattn_bq"]:
                dve.tensor_scalar(v[name][:], v[name][:], DH ** -0.5, None, ALU.mult)
            dve.tensor_tensor(v["ffn_bias"][:], v["L0_ffn_b_con"][:], v["L0_ffn_down_bias"][:], ALU.add)


def narrow_attention(nc, a, v, kind):
    own, cross = kind == "self", kind != "self"
    pre = {"self": "L0_attn", "cross0": "L0_xattn", "cross1": "L1_xattn"}[kind]
    wq = None if own else v[pre + ("_wq" if kind == "cross0" else "_Wq")]
    wk = v[{"self": "L0_attn_Wk", "cross0": "L0_xattn_wk", "cross1": "L1_xattn_Wk"}[kind]]
    wv = v[{"self": "L0_attn_Wv", "cross0": "L0_xattn_wv", "cross1": "L1_xattn_Wv"}[kind]]
    VW = FH // H if own else SLOT
    NV = 2 if own else 1
    with ExitStack() as c:
        sem = c.enter_context(phase_semaphores(nc, kind + "_"))
        by_parity = lambda name: [sem(f"{name}{i}") for i in range(2)]
        sb = lambda name, shape, dt=F32: c.enter_context(nc.sbuf_tensor(f"{kind}_{name}", shape, dt))
        bank = lambda name: c.enter_context(nc.psum_tensor(f"{kind}_{name}", [P, 512], F32))
        passed = {eng: sem("passed_" + eng) for eng in ("dve", "pool", "sp")}
        xn = sb("xn", [P, 2, 2, D])
        ctx = sb("ctx", [P, 2, 2, D]) if cross else None
        hT = sb("hT", [P, 2, 1 if own else 2, W2])
        qk = sb("qk", [P, 2, 2, W2])
        rest = sb("rest", [P, 2 * W2])
        part = sb("part", [P, 2, 3, 2, W2], BF16)
        qs = sb("qs", [P, 2, 2, H, S], BF16)
        ks = sb("ks", [P, 2, 2, H, S], BF16)
        vals = sb("vals", [P, 2, 2, H, VW])
        negmax = sb("negmax", [P, 2, 2, H])
        mrest = sb("mrest", [P, H])
        mpart = sb("mpart", [P, 2, 3 * H], BF16)
        mT = sb("mT", [3 * H, 2, 2, S], BF16)
        expT = sb("expT", [P, NG, G * S])
        recip = sb("recip", [P, 512])
        if kind == "cross0":
            mraw = sb("mraw", [P, 2, 2, S])
            mask_rest = sb("mask_rest", [P, W2])
            mask_a = sb("mask_a", [P, 2, 3, 2, S], BF16)
            mask_b = sb("mask_b", [P, 2, 3, 2, S], BF16)
        if cross:
            oS = sb("oS", [P, 2, 512])
            on = sb("on", [P, 2, D])
            onT = sb("onT", [P, 2, S])
            v = dict(v, stats=sb("stats", [P, 2, 6]))
        scoreA = [bank("scoreA0"), bank("scoreA1")]
        scoreB = [bank("scoreB0"), bank("scoreB1")]
        turnb, projb = bank("turnb"), bank("projb")
        if own:
            unit_pair = [bank("units01"), bank("units23")]
        else:
            outb, endb = bank("outb"), bank("endb")
        ln = {k: sem(k) for k in ["var_ready", "root_ready", "chain"]}
        rows_set, ones_rows = sem("rows_set"), sem("ones_rows")
        ctx_loaded, mask_loaded = by_parity("ctx_loaded"), by_parity("mask_loaded")
        stacked = [by_parity("stacked_first"), by_parity("stacked_second")]
        m_rows = [by_parity("m_rows_first"), by_parity("m_rows_second")]
        scr_written = sem("scr_written")
        ln_done, x_pre, x_mid = sem("ln_done"), sem("x_pre"), sem("x_mid")
        xT_ready, hT_ready, qk_psum, qk_ready = sem("xT_ready"), sem("hT_ready"), sem("qk_psum"), sem("qk_ready")
        part1, pool_split, part3 = sem("part1"), sem("pool_split"), sem("part3")
        v_psum, v_ready = sem("v_psum"), sem("v_ready")
        a_ready, max_done, pool_msplit, mpart_ready, mT_psum, mT_ready = (
            sem("a_ready"), sem("max_done"), sem("pool_msplit"), sem("mpart_ready"), sem("mT_psum"), sem("mT_ready"))
        b_ready, exp_done, pv_done = sem("b_ready"), sem("exp_done"), sem("pv_done")
        recip_done, norm_done = sem("recip_done"), sem("norm_done")
        o_copied, nat_ready, onT_psum, onT_ready, y_ready, upd = (
            sem("o_copied"), sem("nat_ready"), sem("onT_psum"), sem("onT_ready"), sem("y_ready"), sem("upd"))
        mask_p1, pool_mask, mask_p3, mask_turned, mask_copied = (
            sem("mask_p1"), sem("pool_mask"), sem("mask_p3"), sem("mask_turned"), sem("mask_copied"))
        scr = a["part_scratch"]
        KROWS = [0, 24, 40]
        STACKED = 16 * (7 if kind == "cross1" else 6)

        block = c.enter_context(nc.Block())

        def lagged(t, u, lag):
            return (t - 3, u - lag) if u >= lag else (t - 4, u - lag + 8)

        @block.sync
        def _(sp):
            if cross:
                xt = a["ctx_1024"].rearrange("b t d -> t b d")
                mt = a["mask_Bx1xSxS2_ff0"].rearrange("b o q k -> q (b o) k")
            ones = v["ones_bf"][0:3, 0:S].unsqueeze(1).to_broadcast([3, H, S])
            sp.wait_ge(rows_set, 6)
            for p in range(2):
                for b in range(2):
                    sp.dma_start(ks[MAIN:MAIN + 3, p, b, :, :], ones).then_inc(ones_rows, 16)
                    if kind == "cross1":
                        sp.dma_start(qs[48:51, p, b, :, :], ones).then_inc(ones_rows, 16)
            sp.wait_ge(ones_rows, 16 * (8 if kind == "cross1" else 4))

            def stack(n, q, b):
                by_part = scr[q].rearrange("(k s b) d h t -> k s b d h t", k=3, s=2)
                for k in range(3):
                    m = 3 - k
                    r = KROWS[k]
                    sp.dma_start(qs[r:r + 8 * m, q, b, :, :].rearrange("p h t -> p (h t)"),
                                 by_part[k:k + 1, 0, b].to_broadcast([m, DH, H, S]).rearrange(
                                     "m d h t -> m d (h t)")).then_inc(stacked[b][q], 16)
                    sp.dma_start(ks[r:r + 8 * m, q, b, :, :].rearrange("p h t -> p (h t)"),
                                 by_part[0:m, 1, b].rearrange("m d h t -> m d (h t)")).then_inc(stacked[b][q], 16)
                if kind == "cross1":
                    sp.dma_start(ks[48:51, q, b, :, :], a["mask_scratch"][:, bass.ds(n * 2 + b, 1), :].to_broadcast(
                        [3, H, S])).then_inc(stacked[b][q], 16)

            def max_rows(k, p, b):
                sp.wait_ge(mT_ready, 2 * k + b + 1)
                sp.dma_start(qs[MAIN:MAIN + 3, p, b, :, :], mT[:, p, b, :]).then_inc(m_rows[b][p], 16)

            def step(t, p, has):
                q = 1 - p
                if cross and has(t):
                    wait(sp, xT_ready, t - 1)
                    sp.dma_start(ctx[:, p, :, :], xt[:, bass.ds(t * 2, 2), :]).then_inc(ctx_loaded[p], 16)
                    if kind == "cross0":
                        wait(sp, mask_p3, t - 1)
                        sp.dma_start(mraw[:, p, :, :], mt[:, bass.ds(t * 2, 2), :]).then_inc(mask_loaded[p], 16)
                n, k = t - 1, t - 2
                if has(k):
                    wait(sp, b_ready, 8 * (k - 1))
                    stack(k, p, 1)
                if has(t - 3):
                    max_rows(t - 3, q, 1)
                if has(n):
                    sp.wait_ge(part3, n + 1)
                    for b in range(2):
                        wait(sp, stacked[b][q], of_parity(n - 2, q, STACKED))
                    sp.dma_start(scr[q].rearrange("c d h t -> (d h) c t"),
                                 part[:, q, :, :, :].rearrange("p k s (b t) -> p (k s b) t", t=S)).then_inc(scr_written, 16)
                    wait_alone(sp, passed["sp"], scr_written, 16 * (n + 1))
                    wait(sp, b_ready, 8 * (n - 1) - 4)
                    stack(n, q, 0)
                if has(k):
                    max_rows(k, p, 0)
            run_steps(sp, step, 4, 6)

        @block.gpsimd
        def _(pool):
            for tile in (qs, ks):
                for lo in (32, 64, 96):
                    pool.memset(tile[lo:lo + 32, :, :, :, :], 0.0).then_inc(rows_set, 1)
            pool.wait_ge(rows_set, 6)
            if cross:
                pool.memset(vals[:], 0.0).then_inc(rows_set, 1)
                pool.wait_ge(rows_set, 7)
                pool.memset(vals[:, :, :, :, DH:DH + 1], 1.0).then_inc(rows_set, 1)

            def split_max(n, r, b):
                i = 2 * n + b
                whole, parts = negmax[:, r, b, :], [mpart[:, b, H * k:H * k + H] for k in range(3)]
                wait(pool, mT_psum, i - 1)
                wait_alone(pool, passed["pool"], max_done, 4 * i + 4)
                pool.tensor_scalar(parts[0], whole, 1.0, 0.0, ALU.mult, ALU.add).then_inc(pool_msplit, 1)
                wait(pool, mpart_ready, i)
                pool.wait_ge(pool_msplit, 3 * i + 1)
                pool.tensor_tensor(mrest[:], whole, parts[0], ALU.subtract).then_inc(pool_msplit, 1)
                wait_alone(pool, passed["pool"], pool_msplit, 3 * i + 2)
                pool.tensor_scalar(parts[1], mrest[:], 1.0, 0.0, ALU.mult, ALU.add).then_inc(pool_msplit, 1)
                pool.wait_ge(pool_msplit, 3 * i + 3)
                pool.tensor_tensor(parts[2], mrest[:], parts[1], ALU.subtract).then_inc(mpart_ready, 1)

            def step(t, p, has):
                q = 1 - p
                if has(t - 3):
                    split_max(t - 3, q, 1)
                n = t - 1
                if has(n):
                    flat = lambda tile: tile.rearrange("p a t -> p (a t)")
                    pool.wait_ge(part1, n + 1)
                    wait(pool, part3, n)
                    pool.tensor_tensor(rest[:], flat(qk[:, q, :, :]), flat(part[:, q, 0, :, :]), ALU.subtract).then_inc(pool_split, 1)
                    wait_alone(pool, passed["pool"], pool_split, 2 * n + 1)
                    pool.tensor_scalar(flat(part[:, q, 1, :, :]), rest[:], 1.0, 0.0, ALU.mult, ALU.add).then_inc(pool_split, 1)
                    pool.wait_ge(pool_split, 2 * n + 2)
                    pool.tensor_tensor(flat(part[:, q, 2, :, :]), rest[:], flat(part[:, q, 1, :, :]), ALU.subtract).then_inc(part3, 1)
                if kind == "cross0" and has(n):
                    flat = lambda tile: tile.rearrange("p b k -> p (b k)")
                    pool.wait_ge(mask_p1, n + 1)
                    wait(pool, mask_p3, n)
                    pool.tensor_tensor(mask_rest[:], flat(mraw[:, q, :, :]), flat(mask_a[:, q, 0, :, :]), ALU.subtract).then_inc(pool_mask, 1)
                    wait_alone(pool, passed["pool"], pool_mask, 2 * n + 1)
                    pool.tensor_scalar(flat(mask_a[:, q, 1, :, :]), mask_rest[:], 1.0, 0.0, ALU.mult, ALU.add).then_inc(pool_mask, 1)
                    pool.wait_ge(pool_mask, 2 * n + 2)
                    pool.tensor_tensor(flat(mask_a[:, q, 2, :, :]), mask_rest[:], flat(mask_a[:, q, 1, :, :]), ALU.subtract).then_inc(mask_p3, 1)
                if kind in ("self", "cross1") and has(t):
                    wait_alone(pool, passed["pool"], ln_done, 2 * (t + 1))
                    bias = v["L0_attn_bf" if own else "L1_xattn_bv"][:].unsqueeze(1).to_broadcast([P, 2, D])
                    xs = v["x"][:, bass.ds(t * 2, 2), :]
                    if own:
                        placed = xn[:, p, :, :].rearrange("p b (d h) -> p b h d", h=H)
                        heads = xs.rearrange("p b (h d) -> p b h d", h=H)
                        pool.tensor_tensor(heads, heads, placed, ALU.add).then_inc(x_mid, 1)
                        wait_alone(pool, passed["pool"], x_mid, t + 1)
                    pool.tensor_tensor(xs, xs, bias, ALU.add).then_inc(x_pre, 1)
                if has(t - 2):
                    split_max(t - 2, p, 0)
            run_steps(pool, step, 4, 6)

        @block.scalar
        def _(act):
            ln_scale_act(act, v, ln)

            def copy_turned_max(n, r, b):
                act.wait_ge(mT_psum, 2 * n + b + 1)
                wait(act, m_rows[b][r], of_parity(n - 2, r, 16))
                act.copy(mT[:, r, b, :], turnb[0:3 * H, b * S:(b + 1) * S]).then_inc(mT_ready, 1)

            def copy_out(n, b):
                act.wait_ge(pv_done, 8 * n + 4 * b + 4)
                wait(act, nat_ready, 2 * n + b - 1)
                act.copy(oS[:, b, :], outb[:]).then_inc(o_copied, 1)

            def copy_onT(n, b):
                act.wait_ge(onT_psum, 2 * n + b + 1)
                wait(act, y_ready, n)
                act.copy(onT[:, b, :], endb[:, 0:S]).then_inc(onT_ready, 1)

            def copy_mask(k, p, half):
                act.wait_ge(mask_turned, 2 * k + half + 1)
                if half == 0:
                    wait(act, b_ready, 8 * (k - 1))
                    act.copy(mask_b[:, p, 0:2, :, :].rearrange("p c b k -> p (c b k)"), turnb[:]).then_inc(mask_copied, 1)
                else:
                    act.copy(mask_b[:, p, 2, :, :].rearrange("p b k -> p (b k)"), turnb[:, 0:W2]).then_inc(mask_copied, 1)

            def step(t, p, has):
                q = 1 - p
                n, k, m = t - 1, t - 2, t - 3
                for u in range(8):
                    e, j = lagged(t, u, 1)
                    if has(e):
                        act.wait_ge(b_ready, 8 * e + j + 1)
                        wait(act, pv_done, 8 * e + j - 3)
                        act.activation(expT[:, j % 4, :], scoreB[j % 2][:], ACT.Exp).then_inc(exp_done, 1)
                    if u == 0 and has(n):
                        act.wait_ge(qk_psum, n + 1)
                        wait(act, part3, n - 1)
                        if own:
                            act.copy(qk[:, q, 0, :], hT[:, q, 0, :])
                            act.activation(qk[:, q, 1, :], projb[:, W2:2 * W2], ACT.Identity,
                                           bias=v["L0_attn_bk"][:, 0:1]).then_inc(qk_ready, 1)
                        elif kind == "cross0":
                            act.copy(qk[:, q, :, :].rearrange("p a t -> p (a t)"), projb[:]).then_inc(qk_ready, 1)
                        else:
                            act.activation(qk[:, q, 0, :], projb[:, 0:W2], ACT.Identity, bias=v["L1_xattn_bq"][:, 0:1])
                            act.activation(qk[:, q, 1, :], projb[:, W2:2 * W2], ACT.Identity,
                                           bias=v["L1_xattn_bk"][:, 0:1]).then_inc(qk_ready, 1)
                        act.wait_ge(qk_ready, n + 1)
                        wait(act, scr_written, 16 * (n - 1))
                        act.copy(part[:, q, 0, :, :].rearrange("p a t -> p (a t)"),
                                 qk[:, q, :, :].rearrange("p a t -> p (a t)")).then_inc(part1, 1)
                        if kind == "cross0":
                            act.wait_ge(mask_loaded[q], of_parity(n, q, 16))
                            wait(act, a_ready, 8 * (n - 1))
                            wait(act, mask_turned, 2 * (n - 1))
                            act.copy(mask_a[:, q, 0, :, :], mraw[:, q, :, :]).then_inc(mask_p1, 1)
                    if u == 1:
                        if kind == "cross0" and has(k):
                            copy_mask(k, p, 0)
                        if has(m):
                            copy_turned_max(m, q, 1)
                        if cross and has(t - 4):
                            copy_out(t - 4, 1)
                    if kind == "cross0" and u == 2 and has(k):
                        copy_mask(k, p, 1)
                    if own and u in (2, 3) and has(k):
                        b = u - 2
                        act.wait_ge(v_psum, 2 * k + b + 1)
                        act.copy(vals[:, p, b, :, :].rearrange("p h w -> p (h w)"), projb[:]).then_inc(v_ready, 1)
                    if cross and u == 2 and has(k):
                        act.wait_ge(v_psum, k + 1)
                        act.copy(vals[:, p, :, :, 0:DH], projb[:, 0:W2].rearrange("p (b h w) -> p b h w", b=2, h=H)).then_inc(v_ready, 1)
                    if kind == "cross0" and u == 3 and has(t - 4):
                        copy_onT(t - 4, 1)
                    if u == 4 and has(t):
                        act.wait_ge(xT_ready, t + 1)
                        wait(act, v_psum, NV * (t - 1))
                        act.copy(hT[:, p, :, :].rearrange("p a t -> p (a t)"), turnb[:, 0:(W2 if own else 2 * W2)]).then_inc(hT_ready, 1)
                    if u == 5:
                        if has(k):
                            copy_turned_max(k, p, 0)
                        if cross and has(m):
                            copy_out(m, 0)
                    if kind == "cross0" and u == 7 and has(m):
                        copy_onT(m, 0)
            if cross:
                act.wait_ge(rows_set, 8)
            run_steps(act, step, 4, 6)

        @block.vector
        def _(dve):
            ln_scale_dve(dve, v, ln)

            def natural(n, b):
                o = endb[:].rearrange("p (h w) -> p h w", w=SLOT)
                i = 2 * n + b
                dve.wait_ge(nat_ready, i + 1)
                wait(dve, norm_done, i)
                if kind == "cross0":
                    wait(dve, onT_psum, i - 1)
                else:
                    wait(dve, upd, UPDATES * n)
                dve.reciprocal(recip[:, 0:H], o[:, :, DH]).then_inc(recip_done, 1)
                dve.wait_ge(recip_done, i + 1)
                dve.tensor_tensor(on[:, b, :].rearrange("p (h w) -> p h w", h=H), o[:, :, 0:DH],
                                  recip[:, 0:H].unsqueeze(2).to_broadcast([P, H, DH]), ALU.mult).then_inc(norm_done, 1)

            def normalise(n, b, half):
                i = 4 * n + 2 * b + half
                cols = slice(half * W2, (half + 1) * W2)
                dve.wait_ge(pv_done, 2 * i + 2)
                wait(dve, norm_done, i - 1)
                dve.reciprocal(recip[:, cols], unit_pair[half][:, W2:2 * W2]).then_inc(recip_done, 1)
                dve.wait_ge(recip_done, i + 1)
                dve.tensor_tensor(v["o_all"][:, bass.ds(n, 1), 2 * half:2 * half + 2, b * S:(b + 1) * S],
                                  unit_pair[half][:, 0:W2].rearrange("p (o j t) -> p o j t", o=1, j=2),
                                  recip[:, cols].rearrange("p (o j t) -> p o j t", o=1, j=2),
                                  ALU.mult).then_inc(norm_done, 1)

            def step(t, p, has):
                k = t - 2
                for u in range(8):
                    if has(k):
                        b, g = u // 4, u % 4
                        dve.wait_ge(a_ready, 8 * k + u + 1)
                        if g == 0:
                            wait(dve, mpart_ready, 2 * k + b - 3)
                        dve.tensor_reduce(negmax[:, p, b, G * g:G * g + G],
                                          scoreA[u % 2][:].rearrange("p (h k) -> p h k", h=G),
                                          AX.X, ALU.max, negate=True).then_inc(max_done, 1)
                    if own and u % 2:
                        n, j = lagged(t, u, 2)
                        if has(n):
                            normalise(n, j // 4, j % 4 // 2)
                    if cross and u == 2 and has(t - 4):
                        natural(t - 4, 1)
                    if u == (2 if own else 1) and has(t):
                        wait(dve, xT_ready, t - 1)
                        if own:
                            wait(dve, x_mid, t - 1)
                        for b in range(2):
                            apply_ln(dve, v, xn[:, p, b:b + 1, :], t * 2 + b, ln_done, by_place=own)
                    n = t - 4
                    if cross and has(n) and u == (5 if kind == "cross0" else 3):
                        if kind == "cross0":
                            dve.wait_ge(y_ready, n + 1)
                            add = endb[:, S:S + W2].rearrange("p (b d) -> p b d", b=2)
                        else:
                            dve.wait_ge(norm_done, 2 * n + 2)
                            dve.wait_ge(x_pre, n + 1)
                            add = on[:]
                        update_x(dve, v, n, add, passed["dve"], upd)
                    if cross and u == 6 and has(t - 3):
                        natural(t - 3, 0)
            run_steps(dve, step, 4, 6)

        @block.tensor
        def _(pe):
            pe.wait_ge(ones_rows, 16 * (8 if kind == "cross1" else 4))
            ident, identb = v["ident"], v["ident_bf"]

            def mask_product(out, r, b, turned):
                if kind == "self":
                    m = v["causal_t" if turned else "causal"][:].unsqueeze(1).to_broadcast([P, G, S])
                    pe.matmul(out[:].rearrange("p (h k) -> p h k", h=G), identb[:], m, start=True, stop=False)
                elif kind == "cross0":
                    for k in range(3):
                        m = (mask_b if turned else mask_a)[:, r, k, b:b + 1, :].to_broadcast([P, G, S])
                        pe.matmul(out[:].rearrange("p (h k) -> p h k", h=G), identb[:], m, start=(k == 0), stop=False)

            def scores(out, stationary, moving, rows, r, j, ready):
                b, g = j // 4, j % 4
                for i in range(G):
                    h = G * g + i
                    mm = pe.matmul(out[:, i * S:(i + 1) * S], stationary[0:rows, r, b, h, :], moving[0:rows, r, b, h, :],
                                   start=(kind == "cross1"), stop=(kind == "cross1" or i == G - 1))
                mm.then_inc(ready, 1)

            def score_a(n, r, j):
                if j % 4 == 0:
                    pe.wait_ge(stacked[j // 4][r], of_parity(n, r, STACKED))
                    if kind == "cross0":
                        pe.wait_ge(mask_p3, n + 1)
                wait(pe, max_done, 8 * n + j - 1)
                mask_product(scoreA[j % 2], r, j // 4, False)
                scores(scoreA[j % 2], qs, ks, MAIN, r, j, a_ready)

            def score_b(n, r, j):
                if j % 4 == 0:
                    pe.wait_ge(m_rows[j // 4][r], of_parity(n, r, 16))
                    if kind == "cross0":
                        pe.wait_ge(mask_copied, 2 * n + 2)
                wait(pe, exp_done, 8 * n + j - 1)
                mask_product(scoreB[j % 2], r, j // 4, True)
                scores(scoreB[j % 2], ks, qs, P, r, j, b_ready)

            def weigh(n, r, j):
                b, g = j // 4, j % 4
                if j == 0:
                    pe.wait_ge(v_ready, NV * (n + 1))
                pe.wait_ge(exp_done, 8 * n + j + 1)
                if own and g % 2 == 0:
                    wait(pe, norm_done, 4 * n + j // 2 - 1)
                if cross and g == 0:
                    wait(pe, o_copied, 2 * n + b)
                out, at = (unit_pair[g // 2], g % 2 * S) if own else (outb, g * S)
                for i in range(G):
                    mm = pe.matmul(out[SLOT * i:SLOT * i + SLOT, at:at + S], vals[:, r, b, G * g + i, :],
                                   expT[:, g, i * S:(i + 1) * S], start=True, stop=True)
                if own:
                    for i in range(G):
                        mm = pe.matmul(out[SLOT * i:SLOT * i + SLOT, W2 + at:W2 + at + S], v["ones"][:, 0:SLOT],
                                       expT[:, g, i * S:(i + 1) * S], start=True, stop=True)
                mm.then_inc(pv_done, 1)

            def turn_max(n, b):
                pe.wait_ge(mpart_ready, 2 * n + b + 1)
                pe.matmul(turnb[0:3 * H, b * S:(b + 1) * S], mpart[:, b, :], identb[:], start=True, stop=True).then_inc(mT_psum, 1)

            def turn_out(n, b):
                pe.wait_ge(o_copied, 2 * n + b + 1)
                for j in range(NG):
                    mm = pe.transpose(endb[:, j * S:(j + 1) * S], oS[:, b, j * S:(j + 1) * S], ident[:])
                mm.then_inc(nat_ready, 1)

            def turn_normed(n, b):
                pe.wait_ge(norm_done, 2 * n + b + 1)
                pe.transpose(endb[:, 0:S], on[:, b, :], ident[:]).then_inc(onT_psum, 1)

            def turn_mask(k, p, half):
                for c in ((0, 1) if half == 0 else (2,)):
                    for b in range(2):
                        at = (c % 2 * 2 + b) * S
                        mm = pe.matmul(turnb[:, at:at + S], mask_a[:, p, c, b, :], identb[:], start=True, stop=True)
                mm.then_inc(mask_turned, 1)

            def step(t, p, has):
                q = 1 - p
                n, k, m = t - 1, t - 2, t - 3
                for u in range(8):
                    if u == 0 and has(n):
                        pe.wait_ge(hT_ready, n + 1)
                        wait(pe, v_ready, NV * k)
                        if own:
                            pe.matmul(projb[:, W2:2 * W2], wk[:], hT[:, q, 0, :], start=True, stop=True).then_inc(qk_psum, 1)
                        else:
                            pe.matmul(projb[:, 0:W2], wq[:], hT[:, q, 0, :], start=True, stop=True)
                            pe.matmul(projb[:, W2:2 * W2], wk[:], hT[:, q, 1, :], start=True, stop=True).then_inc(qk_psum, 1)
                    if has(k):
                        score_a(k, p, u)
                    e, j = lagged(t, u, 2)
                    if has(e):
                        weigh(e, q if u >= 2 else p, j)
                    e, j = lagged(t, u, 1)
                    if has(e):
                        score_b(e, q if u >= 1 else p, j)
                    if u == 0 and kind == "cross0" and has(k):
                        if has(m):
                            pe.wait_ge(mT_ready, 2 * m + 1)
                        pe.wait_ge(mask_p3, k + 1)
                        turn_mask(k, p, 0)
                    if u == 1 and has(m):
                        pe.wait_ge(mT_ready, 2 * m + 1)
                        if kind == "cross0" and has(k):
                            pe.wait_ge(mask_copied, 2 * k + 1)
                        turn_max(m, 1)
                    if u == 2 and has(k):
                        if kind == "cross0":
                            pe.wait_ge(mask_copied, 2 * k + 1)
                            if has(m):
                                pe.wait_ge(mT_ready, 2 * m + 2)
                            turn_mask(k, p, 1)
                    if u in ((2, 3) if own else (2,)) and has(k):
                        b = u - 2
                        if b:
                            pe.wait_ge(v_ready, 2 * k + 1)
                        elif has(n):
                            pe.wait_ge(qk_ready, n + 1)
                        else:
                            pe.wait_ge(v_ready, NV * k)
                        if own:
                            pe.matmul(projb[:], hT[:, p, 0, b * S:(b + 1) * S], wv[:], start=True, stop=True).then_inc(v_psum, 1)
                        else:
                            for b in range(2):
                                mm = pe.matmul(projb[:, b * S:(b + 1) * S], hT[:, p, 1, b * S:(b + 1) * S], wv[:], start=True, stop=True)
                            mm.then_inc(v_psum, 1)
                    if u == 4 and has(t):
                        pe.wait_ge(ln_done, 2 * (t + 1))
                        if cross:
                            pe.wait_ge(ctx_loaded[p], of_parity(t, p, 16))
                        if has(m):
                            pe.wait_ge(mT_ready, 2 * m + 2)
                        else:
                            wait(pe, hT_ready, t)
                        if kind == "cross0" and has(k):
                            pe.wait_ge(mask_copied, 2 * k + 2)
                        for b in range(2):
                            mm = pe.transpose(turnb[:, b * S:(b + 1) * S], xn[:, p, b, :], ident[:])
                        if cross:
                            for b in range(2):
                                mm = pe.transpose(turnb[:, W2 + b * S:W2 + (b + 1) * S], ctx[:, p, b, :], ident[:])
                        mm.then_inc(xT_ready, 1)
                    if u == 5 and has(k):
                        if has(t):
                            pe.wait_ge(hT_ready, t + 1)
                        elif has(m):
                            pe.wait_ge(mT_ready, 2 * m + 2)
                        if kind == "cross0":
                            pe.wait_ge(mask_copied, 2 * k + 2)
                        turn_max(k, 0)
                    if cross and has(t - 4):
                        e = t - 4
                        if u == 2:
                            pe.wait_ge(onT_ready if kind == "cross0" else norm_done, 2 * e + 1)
                            turn_out(e, 1)
                        if u == 3 and kind == "cross0":
                            turn_normed(e, 1)
                        if u == 4 and kind == "cross0":
                            pe.wait_ge(onT_ready, 2 * e + 2)
                            for b in range(2):
                                mm = pe.matmul(endb[:, S + b * S:2 * S + b * S], onT[:, b, :], v["L0_xattn_wo"][:], start=True, stop=True)
                            mm.then_inc(y_ready, 1)
                    if cross and has(m):
                        if u == 6:
                            if kind == "cross0":
                                wait(pe, upd, UPDATES * (m - 1) + 1)
                            else:
                                wait(pe, norm_done, 2 * m)
                            turn_out(m, 0)
                        if u == 7 and kind == "cross0":
                            turn_normed(m, 0)
            run_steps(pe, step, 4, 6)


def gelu_projection(nc, a, v):
    with ExitStack() as c:
        sem = c.enter_context(phase_semaphores(nc, "wf_"))
        passed = {eng: sem("passed_" + eng) for eng in ("dve", "pool", "sp")}
        sb = lambda name, shape, dt=F32: c.enter_context(nc.sbuf_tensor("wf_" + name, shape, dt))
        g = sb("g", [P, 2, NJ, W2])
        stats = sb("stats", [P, 2, 6])
        v = dict(v, stats=stats)
        yb = [c.enter_context(nc.psum_tensor(f"wf_y{i}", [P, 512], F32)) for i in range(2)]
        g_ready, y_ready, upd = sem("g_ready"), sem("y_ready"), sem("upd")
        block = c.enter_context(nc.Block())

        @block.scalar
        def _(act):
            def step(t, p, has):
                if has(t):
                    wait(act, y_ready, t - 1)
                    for j in range(NJ):
                        act.activation(g[:, p, j:j + 1, :], v["o_all"][:, bass.ds(t, 1), j, :], ACT.Gelu,
                                       bias=v["L0_attn_bv"][:, j:j + 1]).then_inc(g_ready, 1)
            run_steps(act, step, 0)

        @block.tensor
        def _(pe):
            def step(t, p, has):
                if has(t):
                    wait(pe, upd, UPDATES * (t - 1))
                    pe.wait_ge(g_ready, NJ * (t + 1))
                    for b in range(2):
                        for j in range(NJ):
                            mm = pe.matmul(yb[p][:, b * D:(b + 1) * D], g[:, p, j, b * S:(b + 1) * S],
                                           v["L0_attn_Wf"][:, j, :], start=(j == 0), stop=(j == NJ - 1))
                    mm.then_inc(y_ready, 1)
            run_steps(pe, step, 0)

        @block.vector
        def _(dve):
            def step(t, p, has):
                if has(t):
                    dve.wait_ge(y_ready, t + 1)
                    update_x(dve, v, t, yb[p][:, 0:W2].rearrange("p (b d) -> p b d", b=2), passed["dve"], upd)
            run_steps(dve, step, 0)


def butterfly(eng, tile, tmp, w, rows, loaded, chain, down):
    for k in range(9):
        st = 8 - k if down else k
        s = 2 ** st
        src = tile[0:rows, k % 2, :].rearrange("p (n two s) -> p n two s", two=2, s=s)
        dst = tile[0:rows, (k + 1) % 2, :].rearrange("p (n two s) -> p n two s", two=2, s=s)
        ws = w[0:rows, k % 2, :].rearrange("p (n s f) -> p n s f", s=s, f=4)
        eng.wait_ge(loaded[k % 2], 16 * (k // 2 + 1))
        for o in range(2):
            first, second = (o, 2 + o) if down else (2 * o, 2 * o + 1)
            if k:
                eng.wait_ge(chain, 6 * k)
            shape = lambda t: t.rearrange("p (n s) -> p n s", s=s)
            eng.tensor_tensor(shape(tmp[0:rows, 2 * o, :]), src[:, :, 0, :], ws[:, :, :, first], ALU.mult).then_inc(chain, 1)
            eng.tensor_tensor(shape(tmp[0:rows, 2 * o + 1, :]), src[:, :, 1, :], ws[:, :, :, second], ALU.mult).then_inc(chain, 1)
        for o in range(2):
            eng.wait_ge(chain, 6 * k + 2 * o + 2)
            eng.tensor_tensor(dst[:, :, o, :], shape(tmp[0:rows, 2 * o, :]), shape(tmp[0:rows, 2 * o + 1, :]), ALU.add).then_inc(chain, 1)
    eng.wait_ge(chain, 54)


def weights_phase(nc, a, v):
    with ExitStack() as c:
        sem = c.enter_context(phase_semaphores(nc, "bf_"))
        passed = {eng: sem("passed_" + eng) for eng in ("dve", "pool", "sp")}
        sb = lambda name, shape, dt=F32: c.enter_context(nc.sbuf_tensor("bf_" + name, shape, dt))
        up, down, row = sb("up", [P, 2, FH]), sb("down", [P, 2, FH]), sb("row", [1, 2, FH])
        w_up, w_down = sb("w_up", [P, 2, 2 * FH]), sb("w_down", [P, 2, 2 * FH])
        w_row = sb("w_row", [1, 2, 2 * FH])
        tmp, tmp_row = sb("tmp", [P, 4, FH // 2]), sb("tmp_row", [1, 4, FH // 2])
        bank = c.enter_context(nc.psum_tensor("bf_bank", [P, 512], F32))
        bias_bank = c.enter_context(nc.psum_tensor("bf_bias", [P, 512], F32))
        up_loaded, down_loaded, row_loaded = [[sem(f"{n}_loaded{i}") for i in range(2)] for n in ("up", "down", "row")]
        up_chain, down_chain, row_chain = sem("up_chain"), sem("down_chain"), sem("row_chain")
        begun, b_loaded, turned, copied = sem("begun"), sem("b_loaded"), sem("turned"), sem("copied")
        con_loaded, rotary_loaded, late_loaded = sem("con_loaded"), sem("rotary_loaded"), sem("late_loaded")
        queries = ["L1_attn_bq", "L1_attn_bq_swapped", "wqT", "wqT_swapped"]
        others = ["L1_attn_bk", "L1_attn_bk_swapped", "L1_attn_bv", "wkT", "wkT_swapped", "wvT", "woT"]
        block = c.enter_context(nc.Block())

        def stage(name, st, rows):
            return a[name][st:st + 1].rearrange("o k i j -> o (k i j)").to_broadcast([rows, 2 * FH])

        @block.sync
        def _(sp):
            sp.dma_start(row[:, 0, :], a["L0_ffn_b_exp"].rearrange("(o d) -> o d", o=1)).then_inc(b_loaded, 16)
            for k in range(9):
                if k >= 2:
                    sp.wait_ge(up_chain, 6 * (k - 1))
                sp.dma_start(w_up[:, k % 2, :], stage("L0_ffn_up_weights", k, P)).then_inc(up_loaded[k % 2], 16)
                if k >= 2:
                    sp.wait_ge(row_chain, 6 * (k - 1))
                sp.dma_start(w_row[:, k % 2, :], stage("L0_ffn_up_weights", k, 1)).then_inc(row_loaded[k % 2], 16)
            for name in queries:
                sp.dma_start(v[name][:], a[name]).then_inc(rotary_loaded, 16)
            for name in others:
                sp.dma_start(v[name][:], a[name]).then_inc(late_loaded, 16)
            sp.dma_start(v["L1_ffn_ew1"][:], a["L1_ffn_ew1"].rearrange("e d h -> d e h")).then_inc(late_loaded, 16)
            sp.dma_start(v["L1_ffn_ew2"][:], a["L1_ffn_ew2"].rearrange("e h d -> h e d")).then_inc(late_loaded, 16)
            sp.wait_ge(late_loaded, 16 * (len(others) + 2))

        @block.scalar
        def _(act):
            def load_down(k):
                if k >= 2:
                    act.wait_ge(down_chain, 6 * (k - 1))
                act.dma_start(w_down[:, k % 2, :], stage("L0_ffn_down_weights", 8 - k, P)).then_inc(down_loaded[k % 2], 16)
            act.dma_start(down[:, 0, :], a["con_t"]).then_inc(con_loaded, 16)
            load_down(0)
            load_down(1)
            for k in range(2, 9):
                load_down(k)
            act.wait_ge(rotary_loaded, 16 * len(queries))
            for name in queries:
                act.activation(v[name][:], v[name][:], ACT.Copy, scale=HD1 ** -0.5)
            act.wait_ge(turned, 1)
            act.copy(v["up_bias_row"][:], bias_bank[:, 0:NJ]).then_inc(copied, 1)
            act.wait_ge(turned, 2)
            act.copy(v["W_down"][:], bank[:].rearrange("p (j d) -> p j d", j=NJ)).then_inc(copied, 1)

        @block.vector
        def _(dve):
            dve.tensor_copy(up[:, 0, :], v["L0_ffn_W_exp"][:]).then_inc(begun, 1)
            dve.wait_ge(begun, 1)
            butterfly(dve, up, tmp, w_up, P, up_loaded, up_chain, False)
            dve.tensor_copy(v["W_up"][:], up[:, 1, :])
            dve.wait_ge(con_loaded, 16)
            butterfly(dve, down, tmp, w_down, P, down_loaded, down_chain, True)
            dve.wait_ge(copied, 1)
            dve.tensor_tensor(v["up_bias"][:], v["up_bias_row"][:], v["L0_ffn_up_bias"][:], ALU.add)

        @block.gpsimd
        def _(pool):
            pool.wait_ge(b_loaded, 16)
            butterfly(pool, row, tmp_row, w_row, 1, row_loaded, row_chain, False)

        @block.tensor
        def _(pe):
            pe.wait_ge(row_chain, 54)
            for j in range(NJ):
                mm = pe.matmul(bias_bank[:, j:j + 1], row[:, 1, j * P:(j + 1) * P], v["ones"][0:1, 0:1], start=True, stop=True)
            mm.then_inc(turned, 1)
            pe.wait_ge(down_chain, 54)
            for j in range(NJ):
                mm = pe.transpose(bank[:, j * P:(j + 1) * P], down[:, 1, j * P:(j + 1) * P], v["ident"][:])
            mm.then_inc(turned, 1)


def ffn_phase(nc, a, v):
    with ExitStack() as c:
        sem = c.enter_context(phase_semaphores(nc, "ffn_"))
        passed = {eng: sem("passed_" + eng) for eng in ("dve", "pool", "sp")}
        sb = lambda name, shape, dt=F32: c.enter_context(nc.sbuf_tensor("ffn_" + name, shape, dt))
        bank = lambda name: c.enter_context(nc.psum_tensor("ffn_" + name, [P, 512], F32))
        xn, hT, g = sb("xn", [P, 2, 2, D]), sb("hT", [P, 2, W2]), sb("g", [P, 2, NJ, W2])
        v = dict(v, stats=sb("stats", [P, 2, 6]))
        turnb, hidb, yb = [bank("turn0"), bank("turn1")], [bank("hid0"), bank("hid1")], [bank("y0"), bank("y1")]
        ln = {k: sem(k) for k in ["var_ready", "root_ready", "chain"]}
        ln_done, x_pre, xT_ready, hT_ready = sem("ln_done"), sem("x_pre"), sem("xT_ready"), sem("hT_ready")
        hid_ready, g_ready, y_ready, upd = sem("hid_ready"), sem("g_ready"), sem("y_ready"), sem("upd")
        block = c.enter_context(nc.Block())

        @block.gpsimd
        def _(pool):
            def step(t, p, has):
                if has(t):
                    wait_alone(pool, passed["pool"], ln_done, 2 * (t + 1))
                    xs = v["x"][:, bass.ds(t * 2, 2), :]
                    pool.tensor_tensor(xs, xs, v["ffn_bias"][:].unsqueeze(1).to_broadcast([P, 2, D]),
                                       ALU.add).then_inc(x_pre, 1)
            run_steps(pool, step, 0)

        @block.scalar
        def _(act):
            ln_scale_act(act, v, ln)

            def step(t, p, has):
                q = 1 - p
                if has(t):
                    act.wait_ge(xT_ready, t + 1)
                    wait(act, hid_ready, 2 * (t - 1))
                    act.copy(hT[:, p, :], turnb[p][:, 0:W2]).then_inc(hT_ready, 1)
                n = t - 1
                if has(n):
                    wait(act, y_ready, n - 1)
                    for j in range(NJ):
                        act.wait_ge(hid_ready, 2 * n + j // 2 + 1)
                        act.activation(g[:, q, j, :], hidb[j // 2][:, (j % 2) * W2:(j % 2 + 1) * W2], ACT.Gelu,
                                       bias=v["up_bias"][:, j:j + 1]).then_inc(g_ready, 1)
            run_steps(act, step, 2)

        @block.vector
        def _(dve):
            ln_scale_dve(dve, v, ln)

            def step(t, p, has):
                if has(t):
                    wait(dve, xT_ready, t - 1)
                    for b in range(2):
                        apply_ln(dve, v, xn[:, p, b:b + 1, :], t * 2 + b, ln_done)
                n = t - 2
                if has(n):
                    dve.wait_ge(y_ready, n + 1)
                    dve.wait_ge(x_pre, n + 1)
                    update_x(dve, v, n, yb[p][:, 0:W2].rearrange("p (b d) -> p b d", b=2), passed["dve"], upd)
            run_steps(dve, step, 2)

        @block.tensor
        def _(pe):
            def step(t, p, has):
                q = 1 - p
                if has(t):
                    pe.wait_ge(ln_done, 2 * (t + 1))
                    wait(pe, hT_ready, t - 1)
                    for b in range(2):
                        mm = pe.transpose(turnb[p][:, b * S:(b + 1) * S], xn[:, p, b, :], v["ident"][:])
                    mm.then_inc(xT_ready, 1)
                n = t - 2
                if has(n):
                    pe.wait_ge(g_ready, NJ * (n + 1))
                    wait(pe, upd, UPDATES * (n - 1))
                    for b in range(2):
                        for j in range(NJ):
                            mm = pe.matmul(yb[p][:, b * D:(b + 1) * D], g[:, p, j, b * S:(b + 1) * S],
                                           v["W_down"][:, j, :], start=(j == 0), stop=(j == NJ - 1))
                    mm.then_inc(y_ready, 1)
                n = t - 1
                if has(n):
                    pe.wait_ge(hT_ready, n + 1)
                    for j in range(NJ):
                        if j % 2 == 0:
                            wait(pe, g_ready, NJ * (n - 1) + j + 2)
                        mm = pe.matmul(hidb[j // 2][:, (j % 2) * W2:(j % 2 + 1) * W2], v["W_up"][:, j * P:(j + 1) * P],
                                       hT[:, q, :], start=True, stop=True)
                        if j % 2:
                            mm.then_inc(hid_ready, 1)
            run_steps(pe, step, 2)


def rotary_attention(nc, a, v):
    with ExitStack() as c:
        sem = c.enter_context(phase_semaphores(nc, "rot_"))
        passed = {eng: sem("passed_" + eng) for eng in ("dve", "pool", "sp")}
        sb = lambda name, shape, dt=F32: c.enter_context(nc.sbuf_tensor("rot_" + name, shape, dt))
        bank = lambda name: c.enter_context(nc.psum_tensor("rot_" + name, [P, 512], F32))
        xn, hT = sb("xn", [P, 2, 2, D]), sb("hT", [P, 2, W2])
        qT = sb("qT", [P, 2, J1, W2])
        kz = sb("kz", [P, 2, J1, 2, 2, S])
        cosp, sinp = sb("cosp", [P, 2, 2, W2]), sb("sinp", [P, 2, 2, W2])
        vals = sb("vals", [P, 2, 2, H * HD1])
        negmax, sums, inv = sb("negmax", [P, 4, G]), sb("sums", [P, 4, G]), sb("inv", [P, 4, G])
        probs, pT = sb("probs", [P, 4, G * S]), sb("pT", [P, 2, G * S])
        oT = sb("oT", [P, 2, J1, S])
        stats = sb("stats", [P, 6])
        qb, kb = bank("q"), bank("k")
        scoreb, turnb = [bank("score0"), bank("score1")], [bank("turn0"), bank("turn1")]
        outb, mixb = bank("out"), bank("mix")
        ln = {k: sem(k) for k in ["var_ready", "root_ready", "chain"]}
        kz_zero, ln_done, x_pre, xT_ready, hT_ready = (sem("kz_zero"), sem("ln_done"), sem("x_pre"),
                                                       sem("xT_ready"), sem("hT_ready"))
        projected, mixed, q_rotated, k_rotated = sem("projected"), sem("mixed"), sem("q_rotated"), sem("k_rotated")
        v_psum, v_ready, a_ready, max_done, exp_done = (sem("v_psum"), sem("v_ready"), sem("a_ready"),
                                                        sem("max_done"), sem("exp_done"))
        inv_done, normed, turned, pT_ready, pv_done, o_ready, y_ready, upd = (
            sem("inv_done"), sem("normed"), sem("turned"), sem("pT_ready"), sem("pv_done"), sem("o_ready"),
            sem("y_ready"), sem("upd"))
        block = c.enter_context(nc.Block())

        def unit(t, k, lag):
            return (t - 2, k - lag) if k >= lag else (t - 3, k - lag + 8)

        @block.gpsimd
        def _(pool):
            pool.memset(kz[:], 0.0).then_inc(kz_zero, 1)
            pool.wait_ge(kz_zero, 1)

            def step(t, p, has):
                q = 1 - p
                for k in range(8):
                    n = t - 1
                    if has(n):
                        cn = 8 * n + k
                        pool.wait_ge(mixed, 4 * cn + 4)
                        if k == 0:
                            wait(pool, a_ready, 8 * (n - 1))
                        for i in range(2):
                            r = slice(64 * i, 64 * i + 64)
                            if i == 1:
                                if k == 0:
                                    pool.wait_ge(x_pre, n + 1)
                                m, u = unit(t, k - 1, 1) if k else unit(t - 1, 7, 1)
                                if has(m):
                                    pool.wait_ge(normed, 8 * m + u + 1)
                            pool.tensor_tensor(kz[r, q, k, :, i, :], cosp[r, k % 2, 1, :].rearrange("p (b t) -> p b t", b=2),
                                               sinp[r, k % 2, 1, :].rearrange("p (b t) -> p b t", b=2),
                                               ALU.add).then_inc(k_rotated, 1)
                    m, u = unit(t, k, 1)
                    if has(m):
                        un = 8 * m + u
                        pool.wait_ge(inv_done, un + 1)
                        if has(n):
                            pool.wait_ge(k_rotated, 2 * cn + 2)
                        pr = probs[:, u % 4, :].rearrange("p (h k) -> p h k", h=G)
                        pool.tensor_tensor(pr, pr, inv[:, u % 4, :].unsqueeze(2).to_broadcast([P, G, S]),
                                           ALU.mult).then_inc(normed, 1)
                if has(t):
                    wait_alone(pool, passed["pool"], ln_done, 2 * (t + 1))
                    if has(t - 1):
                        pool.wait_ge(k_rotated, 16 * t)
                    xs = v["x"][:, bass.ds(t * 2, 2), :]
                    pool.tensor_tensor(xs, xs, v["L1_attn_bo"][:].unsqueeze(1).to_broadcast([P, 2, D]),
                                       ALU.add).then_inc(x_pre, 1)
            run_steps(pool, step, 3)

        @block.scalar
        def _(act):
            ln_scale_act(act, v, ln)

            def step(t, p, has):
                q = 1 - p
                for k in range(8):
                    m, u = unit(t, k, 2)
                    if has(m):
                        un = 8 * m + u
                        act.wait_ge(turned, un + 1)
                        wait(act, pv_done, un - 1)
                        act.copy(pT[:, u % 2, :], turnb[u % 2][:]).then_inc(pT_ready, 1)
                    n = t - 2
                    if has(n):
                        un = 8 * n + k
                        act.wait_ge(max_done, un + 1)
                        wait(act, turned, un - 3)
                        wait(act, inv_done, un - 3)
                        for i in range(G):
                            act.activation(probs[:, k % 4, i * S:(i + 1) * S], scoreb[k % 2][:, i * S:(i + 1) * S],
                                           ACT.Exp, bias=negmax[:, k % 4, i:i + 1],
                                           accum_out=sums[:, k % 4, i:i + 1]).then_inc(exp_done, 1)
                    m, u = unit(t, k, 3)
                    if has(m) and u % 2:
                        act.wait_ge(pv_done, 8 * m + u + 1)
                        b, j0 = u // 4, (u % 4 - 1) * 2
                        if u % 4 == 1:
                            wait(act, y_ready, 2 * m + b - 1)
                        for i in range(4):
                            act.activation(oT[:, b, j0 + i, :], outb[:, i * S:(i + 1) * S], ACT.Identity,
                                           bias=v["L1_attn_bv"][:, j0 + i:j0 + i + 1]).then_inc(o_ready, 1)
                    n = t - 1
                    if has(n) and k < 4:
                        i = k
                        act.wait_ge(v_psum, 4 * n + i + 1)
                        act.copy(vals[:, q, i // 2, (i % 2) * 512:(i % 2 + 1) * 512], mixb[:]).then_inc(v_ready, 1)
                    if has(t) and k == 6:
                        act.wait_ge(xT_ready, t + 1)
                        act.copy(hT[:, p, :], mixb[:, 0:W2]).then_inc(hT_ready, 1)
            run_steps(act, step, 3)

        @block.vector
        def _(dve):
            ln_scale_dve(dve, v, ln)

            def add_y(n, b):
                k = 2 * n + b
                dve.wait_ge(y_ready, k + 1)
                dve.wait_ge(x_pre, n + 1)
                wait(dve, upd, 4 * k)
                xs = v["x"][:, bass.ds(n * 2 + b, 1), :]
                dve.tensor_tensor(xs, xs, mixb[:, 0:D].unsqueeze(1), ALU.add).then_inc(upd, 1)
                wait_alone(dve, passed["dve"], upd, 4 * k + 1)
                dve.bn_stats(stats[:], xs).then_inc(upd, 1)
                wait_alone(dve, passed["dve"], upd, 4 * k + 2)
                dve.bn_aggr(v["aggr"][:, 0, :], stats[:]).then_inc(upd, 1)
                dve.wait_ge(upd, 4 * k + 3)
                dve.tensor_copy(v["moments"][:, bass.ds(n * 2 + b, 1), :], v["aggr"][:, 0:1, :]).then_inc(upd, 1)

            def step(t, p, has):
                q = 1 - p
                for k in range(8):
                    n = t - 1
                    if has(n):
                        cn = 8 * n + k
                        dve.wait_ge(projected, cn + 1)
                        wait(dve, q_rotated, cn - 1)
                        wait(dve, k_rotated, 2 * (cn - 1))
                        for s, bk, bias in ((0, qb, "L1_attn_bq"), (1, kb, "L1_attn_bk")):
                            for dst, o, name, table in ((cosp, 0, bias, "rope_cos"), (sinp, W2, bias + "_swapped", "rope_sin")):
                                dve.scalar_tensor_tensor(
                                    dst[:, k % 2, s, :].rearrange("p (b t) -> p b t", b=2),
                                    bk[:, o:o + W2].rearrange("p (b t) -> p b t", b=2), v[name][:, k:k + 1],
                                    v[table][:].unsqueeze(1).to_broadcast([P, 2, S]), ALU.add, ALU.mult).then_inc(mixed, 1)
                    n = t - 2
                    if has(n):
                        un = 8 * n + k
                        dve.wait_ge(a_ready, un + 1)
                        dve.tensor_reduce(negmax[:, k % 4, :], scoreb[k % 2][:].rearrange("p (h k) -> p h k", h=G),
                                          AX.X, ALU.max, negate=True).then_inc(max_done, 1)
                    n = t - 1
                    if has(n):
                        cn = 8 * n + k
                        if k == 0:
                            wait(dve, a_ready, 8 * (n - 1))
                        dve.wait_ge(mixed, 4 * cn + 2)
                        dve.tensor_tensor(qT[:, q, k, :], cosp[:, k % 2, 0, :], sinp[:, k % 2, 0, :],
                                          ALU.add).then_inc(q_rotated, 1)
                    m, u = unit(t, k, 1)
                    if has(m):
                        un = 8 * m + u
                        dve.wait_ge(exp_done, 4 * un + 4)
                        wait(dve, normed, un - 3)
                        dve.reciprocal(inv[:, u % 4, :], sums[:, u % 4, :]).then_inc(inv_done, 1)
                    if k == 5 and has(t - 3):
                        add_y(t - 3, 1)
                    if k == 4 and has(t):
                        wait(dve, xT_ready, t - 1)
                        for b in range(2):
                            apply_ln(dve, v, xn[:, p, b:b + 1, :], t * 2 + b, ln_done)
                    if k == 7 and has(t - 2):
                        add_y(t - 2, 0)
            run_steps(dve, step, 3)

        @block.tensor
        def _(pe):
            ident, identb = v["ident"], v["ident_bf"]
            pe.wait_ge(kz_zero, 1)

            def out_projection(n, b):
                k = 2 * n + b
                pe.wait_ge(o_ready, 8 * (k + 1))
                for j in range(J1):
                    mm = pe.matmul(mixb[:, 0:D], oT[:, b, j, :], v["woT"][:, j, :], start=(j == 0), stop=(j == J1 - 1))
                mm.then_inc(y_ready, 1)

            def step(t, p, has):
                q = 1 - p
                m = t - 3
                n = t - 1
                for k in range(8):
                    if has(n):
                        cn = 8 * n + k
                        if k == 0:
                            pe.wait_ge(hT_ready, n + 1)
                        wait(pe, mixed, 4 * cn)
                        for bk, w in ((qb, "wqT"), (kb, "wkT")):
                            pe.matmul(bk[:, 0:W2], v[w][:, k, :], hT[:, q, :], start=True, stop=True)
                            mm = pe.matmul(bk[:, W2:2 * W2], v[w + "_swapped"][:, k, :], hT[:, q, :], start=True, stop=True)
                        mm.then_inc(projected, 1)
                    if has(t - 2):
                        un = 8 * (t - 2) + k
                        b, g = k // 4, k % 4
                        if k == 0:
                            pe.wait_ge(q_rotated, 8 * (t - 1))
                            pe.wait_ge(k_rotated, 16 * (t - 1))
                        wait(pe, exp_done, 4 * (un - 1))
                        out = scoreb[k % 2]
                        pe.matmul(out[:].rearrange("p (h k) -> p h k", h=G), identb[:],
                                  v["causal"][:].unsqueeze(1).to_broadcast([P, G, S]), start=True, stop=False)
                        for i in range(2):
                            j = 2 * g + i
                            mm = pe.matmul(out[:, i * W2:(i + 1) * W2], qT[:, p, j, b * S:(b + 1) * S],
                                           kz[:, p, j, b, :, :].rearrange("p h t -> p (h t)"), start=False, stop=(i == 1))
                        mm.then_inc(a_ready, 1)
                    l, u = unit(t, k, 2)
                    if has(l):
                        un = 8 * l + u
                        pe.wait_ge(normed, un + 1)
                        wait(pe, pT_ready, un - 1)
                        for i in range(G):
                            mm = pe.transpose(turnb[u % 2][:, i * S:(i + 1) * S], probs[:, u % 4, i * S:(i + 1) * S], ident[:])
                        mm.then_inc(turned, 1)
                    l, u = unit(t, k, 3)
                    if has(l):
                        un = 8 * l + u
                        r = p if k >= 3 else q
                        b, g = u // 4, u % 4
                        pe.wait_ge(pT_ready, un + 1)
                        if u == 0:
                            pe.wait_ge(v_ready, 4 * (l + 1))
                        if u % 2 == 0:
                            wait(pe, o_ready, 2 * un)
                        for i in range(G):
                            h = G * g + i
                            col = ((u % 2) * 2 + i // 2) * S
                            mm = pe.matmul(outb[64 * (i % 2):64 * (i % 2) + 64, col:col + S],
                                           vals[:, r, b, h * HD1:(h + 1) * HD1], pT[:, u % 2, i * S:(i + 1) * S],
                                           start=True, stop=True)
                        mm.then_inc(pv_done, 1)
                    if has(n) and k < 4:
                        i = k
                        if i == 0 and has(m):
                            pe.wait_ge(upd, 4 * (2 * m + 1))
                        if i:
                            pe.wait_ge(v_ready, 4 * n + i)
                        pe.matmul(mixb[:], hT[:, q, (i // 2) * S:(i // 2 + 1) * S],
                                  v["wvT"][:, (i % 2) * 4:(i % 2) * 4 + 4, :].rearrange("p j e -> p (j e)"),
                                  start=True, stop=True).then_inc(v_psum, 1)
                    if k == 4 and has(m):
                        if has(n):
                            pe.wait_ge(v_ready, 4 * n + 4)
                        pe.wait_ge(upd, 4 * (2 * m + 1))
                        out_projection(m, 1)
                    if k == 6 and has(t):
                        if has(n):
                            pe.wait_ge(v_ready, 4 * n + 4)
                        if has(m):
                            pe.wait_ge(upd, 4 * (2 * m + 2))
                        pe.wait_ge(ln_done, 2 * (t + 1))
                        for b in range(2):
                            mm = pe.transpose(mixb[:, b * S:(b + 1) * S], xn[:, p, b, :], ident[:])
                        mm.then_inc(xT_ready, 1)
                    if k == 7 and has(t - 2):
                        if has(t):
                            pe.wait_ge(hT_ready, t + 1)
                        elif has(n):
                            pe.wait_ge(v_ready, 4 * n + 4)
                        if has(m):
                            pe.wait_ge(upd, 4 * (2 * m + 2))
                        out_projection(t - 2, 0)
            run_steps(pe, step, 3)


def router_phase(nc, a, v):
    E3 = [P, B, NE]
    with ExitStack() as c:
        sem = c.enter_context(phase_semaphores(nc, "rt_"))
        sb = lambda name, shape, dt=F32: c.enter_context(nc.sbuf_tensor("rt_" + name, shape, dt))
        bank = lambda name: c.enter_context(nc.psum_tensor("rt_" + name, [P, 512], F32))
        xn = sb("xn", [P, 2, 2, D])
        logits, score, sel = sb("logits", E3), sb("score", E3), sb("sel", E3)
        hit, key, rank, tmp = sb("hit", E3), sb("key", E3), sb("rank", E3), sb("tmp", E3)
        chosen = [sb("chosen0", E3), sb("chosen1", E3)]
        best, denom, big, inv = [sb(n, [P, B]) for n in ("best", "denom", "big", "inv")]
        turnb, logitb = [bank("turn0"), bank("turn1")], [bank("logit0"), bank("logit1")]
        ln = {k: sem(k) for k in ["var_ready", "root_ready", "chain"]}
        ln_done, xT_ready, hT_ready, logit_psum, logit_ready = (sem("ln_done"), sem("xT_ready"), sem("hT_ready"),
                                                                sem("logit_psum"), sem("logit_ready"))
        rank_ready, e_ready, g = sem("rank_ready"), sem("e_ready"), sem("gate")
        block = c.enter_context(nc.Block())

        @block.gpsimd
        def _(pool):
            for e in range(NE):
                last = pool.memset(rank[:, :, e:e + 1], float(NE - e))
                last.then_inc(rank_ready, 1)

        @block.scalar
        def _(act):
            ln_scale_act(act, v, ln)

            def step(t, p, has):
                if has(t):
                    act.wait_ge(xT_ready, t + 1)
                    act.copy(v["hT_all"][:, t, :] if isinstance(t, int) else v["hT_all"][:, bass.ds(t, 1), :],
                             turnb[p][:, 0:W2] if isinstance(t, int) else turnb[p][:, 0:W2].unsqueeze(1)).then_inc(hT_ready, 1)
                    act.copy(v["hT_two"][:, p, :], turnb[p][:, 0:W2]).then_inc(hT_ready, 1)
            run_steps(act, step, 0)
            act.wait_ge(logit_ready, NP)
            act.activation(score[:], logits[:], ACT.Exp, scale=-1.0).then_inc(e_ready, 1)

        @block.tensor
        def _(pe):
            def step(t, p, has):
                q = 1 - p
                if has(t):
                    pe.wait_ge(ln_done, 2 * (t + 1))
                    wait(pe, hT_ready, 2 * (t - 1))
                    for b in range(2):
                        mm = pe.transpose(turnb[p][:, b * S:(b + 1) * S], xn[:, p, b, :], v["ident"][:])
                    mm.then_inc(xT_ready, 1)
                n = t - 1
                if has(n):
                    pe.wait_ge(hT_ready, 2 * (n + 1))
                    wait(pe, logit_ready, n - 1)
                    for b in range(2):
                        mm = pe.matmul(logitb[q][:, b * NE:(b + 1) * NE], v["hT_two"][:, q, b * S:(b + 1) * S],
                                       v["router_t"][:], start=True, stop=True)
                    mm.then_inc(logit_psum, 1)
            run_steps(pe, step, 1)

        @block.vector
        def _(dve):
            ln_scale_dve(dve, v, ln)

            def step(t, p, has):
                q = 1 - p
                if has(t):
                    wait(dve, xT_ready, t - 1)
                    for b in range(2):
                        apply_ln(dve, v, xn[:, p, b:b + 1, :], t * 2 + b, ln_done)
                n = t - 1
                if has(n):
                    dve.wait_ge(logit_psum, n + 1)
                    dve.tensor_copy(logits[:, bass.ds(n * 2, 2), :],
                                    logitb[q][:, 0:2 * NE].rearrange("p (b e) -> p b e", b=2)).then_inc(logit_ready, 1)
            run_steps(dve, step, 1)
            dve.wait_ge(rank_ready, NE)
            dve.wait_ge(e_ready, 1)
            wide = lambda t: t[:].unsqueeze(2).to_broadcast(E3)
            dve.tensor_scalar(tmp[:], score[:], 1.0, None, ALU.add).then_inc(g, 1)
            dve.wait_ge(g, 1)
            dve.reciprocal(score[:], tmp[:]).then_inc(g, 1)
            dve.wait_ge(g, 2)
            dve.tensor_tensor(sel[:], score[:], v["L1_ffn_router_bias"][:].unsqueeze(1).to_broadcast(E3), ALU.add).then_inc(g, 1)
            n = 3
            for i in range(2):
                dve.wait_ge(g, n)
                dve.tensor_reduce(best[:], sel[:], AX.X, ALU.max).then_inc(g, 1)
                dve.wait_ge(g, n + 1)
                dve.tensor_tensor(hit[:], sel[:], wide(best), ALU.is_equal).then_inc(g, 1)
                dve.wait_ge(g, n + 2)
                dve.tensor_tensor(key[:], hit[:], rank[:], ALU.mult).then_inc(g, 1)
                dve.wait_ge(g, n + 3)
                dve.tensor_reduce(best[:], key[:], AX.X, ALU.max).then_inc(g, 1)
                dve.wait_ge(g, n + 4)
                dve.tensor_tensor(chosen[i][:], key[:], wide(best), ALU.is_equal).then_inc(g, 1)
                dve.wait_ge(g, n + 5)
                n += 5
                if i == 0:
                    dve.scalar_tensor_tensor(sel[:], chosen[0][:], MASKED, sel[:], ALU.mult, ALU.add).then_inc(g, 1)
                    n += 1
            dve.tensor_tensor(chosen[0][:], chosen[0][:], chosen[1][:], ALU.add).then_inc(g, 1)
            dve.wait_ge(g, n + 1)
            dve.tensor_tensor(tmp[:], score[:], chosen[0][:], ALU.mult).then_inc(g, 1)
            dve.wait_ge(g, n + 2)
            dve.tensor_reduce(denom[:], tmp[:], AX.X, ALU.add).then_inc(g, 1)
            dve.wait_ge(g, n + 3)
            dve.tensor_scalar(big[:], denom[:], 1e-9, None, ALU.is_gt).then_inc(g, 1)
            dve.tensor_scalar(denom[:], denom[:], 1e-9, None, ALU.add).then_inc(g, 1)
            dve.wait_ge(g, n + 5)
            dve.reciprocal(inv[:], denom[:]).then_inc(g, 1)
            dve.wait_ge(g, n + 6)
            dve.tensor_tensor(inv[:], inv[:], big[:], ALU.mult).then_inc(g, 1)
            dve.tensor_scalar(big[:], big[:], -0.5, 0.5, ALU.mult, ALU.add).then_inc(g, 1)
            dve.wait_ge(g, n + 8)
            dve.tensor_tensor(tmp[:], tmp[:], wide(inv), ALU.mult).then_inc(g, 1)
            dve.tensor_tensor(chosen[0][:], chosen[0][:], wide(big), ALU.mult).then_inc(g, 1)
            dve.wait_ge(g, n + 10)
            dve.tensor_tensor(v["gates"][:], tmp[:], chosen[0][:], ALU.add)


def experts_phase(nc, a, v):
    with ExitStack() as c:
        sem = c.enter_context(phase_semaphores(nc, "ex_"))
        passed = {eng: sem("passed_" + eng) for eng in ("dve", "pool", "sp")}
        sb = lambda name, shape, dt=F32: c.enter_context(nc.sbuf_tensor("ex_" + name, shape, dt))
        bank = lambda name: c.enter_context(nc.psum_tensor("ex_" + name, [P, 512], F32))
        th, up, act_in = sb("th", [P, 512]), sb("up", [P, 512]), sb("act_in", [P, 2, 512])
        g = sb("g", [P, 2, NE, W2])
        gateb, linb, hidb = bank("gate"), bank("lin"), [bank("hid0"), bank("hid1")]
        yb, sharedb = [bank("y0"), bank("y1")], bank("shared")
        shared_psum, tanh_done, silu_mid, act_ready = sem("shared_psum"), sem("tanh_done"), sem("silu_mid"), sem("act_ready")
        hid_psum, g_ready, y_psum, shared_y, upd, stored = (sem("hid_psum"), sem("g_ready"), sem("y_psum"),
                                                            sem("shared_y"), sem("upd"), sem("stored"))
        out = a["out"].rearrange("b t d -> t b d")
        UP = NE * 2 + 1
        block = c.enter_context(nc.Block())

        @block.sync
        def _(sp):
            def step(t, p, has):
                n = t - 1
                if has(n):
                    sp.wait_ge(upd, UP * (n + 1))
                    sp.dma_start(out[:, bass.ds(n * 2, 2), :], v["x"][:, bass.ds(n * 2, 2), :]).then_inc(stored, 16)
            run_steps(sp, step, 1)
            sp.wait_ge(stored, 16 * NP)

        @block.scalar
        def _(act):
            def step(t, p, has):
                if has(t):
                    act.wait_ge(shared_psum, t + 1)
                    wait(act, silu_mid, t)
                    act.activation(th[:], gateb[:], ACT.Tanh, scale=0.5).then_inc(tanh_done, 1)
                    wait(act, y_psum, 4 * (t - 1))
                    for i in range(NE // 2):
                        act.wait_ge(hid_psum, 4 * t + i + 1)
                        act.activation(g[:, p, 2 * i:2 * i + 2, :].rearrange("p e t -> p (e t)"), hidb[i % 2][:],
                                       ACT.Gelu).then_inc(g_ready, 1)
            run_steps(act, step, 0)

        @block.vector
        def _(dve):
            def step(t, p, has):
                q = 1 - p
                if has(t):
                    dve.wait_ge(tanh_done, t + 1)
                    wait(dve, act_ready, t)
                    dve.scalar_tensor_tensor(up[:], th[:], 1.0, gateb[:], ALU.add, ALU.mult).then_inc(silu_mid, 1)
                    dve.wait_ge(silu_mid, t + 1)
                    wait(dve, shared_y, t - 1)
                    dve.scalar_tensor_tensor(act_in[:, p, :], up[:], 0.5, linb[:], ALU.mult, ALU.mult).then_inc(act_ready, 1)
                n = t - 1
                if has(n):
                    k = UP * n
                    xs = v["x"][:, bass.ds(n * 2, 2), :]
                    dve.wait_ge(shared_y, n + 1)
                    wait(dve, upd, k)
                    dve.tensor_tensor(xs, xs, sharedb[:, 0:W2].rearrange("p (b d) -> p b d", b=2), ALU.add).then_inc(upd, 1)
                    for i in range(4):
                        dve.wait_ge(y_psum, 4 * n + i + 1)
                        for e in range(2):
                            for b in range(2):
                                if b == 0:
                                    dve.wait_ge(upd, k + 1 + 4 * i + 2 * e)
                                x1 = v["x"][:, bass.ds(n * 2 + b, 1), :]
                                gate = v["gates"][:, bass.ds(n * 2 + b, 1), 2 * i + e:2 * i + e + 1]
                                dve.scalar_tensor_tensor(
                                    x1, yb[i % 2][:, (2 * e + b) * D:(2 * e + b + 1) * D].unsqueeze(1),
                                    gate.rearrange("p a b -> p (a b)"), x1, ALU.mult, ALU.add).then_inc(upd, 1)
            run_steps(dve, step, 1)

        @block.tensor
        def _(pe):
            def step(t, p, has):
                q = 1 - p
                n = t - 1
                if has(t):
                    h = v["hT_all"][:, t, :] if isinstance(t, int) else v["hT_all"][:, bass.ds(t, 1), :].rearrange("p a t -> p (a t)")
                    wait(pe, act_ready, t)
                    for j in range(2):
                        pe.matmul(gateb[:, j * W2:(j + 1) * W2], v["L1_ffn_sw1"][:, j * P:(j + 1) * P], h, start=True, stop=True)
                    for j in range(2):
                        mm = pe.matmul(linb[:, j * W2:(j + 1) * W2], v["L1_ffn_sw3"][:, j * P:(j + 1) * P], h, start=True, stop=True)
                    mm.then_inc(shared_psum, 1)
                for i in range(4):
                    if has(t):
                        wait(pe, g_ready, 4 * t + i - 1)
                        for e in range(2):
                            mm = pe.matmul(hidb[i % 2][:, e * W2:(e + 1) * W2], v["L1_ffn_ew1"][:, 2 * i + e, :], h, start=True, stop=True)
                        mm.then_inc(hid_psum, 1)
                    if has(n):
                        if i == 0:
                            pe.wait_ge(act_ready, n + 1)
                            wait(pe, upd, UP * (n - 1) + 1)
                            for b in range(2):
                                for j in range(2):
                                    mm = pe.matmul(sharedb[:, b * D:(b + 1) * D], act_in[:, q, j * W2 + b * S:j * W2 + (b + 1) * S],
                                                   v["L1_ffn_sw2"][:, j, :], start=(j == 0), stop=(j == 1))
                            mm.then_inc(shared_y, 1)
                        pe.wait_ge(g_ready, 4 * n + i + 1)
                        wait(pe, upd, UP * n + 1 + 4 * (i - 1) if i >= 2 else UP * (n - 1) + 1 + 4 * (i + 3))
                        for e in range(2):
                            for b in range(2):
                                mm = pe.matmul(yb[i % 2][:, (2 * e + b) * D:(2 * e + b + 1) * D],
                                               g[:, q, 2 * i + e, b * S:(b + 1) * S], v["L1_ffn_ew2"][:, 2 * i + e, :],
                                               start=True, stop=True)
                        mm.then_inc(y_psum, 1)
            run_steps(pe, step, 1)


def rope_tables():
    theta = np.float32(10000.0) ** (np.arange(0, HD1, 2, dtype=np.float32) / np.float32(HD1))
    freqs = np.arange(S, dtype=np.float32)[:, None] * (np.float32(1.0) / theta)[None, :]
    emb = np.concatenate([freqs, freqs], axis=-1).astype(np.float64).T
    sign = np.where(np.arange(HD1) % 2 == 0, -1.0, 1.0)[:, None]
    return (np.tile(np.cos(emb), (2, 1)).astype(np.float32), np.tile(np.sin(emb) * sign, (2, 1)).astype(np.float32))


def laid_out(x):
    by_place = np.arange(D).reshape(H, DH).T.reshape(-1)
    partner = np.arange(H * HD1).reshape(-1, 2)[:, ::-1].reshape(-1)
    given = {name: x[name] for name in [
        "x", "ctx_1024", "mask_Bx1xSxS2_ff0", "mask_Bx1x1xS2_ff0", "L0_attn_Wf", "L0_attn_bf",
        "L0_ffn_W_exp", "L0_ffn_b_exp", "L0_ffn_up_weights", "L0_ffn_down_weights", "L0_ffn_b_con",
        "L0_ffn_down_bias", "L1_attn_bo", "L1_xattn_Wv", "L1_xattn_bv", "L1_ffn_router_bias", "L1_ffn_sw1",
        "L1_ffn_sw3", "L1_ffn_sw2", "L1_ffn_ew1", "L1_ffn_ew2"]}
    given["L0_attn_Wk"] = x["L0_attn_Wk"][by_place][:, by_place]
    given["L0_attn_Wv"] = x["L0_attn_Wv"][by_place]
    for name in ["L1_xattn_Wq", "L1_xattn_Wk"]:
        given[name] = x[name][:, by_place]
    for name in ["L0_xattn_wq", "L0_xattn_wk"]:
        given[name] = x[name].reshape(D, D)[:, by_place]
    given["L0_xattn_wv"] = x["L0_xattn_wv"].reshape(D, D)
    given["L0_xattn_wo"] = x["L0_xattn_wo"].reshape(D, D)
    for name in ["L0_attn_bk", "L1_xattn_bq", "L1_xattn_bk"]:
        given[name] = x[name][by_place].reshape(D, 1)
    for name in ["L0_attn_bv", "L0_ffn_up_bias"]:
        given[name] = x[name].reshape(NJ, P).T
    for name in ["L1_attn_bq", "L1_attn_bk", "L1_attn_bv"]:
        given[name] = x[name].reshape(J1, P).T
    for name in ["L1_attn_bq", "L1_attn_bk"]:
        given[name + "_swapped"] = x[name][partner].reshape(J1, P).T
    for name in ["wq", "wk", "wv"]:
        given[name + "T"] = x["L1_attn_" + name].T.reshape(D, J1, P)
    for name in ["wq", "wk"]:
        given[name + "T_swapped"] = x["L1_attn_" + name][partner].T.reshape(D, J1, P)
    given["woT"] = x["L1_attn_wo"].T.reshape(J1, P, D).transpose(1, 0, 2)
    given["con_t"] = x["L0_ffn_W_con"].T
    given["router_t"] = x["L1_ffn_router_w"].T
    given["rope_cos"], given["rope_sin"] = rope_tables()
    return {name: np.ascontiguousarray(value) for name, value in given.items()}


def build_program(nc, a):
    a = dict(a)
    a["part_scratch"] = nc.dram_tensor("part_scratch", [2, 3 * 2 * 2, DH, H, S], BF16, kind="Internal").ap()
    a["mask_scratch"] = nc.dram_tensor("mask_scratch", [3, B, S], BF16, kind="Internal").ap()
    with ExitStack() as c:
        v = {}

        def keep(name, shape, dt=F32):
            v[name] = c.enter_context(nc.sbuf_tensor("v_" + name, shape, dt))
        keep("x", [P, B, D])
        for name in ["vareps", "root", "rstd0", "newton", "rstd", "shift"]:
            keep(name, [P, B])
        keep("moments", [P, B, 2])
        keep("aggr", [P, 2, 2])
        keep("ident", [P, P])
        keep("ident_bf", [P, P], BF16)
        keep("causal", [P, S], BF16)
        keep("causal_t", [P, S], BF16)
        keep("ones", [P, SLOT])
        keep("ones_bf", [P, W2], BF16)
        for name in ["L0_attn_Wk", "L1_xattn_Wq", "L1_xattn_Wk", "L1_xattn_Wv", "L0_xattn_wq", "L0_xattn_wk",
                     "L0_xattn_wv", "L0_xattn_wo", "L0_attn_bf", "L1_xattn_bv", "L1_attn_bo", "L0_ffn_b_con",
                     "L0_ffn_down_bias", "ffn_bias", "rope_cos", "rope_sin"]:
            keep(name, [P, D])
        for name in ["L0_attn_Wv", "L0_ffn_W_exp", "W_up"]:
            keep(name, [P, FH])
        for name in ["L0_attn_Wf", "W_down"]:
            keep(name, [P, NJ, D])
        keep("L1_ffn_sw1", [P, SH])
        keep("L1_ffn_sw3", [P, SH])
        keep("L1_ffn_sw2", [P, SH // P, D])
        keep("router_t", [P, NE])
        keep("L1_ffn_router_bias", [P, NE])
        keep("gates", [P, B, NE])
        for name in ["L0_attn_bk", "L1_xattn_bq", "L1_xattn_bk"]:
            keep(name, [P, 1])
        for name in ["L0_attn_bv", "L0_ffn_up_bias", "up_bias", "up_bias_row"]:
            keep(name, [P, NJ])
        setup_phase(nc, a, v)
        with ExitStack() as own:
            v["o_all"] = own.enter_context(nc.sbuf_tensor("v_o_all", [P, NP, NJ, W2], F32))
            narrow_attention(nc, a, v, "self")
            gelu_projection(nc, a, v)
        narrow_attention(nc, a, v, "cross0")
        keep("L1_ffn_ew1", [P, NE, P])
        keep("L1_ffn_ew2", [P, NE, D])
        for name in ["wqT", "wkT", "wvT", "woT", "wqT_swapped", "wkT_swapped"]:
            keep(name, [P, J1, P])
        for name in ["L1_attn_bq", "L1_attn_bk", "L1_attn_bv", "L1_attn_bq_swapped", "L1_attn_bk_swapped"]:
            keep(name, [P, J1])
        weights_phase(nc, a, v)
        ffn_phase(nc, a, v)
        rotary_attention(nc, a, v)
        narrow_attention(nc, a, v, "cross1")
        v["hT_all"] = c.enter_context(nc.sbuf_tensor("v_hT_all", [P, NP, W2], F32))
        v["hT_two"] = c.enter_context(nc.sbuf_tensor("v_hT_two", [P, 2, W2], F32))
        router_phase(nc, a, v)
        experts_phase(nc, a, v)


def kernel(**inputs):
    import concourse.bacc as bacc
    from concourse.bass_utils import run_bass_kernel_spmd

    nc = bacc.Bacc("TRN2", target_bir_lowering=False, num_devices=1)
    arrays, aps = {}, {}
    for name, value in laid_out(inputs).items():
        arrays["in_" + name] = value
        aps[name] = nc.dram_tensor("in_" + name, value.shape, mybir.dt.from_np(value.dtype), kind="ExternalInput").ap()
    aps["out"] = nc.dram_tensor("out_x", [B, S, D], F32, kind="ExternalOutput").ap()
    build_program(nc, aps)
    result = run_bass_kernel_spmd(nc, [arrays], core_ids=[0])
    return result.results[0]["out_x"]
```

```python
from contextlib import ExitStack, contextmanager

import numpy as np

import concourse.bass as bass
from concourse import mybir

ALU = mybir.AluOpType
ACT = mybir.ActivationFunctionType
AX = mybir.AxisListType
F32 = mybir.dt.float32
BF16 = mybir.dt.bfloat16
F32R = mybir.dt.float32r

P = 128
B = 32
S = 128
D = 128
H = 16
DH = D // H
NP = B // 2
W2 = 2 * S
G = 4
NG = H // G
FH = 512
NJ = FH // P
HD1 = 64
J1 = H * HD1 // P
NE = 8
SH = 256
SLOT = 32
MAIN = 96
MASKED = -1e30
PEEL = 4
EPS = 1e-5


@contextmanager
def phase_semaphores(nc, prefix):
    taken = []

    def sem(name):
        taken.append(nc.alloc_semaphore(name=prefix + name))
        return taken[-1]
    yield sem
    nc.clear_and_free_semaphores(taken)
    nc.all_engine_barrier()


def wait(eng, sem, value):
    if isinstance(value, int) and value <= 0:
        return
    eng.wait_ge(sem, value)


def wait_alone(eng, passed, sem, value):
    wait(eng, sem, value)
    eng.sem_inc(passed, 1)


def of_parity(n, parity, each):
    return (n - parity) * (each // 2) + each


def run_steps(eng, step, depth, peel=PEEL):
    def exists(n):
        return 0 <= n < NP
    for t in range(peel):
        step(t, t % 2, exists)
    with eng.Fori(peel // 2, NP // 2) as i:
        step(i * 2, 0, lambda n: True)
        step(i * 2 + 1, 1, lambda n: True)
    for t in range(NP, NP + depth):
        step(t, t % 2, exists)


def ln_scale_dve(dve, v, ln):
    var = v["moments"][:, :, 1]
    dve.tensor_scalar(v["vareps"][:], var, EPS, None, ALU.add).then_inc(ln["var_ready"], 1)
    dve.wait_ge(ln["root_ready"], 1)
    dve.reciprocal(v["rstd0"][:], v["root"][:]).then_inc(ln["chain"], 1)
    dve.wait_ge(ln["chain"], 1)
    dve.tensor_tensor(v["newton"][:], v["rstd0"][:], v["rstd0"][:], ALU.mult).then_inc(ln["chain"], 1)
    dve.wait_ge(ln["chain"], 2)
    dve.tensor_tensor(v["newton"][:], v["newton"][:], v["vareps"][:], ALU.mult).then_inc(ln["chain"], 1)
    dve.wait_ge(ln["chain"], 3)
    dve.tensor_scalar(v["newton"][:], v["newton"][:], -0.5, 1.5, ALU.mult, ALU.add).then_inc(ln["chain"], 1)
    dve.wait_ge(ln["chain"], 4)
    dve.tensor_tensor(v["rstd"][:], v["rstd0"][:], v["newton"][:], ALU.mult).then_inc(ln["chain"], 1)
    dve.wait_ge(ln["chain"], 5)
    dve.scalar_tensor_tensor(v["shift"][:], v["moments"][:, :, 0], -1.0, v["rstd"][:], ALU.mult,
                             ALU.mult).then_inc(ln["chain"], 1)
    dve.wait_ge(ln["chain"], 6)


def ln_scale_act(act, v, ln):
    act.wait_ge(ln["var_ready"], 1)
    act.activation(v["root"][:], v["vareps"][:], ACT.Sqrt).then_inc(ln["root_ready"], 1)


def apply_ln(dve, v, out, b, sem, by_place=False):
    src = v["x"][:, bass.ds(b, 1), :]
    if by_place:
        src = src.rearrange("p o (h d) -> p (o h) d", h=H)
        out = out.rearrange("p o (d h) -> p (o h) d", h=H)
    dve.tensor_scalar(out, src, v["rstd"][:, bass.ds(b, 1)], v["shift"][:, bass.ds(b, 1)],
                      ALU.mult, ALU.add).then_inc(sem, 1)


UPDATES = 6


def update_x(dve, v, n, add, passed, upd):
    base = UPDATES * n
    wait(dve, upd, base)
    xs = v["x"][:, bass.ds(n * 2, 2), :]
    dve.tensor_tensor(xs, xs, add, ALU.add).then_inc(upd, 1)
    for b in range(2):
        wait_alone(dve, passed, upd, base + 1)
        dve.bn_stats(v["stats"][:, b, :], v["x"][:, bass.ds(n * 2 + b, 1), :]).then_inc(upd, 1)
    for b in range(2):
        wait_alone(dve, passed, upd, base + 2 + b)
        dve.bn_aggr(v["aggr"][:, b, :], v["stats"][:, b, :]).then_inc(upd, 1)
    dve.wait_ge(upd, base + 5)
    dve.tensor_copy(v["moments"][:, bass.ds(n * 2, 2), :], v["aggr"][:]).then_inc(upd, 1)


def setup_phase(nc, a, v):
    with ExitStack() as c:
        sem = c.enter_context(phase_semaphores(nc, "setup_"))
        passed = {eng: sem("passed_" + eng) for eng in ("dve", "pool", "sp")}
        stats = c.enter_context(nc.sbuf_tensor("xstats", [P, B, 6], F32))
        maskrow = c.enter_context(nc.sbuf_tensor("maskrow", [B, 4, S], F32))
        maskpart = c.enter_context(nc.sbuf_tensor("maskpart", [B, 3, S], BF16))
        x_loaded = [sem(f"x_loaded{i}") for i in range(4)]
        small_loaded = sem("small_loaded")
        ident_zero, ident_ready, masks_zero, masks_ready = (sem("ident_zero"), sem("ident_ready"),
                                                            sem("masks_zero"), sem("masks_ready"))
        consts_ready = sem("consts_ready")
        stat_ready, mask_chain, mask_stored = sem("stat_ready"), sem("mask_chain"), sem("mask_stored")
        small = []
        for name in ["L0_attn_Wk", "L0_attn_Wv", "L1_xattn_Wq", "L1_xattn_Wk", "L1_xattn_Wv", "L0_xattn_wq",
                     "L0_xattn_wk", "L0_xattn_wv", "L0_xattn_wo", "L1_ffn_sw1", "L1_ffn_sw3", "L0_ffn_W_exp",
                     "router_t", "rope_cos", "rope_sin", "L0_attn_bk", "L1_xattn_bq", "L1_xattn_bk",
                     "L0_attn_bv", "L0_ffn_up_bias"]:
            small.append((v[name][:], a[name]))
        small.append((v["L0_attn_Wf"][:], a["L0_attn_Wf"].rearrange("(j p) d -> p j d", p=P)))
        small.append((v["L1_ffn_sw2"][:], a["L1_ffn_sw2"].rearrange("(j p) d -> p j d", p=P)))
        small.append((maskrow[:, 0, :], a["mask_Bx1x1xS2_ff0"].rearrange("b o t k -> b (o t k)")))
        for name in ["L0_attn_bf", "L1_xattn_bv", "L1_attn_bo", "L0_ffn_b_con", "L0_ffn_down_bias"]:
            small.append((v[name][:], a[name].rearrange("(o d) -> o d", o=1).to_broadcast([P, D])))
        small.append((v["L1_ffn_router_bias"][:],
                      a["L1_ffn_router_bias"].rearrange("(o d) -> o d", o=1).to_broadcast([P, NE])))

        block = c.enter_context(nc.Block())

        @block.sync
        def _(sp):
            xt = a["x"].rearrange("b t d -> t b d")
            for i in range(4):
                sp.dma_start(v["x"][:, 8 * i:8 * i + 8, :], xt[:, 8 * i:8 * i + 8, :]).then_inc(x_loaded[i], 16)
            for dst, src in small:
                sp.dma_start(dst, src).then_inc(small_loaded, 16)
            sp.wait_ge(small_loaded, 16 * len(small))
            sp.wait_ge(mask_chain, 6)
            sp.dma_start(a["mask_scratch"].rearrange("c b k -> b c k"), maskpart[:]).then_inc(mask_stored, 16)
            sp.wait_ge(mask_stored, 16)

        @block.gpsimd
        def _(pool):
            pool.memset(v["ident"][:], 0.0).then_inc(ident_zero, 1)
            pool.wait_ge(ident_zero, 1)
            pool.affine_select(out=v["ident"][:], in_=v["ident"][:], compare_op=ALU.not_equal, fill=1.0,
                               base=0, pattern=[[-1, P]], channel_multiplier=1).then_inc(ident_ready, 1)
            pool.memset(v["causal"][:], 0.0).then_inc(masks_zero, 1)
            pool.memset(v["causal_t"][:], 0.0).then_inc(masks_zero, 1)
            pool.wait_ge(masks_zero, 2)
            pool.affine_select(out=v["causal"][:], in_=v["causal"][:], compare_op=ALU.is_ge, fill=MASKED,
                               base=0, pattern=[[-1, S]], channel_multiplier=1).then_inc(masks_ready, 1)
            pool.affine_select(out=v["causal_t"][:], in_=v["causal_t"][:], compare_op=ALU.is_ge, fill=MASKED,
                               base=0, pattern=[[1, S]], channel_multiplier=-1).then_inc(masks_ready, 1)
            pool.memset(v["ones"][:], 1.0)
            pool.memset(v["ones_bf"][:], 1.0).then_inc(consts_ready, 1)
            pool.wait_ge(ident_ready, 1)
            pool.tensor_copy(v["ident_bf"][:], v["ident"][:]).then_inc(consts_ready, 1)
            pool.tensor_copy(v["ident_r"][:], v["ident"][:]).then_inc(consts_ready, 1)

        @block.vector
        def _(dve):
            for b in range(B):
                if b % 8 == 0:
                    dve.wait_ge(x_loaded[b // 8], 16)
                dve.bn_stats(stats[:, b, :], v["x"][:, b, :]).then_inc(stat_ready, 1)
            for b in range(B):
                dve.wait_ge(stat_ready, b + 1)
                dve.bn_aggr(v["moments"][:, b, :], stats[:, b, :]).then_inc(stat_ready, 1)
            dve.wait_ge(small_loaded, 16 * len(small))
            row = maskrow[:]
            dve.tensor_copy(maskpart[:, 0, :], row[:, 0, :]).then_inc(mask_chain, 1)
            dve.wait_ge(mask_chain, 1)
            dve.tensor_tensor(row[:, 1, :], row[:, 0, :], maskpart[:, 0, :], ALU.subtract).then_inc(mask_chain, 1)
            dve.wait_ge(mask_chain, 2)
            dve.tensor_copy(maskpart[:, 1, :], row[:, 1, :]).then_inc(mask_chain, 1)
            dve.wait_ge(mask_chain, 3)
            dve.tensor_tensor(row[:, 2, :], row[:, 1, :], maskpart[:, 1, :], ALU.subtract).then_inc(mask_chain, 1)
            dve.wait_ge(mask_chain, 4)
            dve.tensor_copy(maskpart[:, 2, :], row[:, 2, :]).then_inc(mask_chain, 2)
            for name in ["L0_xattn_wq", "L1_xattn_Wq", "L1_xattn_bq"]:
                dve.tensor_scalar(v[name][:], v[name][:], DH ** -0.5, None, ALU.mult)
            dve.tensor_tensor(v["ffn_bias"][:], v["L0_ffn_b_con"][:], v["L0_ffn_down_bias"][:], ALU.add)


def narrow_attention(nc, a, v, kind):
    own, cross = kind == "self", kind != "self"
    pre = {"self": "L0_attn", "cross0": "L0_xattn", "cross1": "L1_xattn"}[kind]
    wq = None if own else v[pre + ("_wq" if kind == "cross0" else "_Wq")]
    wk = v[{"self": "L0_attn_Wk", "cross0": "L0_xattn_wk", "cross1": "L1_xattn_Wk"}[kind]]
    wv = v[{"self": "L0_attn_Wv", "cross0": "L0_xattn_wv", "cross1": "L1_xattn_Wv"}[kind]]
    VW = FH // H if own else SLOT
    NV = 2 if own else 1
    with ExitStack() as c:
        sem = c.enter_context(phase_semaphores(nc, kind + "_"))
        by_parity = lambda name: [sem(f"{name}{i}") for i in range(2)]
        sb = lambda name, shape, dt=F32: c.enter_context(nc.sbuf_tensor(f"{kind}_{name}", shape, dt))
        bank = lambda name: c.enter_context(nc.psum_tensor(f"{kind}_{name}", [P, 512], F32))
        passed = {eng: sem("passed_" + eng) for eng in ("dve", "pool", "sp")}
        xn = sb("xn", [P, 2, 2, D])
        ctx = sb("ctx", [P, 2, 2, D]) if cross else None
        hT = sb("hT", [P, 2, 1 if own else 2, W2])
        qk = sb("qk", [P, 2, 2, W2])
        rest = sb("rest", [P, 2 * W2])
        part = sb("part", [P, 2, 2, 3, 2, S], BF16)
        qs = sb("qs", [P, 2, 2, H, S], BF16)
        ks = sb("ks", [P, 2, 2, H, S], BF16)
        vals = sb("vals", [P, 2, 2, H, VW])
        negmax = sb("negmax", [P, 2, 2, H])
        mrest = sb("mrest", [P, H])
        mpart = sb("mpart", [P, 2, 3 * H], BF16)
        mT = sb("mT", [3 * H, 2, 2, S], BF16)
        expT = sb("expT", [P, NG, G * S])
        recip = sb("recip", [P, 512])
        if kind == "cross0":
            mraw = sb("mraw", [P, 2, 2, S])
            mask_a = sb("mask_a", [P, 2, 2, 2, S], F32R)
            mask_b = sb("mask_b", [P, 2, 2, 2, S], F32R)
        if cross:
            oS = sb("oS", [P, 2, 512])
            on = sb("on", [P, 2, D])
            onT = sb("onT", [P, 2, S])
            v = dict(v, stats=sb("stats", [P, 2, 6]))
        scoreA = [bank("scoreA0"), bank("scoreA1")]
        scoreB = [bank("scoreB0"), bank("scoreB1")]
        turnb, projb = bank("turnb"), bank("projb")
        if own:
            unit_pair = [bank("units01"), bank("units23")]
        else:
            outb, endb = bank("outb"), bank("endb")
        ln = {k: sem(k) for k in ["var_ready", "root_ready", "chain"]}
        rows_set, vals_set, ones_rows = sem("rows_set"), sem("vals_set"), sem("ones_rows")
        ctx_loaded, mask_loaded = by_parity("ctx_loaded"), by_parity("mask_loaded")
        stacked = [by_parity("stacked_first"), by_parity("stacked_second")]
        m_rows = [by_parity("m_rows_first"), by_parity("m_rows_second")]
        scr_written = sem("scr_written")
        ln_done, x_pre, x_mid = sem("ln_done"), sem("x_pre"), sem("x_mid")
        xT_ready, hT_ready, qk_psum, qk_ready = sem("xT_ready"), sem("hT_ready"), sem("qk_psum"), sem("qk_ready")
        part1, pool_split, part3 = sem("part1"), sem("pool_split"), sem("part3")
        v_psum, v_ready = sem("v_psum"), sem("v_ready")
        a_ready, max_done, pool_msplit, mpart_ready, mT_psum, mT_ready = (
            sem("a_ready"), sem("max_done"), sem("pool_msplit"), sem("mpart_ready"), sem("mT_psum"), sem("mT_ready"))
        b_ready, exp_done, pv_done = sem("b_ready"), sem("exp_done"), sem("pv_done")
        recip_done, norm_done = sem("recip_done"), sem("norm_done")
        o_copied, nat_ready, onT_psum, onT_ready, y_ready, upd = (
            sem("o_copied"), sem("nat_ready"), sem("onT_psum"), sem("onT_ready"), sem("y_ready"), sem("upd"))
        mask_high, mask_split, mask_turned, mask_copied = (
            sem("mask_high"), sem("mask_split"), sem("mask_turned"), sem("mask_copied"))
        query_scratch, key_scratch = a["query_scratch"], a["key_scratch"]
        TERMS = [0, 3, 5]
        STORED = 16 * 4
        STACKED = 16 * (5 if kind == "cross1" else 4)

        block = c.enter_context(nc.Block())

        def lagged(t, u, lag):
            return (t - 3, u - lag) if u >= lag else (t - 4, u - lag + 8)

        @block.sync
        def _(sp):
            if cross:
                xt = a["ctx_1024"].rearrange("b t d -> t b d")
                mt = a["mask_Bx1xSxS2_ff0"].rearrange("b o q k -> q (b o) k")
            ones = v["ones_bf"][0:3, 0:S].unsqueeze(1).to_broadcast([3, H, S])
            sp.wait_ge(rows_set, 2)
            for p in range(2):
                for b in range(2):
                    sp.dma_start(ks[MAIN:MAIN + 3, p, b, :, :], ones).then_inc(ones_rows, 16)
                    if kind == "cross1":
                        sp.dma_start(qs[48:51, p, b, :, :], ones).then_inc(ones_rows, 16)
            sp.wait_ge(ones_rows, 16 * (8 if kind == "cross1" else 4))

            def stack(n, q, b):
                sp.dma_start(qs[0:48, q, b, :, :].rearrange("p h t -> p (h t)"),
                             query_scratch[q, :, b].rearrange("c d h t -> c d (h t)")).then_inc(stacked[b][q], 16)
                for k in range(3):
                    m = 3 - k
                    r = 8 * TERMS[k]
                    sp.dma_start(ks[r:r + 8 * m, q, b, :, :].rearrange("p h t -> p (h t)"),
                                 key_scratch[q, k:k + 1, b].to_broadcast([m, DH, H, S]).rearrange(
                                     "m d h t -> m d (h t)")).then_inc(stacked[b][q], 16)
                if kind == "cross1":
                    sp.dma_start(ks[48:51, q, b, :, :], a["mask_scratch"][:, bass.ds(n * 2 + b, 1), :].to_broadcast(
                        [3, H, S])).then_inc(stacked[b][q], 16)

            def max_rows(k, p, b):
                sp.wait_ge(mT_ready, 2 * k + b + 1)
                sp.dma_start(qs[MAIN:MAIN + 3, p, b, :, :], mT[:, p, b, :]).then_inc(m_rows[b][p], 16)

            def step(t, p, has):
                q = 1 - p
                if cross and has(t):
                    wait(sp, xT_ready, t - 1)
                    sp.dma_start(ctx[:, p, :, :], xt[:, bass.ds(t * 2, 2), :]).then_inc(ctx_loaded[p], 16)
                    if kind == "cross0":
                        wait(sp, mask_split, t - 1)
                        sp.dma_start(mraw[:, p, :, :], mt[:, bass.ds(t * 2, 2), :]).then_inc(mask_loaded[p], 16)
                n, k = t - 1, t - 2
                if has(k):
                    wait(sp, b_ready, 8 * (k - 1))
                    stack(k, p, 1)
                if has(t - 3):
                    max_rows(t - 3, q, 1)
                if has(n):
                    sp.wait_ge(part3, n + 1)
                    for b in range(2):
                        wait(sp, stacked[b][q], of_parity(n - 2, q, STACKED))
                    for m, first in zip((3, 2, 1), TERMS):
                        sp.dma_start(query_scratch[q, first:first + m].rearrange("c b d h t -> (d h) (c b) t"),
                                     part[:, q, 0, 0:m, :, :].rearrange("p c b t -> p (c b) t")).then_inc(scr_written, 16)
                    sp.dma_start(key_scratch[q].rearrange("c b d h t -> (d h) (c b) t"),
                                 part[:, q, 1, :, :, :].rearrange("p c b t -> p (c b) t")).then_inc(scr_written, 16)
                    wait_alone(sp, passed["sp"], scr_written, STORED * (n + 1))
                    wait(sp, b_ready, 8 * (n - 1) - 4)
                    stack(n, q, 0)
                if has(k):
                    max_rows(k, p, 0)
            run_steps(sp, step, 4, 6)

        @block.gpsimd
        def _(pool):
            pool.memset(ks[:], 0.0).then_inc(rows_set, 1)
            if cross:
                pool.memset(vals[:], 0.0).then_inc(vals_set, 1)
                pool.wait_ge(vals_set, 1)
                pool.memset(vals[:, :, :, :, DH:DH + 1], 1.0).then_inc(vals_set, 1)

            def split_max(n, r, b):
                i = 2 * n + b
                whole, parts = negmax[:, r, b, :], [mpart[:, b, H * k:H * k + H] for k in range(3)]
                wait(pool, mT_psum, i - 1)
                wait_alone(pool, passed["pool"], max_done, 4 * i + 4)
                pool.tensor_scalar(parts[0], whole, 1.0, 0.0, ALU.mult, ALU.add).then_inc(pool_msplit, 1)
                wait(pool, mpart_ready, i)
                pool.wait_ge(pool_msplit, 3 * i + 1)
                pool.tensor_tensor(mrest[:], whole, parts[0], ALU.subtract).then_inc(pool_msplit, 1)
                wait_alone(pool, passed["pool"], pool_msplit, 3 * i + 2)
                pool.tensor_scalar(parts[1], mrest[:], 1.0, 0.0, ALU.mult, ALU.add).then_inc(pool_msplit, 1)
                pool.wait_ge(pool_msplit, 3 * i + 3)
                pool.tensor_tensor(parts[2], mrest[:], parts[1], ALU.subtract).then_inc(mpart_ready, 1)

            def step(t, p, has):
                q = 1 - p
                if has(t - 3):
                    split_max(t - 3, q, 1)
                n = t - 1
                if has(n):
                    by_seq = lambda k: part[:, q, :, k, :, :].rearrange("p s b t -> p s (b t)")
                    left = rest[:].rearrange("p (s t) -> p s t", s=2)
                    pool.wait_ge(part1, n + 1)
                    wait(pool, part3, n)
                    pool.tensor_tensor(left, qk[:, q, :, :], by_seq(0), ALU.subtract).then_inc(pool_split, 1)
                    wait_alone(pool, passed["pool"], pool_split, 2 * n + 1)
                    pool.tensor_scalar(by_seq(1), left, 1.0, 0.0, ALU.mult, ALU.add).then_inc(pool_split, 1)
                    pool.wait_ge(pool_split, 2 * n + 2)
                    pool.tensor_tensor(by_seq(2), left, by_seq(1), ALU.subtract).then_inc(part3, 1)
                if kind == "cross0" and has(n):
                    flat = lambda tile: tile.rearrange("p b k -> p (b k)")
                    pool.wait_ge(mask_high, n + 1)
                    pool.tensor_tensor(flat(mask_a[:, q, 1, :, :]), flat(mraw[:, q, :, :]),
                                       flat(mask_a[:, q, 0, :, :].bitcast(F32)), ALU.subtract).then_inc(mask_split, 1)
                if kind in ("self", "cross1") and has(t):
                    wait_alone(pool, passed["pool"], ln_done, 2 * (t + 1))
                    bias = v["L0_attn_bf" if own else "L1_xattn_bv"][:].unsqueeze(1).to_broadcast([P, 2, D])
                    xs = v["x"][:, bass.ds(t * 2, 2), :]
                    if own:
                        placed = xn[:, p, :, :].rearrange("p b (d h) -> p b h d", h=H)
                        heads = xs.rearrange("p b (h d) -> p b h d", h=H)
                        pool.tensor_tensor(heads, heads, placed, ALU.add).then_inc(x_mid, 1)
                        wait_alone(pool, passed["pool"], x_mid, t + 1)
                    pool.tensor_tensor(xs, xs, bias, ALU.add).then_inc(x_pre, 1)
                if has(t - 2):
                    split_max(t - 2, p, 0)
            run_steps(pool, step, 4, 6)

        @block.scalar
        def _(act):
            ln_scale_act(act, v, ln)

            def copy_turned_max(n, r, b):
                act.wait_ge(mT_psum, 2 * n + b + 1)
                wait(act, m_rows[b][r], of_parity(n - 2, r, 16))
                act.copy(mT[:, r, b, :], turnb[0:3 * H, b * S:(b + 1) * S]).then_inc(mT_ready, 1)

            def copy_out(n, b):
                act.wait_ge(pv_done, 8 * n + 4 * b + 4)
                wait(act, nat_ready, 2 * n + b - 1)
                act.copy(oS[:, b, :], outb[:]).then_inc(o_copied, 1)

            def copy_onT(n, b):
                act.wait_ge(onT_psum, 2 * n + b + 1)
                wait(act, y_ready, n)
                act.copy(onT[:, b, :], endb[:, 0:S]).then_inc(onT_ready, 1)

            def step(t, p, has):
                q = 1 - p
                n, k, m = t - 1, t - 2, t - 3
                for u in range(8):
                    e, j = lagged(t, u, 1)
                    if has(e):
                        act.wait_ge(b_ready, 8 * e + j + 1)
                        wait(act, pv_done, 8 * e + j - 3)
                        act.activation(expT[:, j % 4, :], scoreB[j % 2][:], ACT.Exp).then_inc(exp_done, 1)
                    if u == 0 and kind == "cross0" and has(n):
                        act.wait_ge(mask_loaded[q], of_parity(n, q, 16))
                        wait(act, a_ready, 8 * (n - 1))
                        wait(act, mask_turned, n - 1)
                        act.copy(mask_a[:, q, 0, :, :], mraw[:, q, :, :]).then_inc(mask_high, 1)
                    if u == 1:
                        if kind == "cross0" and has(k):
                            act.wait_ge(mask_turned, k + 1)
                            wait(act, b_ready, 8 * (k - 1))
                            act.copy(mask_b[:, p, :, :, :].rearrange("p c b k -> p (c b k)"), turnb[:]).then_inc(mask_copied, 1)
                        if has(m):
                            copy_turned_max(m, q, 1)
                    if cross and u == 2 and has(t - 4):
                        copy_out(t - 4, 1)
                    if own and u in (2, 3) and has(k):
                        b = u - 2
                        act.wait_ge(v_psum, 2 * k + b + 1)
                        act.copy(vals[:, p, b, :, :].rearrange("p h w -> p (h w)"), projb[:]).then_inc(v_ready, 1)
                    if cross and u == 2 and has(k):
                        act.wait_ge(v_psum, k + 1)
                        act.copy(vals[:, p, :, :, 0:DH], projb[:, 0:W2].rearrange("p (b h w) -> p b h w", b=2, h=H)).then_inc(v_ready, 1)
                    if kind == "cross0" and u in (0, 4) and has(t - 4):
                        copy_onT(t - 4, u // 4)
                    if u == 4 and has(t):
                        act.wait_ge(xT_ready, t + 1)
                        wait(act, v_psum, NV * (t - 1))
                        act.copy(hT[:, p, :, :].rearrange("p a t -> p (a t)"), turnb[:, 0:(W2 if own else 2 * W2)]).then_inc(hT_ready, 1)
                    if u == 5 and has(k):
                        copy_turned_max(k, p, 0)
                    if cross and u == 6 and has(m):
                        copy_out(m, 0)
                    if u == 6 and has(t):
                        act.wait_ge(qk_psum, t + 1)
                        wait(act, part3, t - 1)
                        if own:
                            act.copy(qk[:, p, 0, :], hT[:, p, 0, :])
                            act.activation(qk[:, p, 1, :], projb[:, W2:2 * W2], ACT.Identity,
                                           bias=v["L0_attn_bk"][:, 0:1]).then_inc(qk_ready, 1)
                        elif kind == "cross0":
                            act.copy(qk[:, p, :, :].rearrange("p a t -> p (a t)"), projb[:]).then_inc(qk_ready, 1)
                        else:
                            act.activation(qk[:, p, 0, :], projb[:, 0:W2], ACT.Identity, bias=v["L1_xattn_bq"][:, 0:1])
                            act.activation(qk[:, p, 1, :], projb[:, W2:2 * W2], ACT.Identity,
                                           bias=v["L1_xattn_bk"][:, 0:1]).then_inc(qk_ready, 1)
                        act.wait_ge(qk_ready, t + 1)
                        wait(act, scr_written, STORED * (t - 1))
                        act.copy(part[:, p, :, 0, :, :].rearrange("p s b t -> p s (b t)"), qk[:, p, :, :]).then_inc(part1, 1)
            if cross:
                act.wait_ge(vals_set, 2)
            run_steps(act, step, 4, 6)

        @block.vector
        def _(dve):
            dve.memset(qs[:], 0.0).then_inc(rows_set, 1)
            ln_scale_dve(dve, v, ln)

            def natural(n, b):
                o = endb[:].rearrange("p (h w) -> p h w", w=SLOT)
                i = 2 * n + b
                dve.wait_ge(nat_ready, i + 1)
                wait(dve, norm_done, i)
                if kind == "cross0":
                    wait(dve, onT_psum, i - 1)
                else:
                    wait(dve, upd, UPDATES * n)
                dve.reciprocal(recip[:, 0:H], o[:, :, DH]).then_inc(recip_done, 1)
                dve.wait_ge(recip_done, i + 1)
                dve.tensor_tensor(on[:, b, :].rearrange("p (h w) -> p h w", h=H), o[:, :, 0:DH],
                                  recip[:, 0:H].unsqueeze(2).to_broadcast([P, H, DH]), ALU.mult).then_inc(norm_done, 1)

            def normalise(n, b, half):
                i = 4 * n + 2 * b + half
                cols = slice(half * W2, (half + 1) * W2)
                dve.wait_ge(pv_done, 2 * i + 2)
                wait(dve, norm_done, i - 1)
                dve.reciprocal(recip[:, cols], unit_pair[half][:, W2:2 * W2]).then_inc(recip_done, 1)
                dve.wait_ge(recip_done, i + 1)
                dve.tensor_tensor(v["o_all"][:, bass.ds(n, 1), 2 * half:2 * half + 2, b * S:(b + 1) * S],
                                  unit_pair[half][:, 0:W2].rearrange("p (o j t) -> p o j t", o=1, j=2),
                                  recip[:, cols].rearrange("p (o j t) -> p o j t", o=1, j=2),
                                  ALU.mult).then_inc(norm_done, 1)

            def step(t, p, has):
                k = t - 2
                for u in range(8):
                    if has(k):
                        b, g = u // 4, u % 4
                        dve.wait_ge(a_ready, 8 * k + u + 1)
                        if g == 0:
                            wait(dve, mpart_ready, 2 * k + b - 3)
                        dve.tensor_reduce(negmax[:, p, b, G * g:G * g + G],
                                          scoreA[u % 2][:].rearrange("p (h k) -> p h k", h=G),
                                          AX.X, ALU.max, negate=True).then_inc(max_done, 1)
                    if own and u % 2 == 0:
                        n, j = lagged(t, u, 3)
                        if has(n):
                            normalise(n, j // 4, j % 4 // 2)
                    if cross and u == 3 and has(t - 4):
                        natural(t - 4, 1)
                    if u == (2 if own else 1) and has(t):
                        wait(dve, xT_ready, t - 1)
                        if own:
                            wait(dve, x_mid, t - 1)
                        for b in range(2):
                            apply_ln(dve, v, xn[:, p, b:b + 1, :], t * 2 + b, ln_done, by_place=own)
                    n = t - 4
                    if cross and has(n) and u == (6 if kind == "cross0" else 4):
                        if kind == "cross0":
                            dve.wait_ge(y_ready, n + 1)
                            add = endb[:, S:S + W2].rearrange("p (b d) -> p b d", b=2)
                        else:
                            dve.wait_ge(norm_done, 2 * n + 2)
                            dve.wait_ge(x_pre, n + 1)
                            add = on[:]
                        update_x(dve, v, n, add, passed["dve"], upd)
                    if cross and u == 7 and has(t - 3):
                        natural(t - 3, 0)
            run_steps(dve, step, 4, 6)

        @block.tensor
        def _(pe):
            ident, identb = v["ident"], v["ident_bf"]

            def mask_product(out, r, b, turned):
                if kind == "self":
                    m = v["causal_t" if turned else "causal"][:].unsqueeze(1).to_broadcast([P, G, S])
                    pe.matmul(out[:].rearrange("p (h k) -> p h k", h=G), identb[:], m, start=True, stop=False)
                elif kind == "cross0":
                    for k in range(2):
                        m = (mask_b if turned else mask_a)[:, r, k, b:b + 1, :].to_broadcast([P, G, S])
                        pe.matmul(out[:].rearrange("p (h k) -> p h k", h=G), v["ident_r"][:], m, start=(k == 0), stop=False)

            def scores(out, stationary, moving, rows, r, j, ready):
                b, g = j // 4, j % 4
                for i in range(G):
                    h = G * g + i
                    mm = pe.matmul(out[:, i * S:(i + 1) * S], stationary[0:rows, r, b, h, :], moving[0:rows, r, b, h, :],
                                   start=(kind == "cross1"), stop=(kind == "cross1" or i == G - 1))
                mm.then_inc(ready, 1)

            def score_a(n, r, j):
                if j == 0 and isinstance(n, int) and n == 0:
                    pe.wait_ge(ones_rows, 16 * (8 if kind == "cross1" else 4))
                if j % 4 == 0:
                    pe.wait_ge(stacked[j // 4][r], of_parity(n, r, STACKED))
                    if kind == "cross0":
                        pe.wait_ge(mask_split, n + 1)
                wait(pe, max_done, 8 * n + j - 1)
                mask_product(scoreA[j % 2], r, j // 4, False)
                scores(scoreA[j % 2], qs, ks, MAIN, r, j, a_ready)

            def score_b(n, r, j):
                if j % 4 == 0:
                    pe.wait_ge(m_rows[j // 4][r], of_parity(n, r, 16))
                    if kind == "cross0":
                        pe.wait_ge(mask_copied, n + 1)
                wait(pe, exp_done, 8 * n + j - 1)
                mask_product(scoreB[j % 2], r, j // 4, True)
                scores(scoreB[j % 2], ks, qs, P, r, j, b_ready)

            def weigh(n, r, j):
                b, g = j // 4, j % 4
                if j == 0:
                    pe.wait_ge(v_ready, NV * (n + 1))
                pe.wait_ge(exp_done, 8 * n + j + 1)
                if own and g % 2 == 0:
                    wait(pe, norm_done, 4 * n + j // 2 - 1)
                if cross and g == 0:
                    wait(pe, o_copied, 2 * n + b)
                out, at = (unit_pair[g // 2], g % 2 * S) if own else (outb, g * S)
                for i in range(G):
                    mm = pe.matmul(out[SLOT * i:SLOT * i + SLOT, at:at + S], vals[:, r, b, G * g + i, :],
                                   expT[:, g, i * S:(i + 1) * S], start=True, stop=True)
                if own:
                    for i in range(G):
                        mm = pe.matmul(out[SLOT * i:SLOT * i + SLOT, W2 + at:W2 + at + S], v["ones"][:, 0:SLOT],
                                       expT[:, g, i * S:(i + 1) * S], start=True, stop=True)
                mm.then_inc(pv_done, 1)

            def turn_max(n, b):
                pe.wait_ge(mpart_ready, 2 * n + b + 1)
                pe.matmul(turnb[0:3 * H, b * S:(b + 1) * S], mpart[:, b, :], identb[:], start=True, stop=True).then_inc(mT_psum, 1)

            def turn_out(n, b):
                pe.wait_ge(o_copied, 2 * n + b + 1)
                for j in range(NG):
                    mm = pe.transpose(endb[:, j * S:(j + 1) * S], oS[:, b, j * S:(j + 1) * S], ident[:])
                mm.then_inc(nat_ready, 1)

            def turn_normed(n, b):
                pe.wait_ge(norm_done, 2 * n + b + 1)
                pe.transpose(endb[:, 0:S], on[:, b, :], ident[:]).then_inc(onT_psum, 1)

            def turn_mask(p):
                for c in range(2):
                    for b in range(2):
                        at = (2 * c + b) * S
                        mm = pe.transpose(turnb[:, at:at + S], mask_a[:, p, c, b, :].bitcast(F32), ident[:])
                mm.then_inc(mask_turned, 1)

            def step(t, p, has):
                q = 1 - p
                n, k, m = t - 1, t - 2, t - 3
                for u in range(8):
                    if has(k):
                        score_a(k, p, u)
                    e, j = lagged(t, u, 3)
                    if has(e):
                        weigh(e, q if u >= 3 else p, j)
                    e, j = lagged(t, u, 1)
                    if has(e):
                        score_b(e, q if u >= 1 else p, j)
                    if u == 0 and kind == "cross0" and has(k):
                        if has(m):
                            pe.wait_ge(mT_ready, 2 * m + 1)
                        pe.wait_ge(mask_split, k + 1)
                        turn_mask(p)
                    if u == 1 and has(m):
                        pe.wait_ge(mT_ready, 2 * m + 1)
                        if kind == "cross0" and has(k):
                            pe.wait_ge(mask_copied, k + 1)
                        turn_max(m, 1)
                    if u in ((2, 3) if own else (2,)) and has(k):
                        b = u - 2
                        if b:
                            pe.wait_ge(v_ready, 2 * k + 1)
                        elif has(n):
                            pe.wait_ge(qk_ready, n + 1)
                        else:
                            pe.wait_ge(v_ready, NV * k)
                        if own:
                            pe.matmul(projb[:], hT[:, p, 0, b * S:(b + 1) * S], wv[:], start=True, stop=True).then_inc(v_psum, 1)
                        else:
                            for b in range(2):
                                mm = pe.matmul(projb[:, b * S:(b + 1) * S], hT[:, p, 1, b * S:(b + 1) * S], wv[:], start=True, stop=True)
                            mm.then_inc(v_psum, 1)
                    if u == 4 and has(t):
                        pe.wait_ge(ln_done, 2 * (t + 1))
                        if cross:
                            pe.wait_ge(ctx_loaded[p], of_parity(t, p, 16))
                        if has(m):
                            pe.wait_ge(mT_ready, 2 * m + 2)
                        else:
                            wait(pe, hT_ready, t)
                        if kind == "cross0" and has(k):
                            pe.wait_ge(mask_copied, k + 1)
                        for b in range(2):
                            mm = pe.transpose(turnb[:, b * S:(b + 1) * S], xn[:, p, b, :], ident[:])
                        if cross:
                            for b in range(2):
                                mm = pe.transpose(turnb[:, W2 + b * S:W2 + (b + 1) * S], ctx[:, p, b, :], ident[:])
                        mm.then_inc(xT_ready, 1)
                    if u == 5 and has(k):
                        if has(t):
                            pe.wait_ge(hT_ready, t + 1)
                        elif has(m):
                            pe.wait_ge(mT_ready, 2 * m + 2)
                        if kind == "cross0":
                            pe.wait_ge(mask_copied, k + 1)
                        turn_max(k, 0)
                    if u == 6 and has(t):
                        pe.wait_ge(hT_ready, t + 1)
                        wait(pe, v_ready, NV * (t - 1))
                        if own:
                            pe.matmul(projb[:, W2:2 * W2], wk[:], hT[:, p, 0, :], start=True, stop=True).then_inc(qk_psum, 1)
                        else:
                            pe.matmul(projb[:, 0:W2], wq[:], hT[:, p, 0, :], start=True, stop=True)
                            pe.matmul(projb[:, W2:2 * W2], wk[:], hT[:, p, 1, :], start=True, stop=True).then_inc(qk_psum, 1)
                    if cross and has(t - 4):
                        e = t - 4
                        if u == 0 and kind == "cross0":
                            turn_normed(e, 0)
                        if u == 3:
                            pe.wait_ge(onT_ready if kind == "cross0" else norm_done, 2 * e + 1)
                            turn_out(e, 1)
                        if u == 4 and kind == "cross0":
                            turn_normed(e, 1)
                        if u == 5 and kind == "cross0":
                            pe.wait_ge(onT_ready, 2 * e + 2)
                            for b in range(2):
                                mm = pe.matmul(endb[:, S + b * S:2 * S + b * S], onT[:, b, :], v["L0_xattn_wo"][:], start=True, stop=True)
                            mm.then_inc(y_ready, 1)
                    if cross and has(m):
                        if u == 7:
                            if kind == "cross0":
                                wait(pe, upd, UPDATES * (m - 1) + 1)
                            else:
                                wait(pe, norm_done, 2 * m)
                            turn_out(m, 0)
            run_steps(pe, step, 4, 6)


def gelu_projection(nc, a, v):
    with ExitStack() as c:
        sem = c.enter_context(phase_semaphores(nc, "wf_"))
        passed = {eng: sem("passed_" + eng) for eng in ("dve", "pool", "sp")}
        sb = lambda name, shape, dt=F32: c.enter_context(nc.sbuf_tensor("wf_" + name, shape, dt))
        g = sb("g", [P, 2, NJ, W2])
        stats = sb("stats", [P, 2, 6])
        v = dict(v, stats=stats)
        yb = [c.enter_context(nc.psum_tensor(f"wf_y{i}", [P, 512], F32)) for i in range(2)]
        g_ready, y_ready, upd = sem("g_ready"), sem("y_ready"), sem("upd")
        block = c.enter_context(nc.Block())

        @block.scalar
        def _(act):
            def step(t, p, has):
                if has(t):
                    wait(act, y_ready, t - 1)
                    for j in range(NJ):
                        act.activation(g[:, p, j:j + 1, :], v["o_all"][:, bass.ds(t, 1), j, :], ACT.Gelu,
                                       bias=v["L0_attn_bv"][:, j:j + 1]).then_inc(g_ready, 1)
            run_steps(act, step, 0)

        @block.tensor
        def _(pe):
            def step(t, p, has):
                if has(t):
                    wait(pe, upd, UPDATES * (t - 1))
                    pe.wait_ge(g_ready, NJ * (t + 1))
                    for b in range(2):
                        for j in range(NJ):
                            mm = pe.matmul(yb[p][:, b * D:(b + 1) * D], g[:, p, j, b * S:(b + 1) * S],
                                           v["L0_attn_Wf"][:, j, :], start=(j == 0), stop=(j == NJ - 1))
                    mm.then_inc(y_ready, 1)
            run_steps(pe, step, 0)

        @block.vector
        def _(dve):
            def step(t, p, has):
                if has(t):
                    dve.wait_ge(y_ready, t + 1)
                    update_x(dve, v, t, yb[p][:, 0:W2].rearrange("p (b d) -> p b d", b=2), passed["dve"], upd)
            run_steps(dve, step, 0)


def split_product(pe, out, stationary, moving, start=True, stop=True):
    pe.matmul(out, stationary[0], moving[0], start=start, stop=False)
    pe.matmul(out, stationary[0], moving[1], start=False, stop=False)
    return pe.matmul(out, stationary[1], moving[0], start=False, stop=stop)


STAGE = 3


def butterfly_stage(eng, k, tile, tmp, w, rows, loaded, chain, down):
    st = 8 - k if down else k
    s = 2 ** st
    src = tile[0:rows, k % 2, :].rearrange("p (n two s) -> p n two s", two=2, s=s)
    ws = w[0:rows, k % 2, :].rearrange("p (n s i j) -> p i j n s", s=s, i=2, j=2)
    eng.wait_ge(loaded[k % 2], 16 * (k // 2 + 1))
    if k:
        eng.wait_ge(chain, STAGE * k)
    for member in range(2):
        weight = ws[:, member, :] if down else ws[:, :, member]
        old = src[:, :, member, :].unsqueeze(1).to_broadcast([rows, 2, FH // 2 // s, s])
        product = tmp[0:rows, member, :].rearrange("p (n o s) -> p o n s", o=2, s=s)
        eng.tensor_tensor(product, old, weight, ALU.mult).then_inc(chain, 1)
    eng.wait_ge(chain, STAGE * k + 2)
    eng.tensor_tensor(tile[0:rows, (k + 1) % 2, :], tmp[0:rows, 0, :], tmp[0:rows, 1, :], ALU.add).then_inc(chain, 1)


def weights_phase(nc, a, v):
    with ExitStack() as c:
        sem = c.enter_context(phase_semaphores(nc, "bf_"))
        passed = {eng: sem("passed_" + eng) for eng in ("dve", "pool", "sp")}
        sb = lambda name, shape, dt=F32: c.enter_context(nc.sbuf_tensor("bf_" + name, shape, dt))
        up, down, row = sb("up", [P, 2, FH]), sb("down", [P, 2, FH]), sb("row", [1, 2, FH])
        w_up, w_down = sb("w_up", [P, 2, 2 * FH]), sb("w_down", [P, 2, 2 * FH])
        w_row = sb("w_row", [1, 2, 2 * FH])
        tmp, tmp_down, tmp_row = sb("tmp", [P, 2, FH]), sb("tmp_down", [P, 2, FH]), sb("tmp_row", [1, 2, FH])
        bank = c.enter_context(nc.psum_tensor("bf_bank", [P, 512], F32))
        bias_bank = c.enter_context(nc.psum_tensor("bf_bias", [P, 512], F32))
        up_loaded, down_loaded, row_loaded = [[sem(f"{n}_loaded{i}") for i in range(2)] for n in ("up", "down", "row")]
        up_chain, down_chain, row_chain = sem("up_chain"), sem("down_chain"), sem("row_chain")
        begun, b_loaded, turned, copied = sem("begun"), sem("b_loaded"), sem("turned"), sem("copied")
        con_loaded, rotary_loaded, late_loaded = sem("con_loaded"), sem("rotary_loaded"), sem("late_loaded")
        queries = ["L1_attn_bq", "L1_attn_bq_swapped"]
        split = ["wqT", "wqT_swapped", "wkT", "wkT_swapped", "wvT"]
        others = ["L1_attn_bk", "L1_attn_bk_swapped", "L1_attn_bv", "woT"]
        whole = sb("whole", [P, len(split), J1, P])
        highs = sem("highs")
        block = c.enter_context(nc.Block())

        def stage(name, st, rows):
            return a[name][st:st + 1].rearrange("o k i j -> o (k i j)").to_broadcast([rows, 2 * FH])

        @block.sync
        def _(sp):
            sp.dma_start(row[:, 0, :], a["L0_ffn_b_exp"].rearrange("(o d) -> o d", o=1)).then_inc(b_loaded, 16)
            for k in range(9):
                if k >= 2:
                    sp.wait_ge(up_chain, STAGE * (k - 1))
                sp.dma_start(w_up[:, k % 2, :], stage("L0_ffn_up_weights", k, P)).then_inc(up_loaded[k % 2], 16)
                if k >= 2:
                    sp.wait_ge(row_chain, STAGE * (k - 1))
                sp.dma_start(w_row[:, k % 2, :], stage("L0_ffn_up_weights", k, 1)).then_inc(row_loaded[k % 2], 16)
            for name in queries:
                sp.dma_start(v[name][:], a[name]).then_inc(rotary_loaded, 16)
            for i, name in enumerate(split):
                sp.dma_start(whole[:, i, :, :], a[name]).then_inc(rotary_loaded, 16)
            for name in others:
                sp.dma_start(v[name][:], a[name]).then_inc(late_loaded, 16)
            sp.dma_start(v["L1_ffn_ew1"][:], a["L1_ffn_ew1"].rearrange("e d h -> d e h")).then_inc(late_loaded, 16)
            sp.dma_start(v["L1_ffn_ew2"][:], a["L1_ffn_ew2"].rearrange("e h d -> h e d")).then_inc(late_loaded, 16)
            sp.wait_ge(late_loaded, 16 * (len(others) + 2))

        @block.scalar
        def _(act):
            def load_down(k):
                if k >= 2:
                    act.wait_ge(down_chain, STAGE * (k - 1))
                act.dma_start(w_down[:, k % 2, :], stage("L0_ffn_down_weights", 8 - k, P)).then_inc(down_loaded[k % 2], 16)
            act.dma_start(down[:, 0, :], a["con_t"]).then_inc(con_loaded, 16)
            load_down(0)
            load_down(1)
            for k in range(2, 9):
                load_down(k)
            act.wait_ge(rotary_loaded, 16 * (len(queries) + len(split)))
            for name in queries:
                act.activation(v[name][:], v[name][:], ACT.Copy, scale=HD1 ** -0.5)
            act.activation(whole[:, 0:2, :, :], whole[:, 0:2, :, :], ACT.Copy, scale=HD1 ** -0.5).then_inc(highs, 1)
            act.wait_ge(highs, 1)
            for i, name in enumerate(split):
                act.copy(v[name][:, 0, :, :], whole[:, i, :, :]).then_inc(highs, 1)
            act.wait_ge(turned, 1)
            act.copy(v["up_bias_row"][:], bias_bank[:, 0:NJ]).then_inc(copied, 1)
            act.wait_ge(turned, 2)
            act.copy(v["W_down"][:], bank[:].rearrange("p (j d) -> p j d", j=NJ)).then_inc(copied, 1)

        @block.vector
        def _(dve):
            dve.tensor_copy(up[:, 0, :], v["L0_ffn_W_exp"][:]).then_inc(begun, 1)
            dve.wait_ge(begun, 1)
            dve.wait_ge(con_loaded, 16)
            for k in range(9):
                butterfly_stage(dve, k, up, tmp, w_up, P, up_loaded, up_chain, False)
                butterfly_stage(dve, k, down, tmp_down, w_down, P, down_loaded, down_chain, True)
            dve.wait_ge(up_chain, STAGE * 9)
            dve.tensor_copy(v["W_up"][:], up[:, 1, :])
            for i, name in enumerate(split):
                dve.wait_ge(highs, i + 2)
                dve.tensor_tensor(v[name][:, 1, :, :], whole[:, i, :, :], v[name][:, 0, :, :].bitcast(F32), ALU.subtract)
            dve.wait_ge(copied, 1)
            dve.tensor_tensor(v["up_bias"][:], v["up_bias_row"][:], v["L0_ffn_up_bias"][:], ALU.add)

        @block.gpsimd
        def _(pool):
            pool.wait_ge(b_loaded, 16)
            for k in range(9):
                butterfly_stage(pool, k, row, tmp_row, w_row, 1, row_loaded, row_chain, False)

        @block.tensor
        def _(pe):
            pe.wait_ge(row_chain, STAGE * 9)
            for j in range(NJ):
                mm = pe.matmul(bias_bank[:, j:j + 1], row[:, 1, j * P:(j + 1) * P], v["ones"][0:1, 0:1], start=True, stop=True)
            mm.then_inc(turned, 1)
            pe.wait_ge(down_chain, STAGE * 9)
            for j in range(NJ):
                mm = pe.transpose(bank[:, j * P:(j + 1) * P], down[:, 1, j * P:(j + 1) * P], v["ident"][:])
            mm.then_inc(turned, 1)


def ffn_phase(nc, a, v):
    with ExitStack() as c:
        sem = c.enter_context(phase_semaphores(nc, "ffn_"))
        passed = {eng: sem("passed_" + eng) for eng in ("dve", "pool", "sp")}
        sb = lambda name, shape, dt=F32: c.enter_context(nc.sbuf_tensor("ffn_" + name, shape, dt))
        bank = lambda name: c.enter_context(nc.psum_tensor("ffn_" + name, [P, 512], F32))
        xn, hT, g = sb("xn", [P, 2, 2, D]), sb("hT", [P, 2, W2]), sb("g", [P, 2, NJ, W2])
        v = dict(v, stats=sb("stats", [P, 2, 6]))
        turnb, hidb, yb = [bank("turn0"), bank("turn1")], [bank("hid0"), bank("hid1")], [bank("y0"), bank("y1")]
        ln = {k: sem(k) for k in ["var_ready", "root_ready", "chain"]}
        ln_done, x_pre, xT_ready, hT_ready = sem("ln_done"), sem("x_pre"), sem("xT_ready"), sem("hT_ready")
        hid_ready, g_ready, y_ready, upd = sem("hid_ready"), sem("g_ready"), sem("y_ready"), sem("upd")
        block = c.enter_context(nc.Block())

        @block.gpsimd
        def _(pool):
            def step(t, p, has):
                if has(t):
                    wait_alone(pool, passed["pool"], ln_done, 2 * (t + 1))
                    xs = v["x"][:, bass.ds(t * 2, 2), :]
                    pool.tensor_tensor(xs, xs, v["ffn_bias"][:].unsqueeze(1).to_broadcast([P, 2, D]),
                                       ALU.add).then_inc(x_pre, 1)
            run_steps(pool, step, 0)

        @block.scalar
        def _(act):
            ln_scale_act(act, v, ln)

            def step(t, p, has):
                q = 1 - p
                if has(t):
                    act.wait_ge(xT_ready, t + 1)
                    wait(act, hid_ready, 2 * (t - 1))
                    act.copy(hT[:, p, :], turnb[p][:, 0:W2]).then_inc(hT_ready, 1)
                n = t - 1
                if has(n):
                    wait(act, y_ready, n - 1)
                    for j in range(NJ):
                        act.wait_ge(hid_ready, 2 * n + j // 2 + 1)
                        act.activation(g[:, q, j, :], hidb[j // 2][:, (j % 2) * W2:(j % 2 + 1) * W2], ACT.Gelu,
                                       bias=v["up_bias"][:, j:j + 1]).then_inc(g_ready, 1)
            run_steps(act, step, 2)

        @block.vector
        def _(dve):
            ln_scale_dve(dve, v, ln)

            def step(t, p, has):
                if has(t):
                    wait(dve, xT_ready, t - 1)
                    for b in range(2):
                        apply_ln(dve, v, xn[:, p, b:b + 1, :], t * 2 + b, ln_done)
                n = t - 2
                if has(n):
                    dve.wait_ge(y_ready, n + 1)
                    dve.wait_ge(x_pre, n + 1)
                    update_x(dve, v, n, yb[p][:, 0:W2].rearrange("p (b d) -> p b d", b=2), passed["dve"], upd)
            run_steps(dve, step, 2)

        @block.tensor
        def _(pe):
            def step(t, p, has):
                q = 1 - p
                if has(t):
                    pe.wait_ge(ln_done, 2 * (t + 1))
                    wait(pe, hT_ready, t - 1)
                    for b in range(2):
                        mm = pe.transpose(turnb[p][:, b * S:(b + 1) * S], xn[:, p, b, :], v["ident"][:])
                    mm.then_inc(xT_ready, 1)
                n = t - 2
                if has(n):
                    pe.wait_ge(g_ready, NJ * (n + 1))
                    wait(pe, upd, UPDATES * (n - 1))
                    for b in range(2):
                        for j in range(NJ):
                            mm = pe.matmul(yb[p][:, b * D:(b + 1) * D], g[:, p, j, b * S:(b + 1) * S],
                                           v["W_down"][:, j, :], start=(j == 0), stop=(j == NJ - 1))
                    mm.then_inc(y_ready, 1)
                n = t - 1
                if has(n):
                    pe.wait_ge(hT_ready, n + 1)
                    for j in range(NJ):
                        if j % 2 == 0:
                            wait(pe, g_ready, NJ * (n - 1) + j + 2)
                        mm = pe.matmul(hidb[j // 2][:, (j % 2) * W2:(j % 2 + 1) * W2], v["W_up"][:, j * P:(j + 1) * P],
                                       hT[:, q, :], start=True, stop=True)
                        if j % 2:
                            mm.then_inc(hid_ready, 1)
            run_steps(pe, step, 2)


def rotary_attention(nc, a, v):
    with ExitStack() as c:
        sem = c.enter_context(phase_semaphores(nc, "rot_"))
        passed = {eng: sem("passed_" + eng) for eng in ("dve", "pool", "sp")}
        sb = lambda name, shape, dt=F32: c.enter_context(nc.sbuf_tensor("rot_" + name, shape, dt))
        bank = lambda name: c.enter_context(nc.psum_tensor("rot_" + name, [P, 512], F32))
        xn = sb("xn", [P, 2, 2, D])
        hT = sb("hT", [P, 2, 2, W2], F32R)
        qT = sb("qT", [P, 2, J1, W2])
        kz = sb("kz", [P, 2, J1, 2, 2, S])
        cosp, sinp = sb("cosp", [P, 2, 2, W2]), sb("sinp", [P, 2, 2, W2])
        vals = sb("vals", [P, 2, 2, H * HD1])
        negmax, sums, inv = sb("negmax", [P, 4, G]), sb("sums", [P, 4, G]), sb("inv", [P, 4, G])
        probs, pT = sb("probs", [P, 4, G * S]), sb("pT", [P, 2, G * S])
        oT = sb("oT", [P, 2, J1, S])
        stats = sb("stats", [P, 6])
        qb, kb = bank("q"), bank("k")
        scoreb, turnb = [bank("score0"), bank("score1")], [bank("turn0"), bank("turn1")]
        outb, mixb = bank("out"), bank("mix")
        ln = {k: sem(k) for k in ["var_ready", "root_ready", "chain"]}
        kz_zero, ln_done, x_pre, xT_ready, hT_ready = (sem("kz_zero"), sem("ln_done"), sem("x_pre"),
                                                       sem("xT_ready"), sem("hT_ready"))
        hT_high = sem("hT_high")
        projected, mixed, q_rotated, k_rotated = sem("projected"), sem("mixed"), sem("q_rotated"), sem("k_rotated")
        v_psum, v_ready, a_ready, max_done, exp_done = (sem("v_psum"), sem("v_ready"), sem("a_ready"),
                                                        sem("max_done"), sem("exp_done"))
        inv_done, normed, turned, pT_ready, pv_done, o_ready, y_ready, upd = (
            sem("inv_done"), sem("normed"), sem("turned"), sem("pT_ready"), sem("pv_done"), sem("o_ready"),
            sem("y_ready"), sem("upd"))
        block = c.enter_context(nc.Block())

        def unit(t, k, lag):
            return (t - 2, k - lag) if k >= lag else (t - 3, k - lag + 8)

        @block.gpsimd
        def _(pool):
            pool.memset(kz[:], 0.0).then_inc(kz_zero, 1)
            pool.wait_ge(kz_zero, 1)

            def step(t, p, has):
                q = 1 - p
                for k in range(8):
                    n = t - 1
                    if has(n):
                        cn = 8 * n + k
                        pool.wait_ge(mixed, 4 * cn + 4)
                        if k == 0:
                            wait(pool, a_ready, 8 * (n - 1))
                        for i in range(2):
                            r = slice(64 * i, 64 * i + 64)
                            if i == 1:
                                if k == 0:
                                    pool.wait_ge(x_pre, n + 1)
                                m, u = unit(t, k - 1, 1) if k else unit(t - 1, 7, 1)
                                if has(m):
                                    pool.wait_ge(normed, 8 * m + u + 1)
                            pool.tensor_tensor(kz[r, q, k, :, i, :], cosp[r, k % 2, 1, :].rearrange("p (b t) -> p b t", b=2),
                                               sinp[r, k % 2, 1, :].rearrange("p (b t) -> p b t", b=2),
                                               ALU.add).then_inc(k_rotated, 1)
                    m, u = unit(t, k, 1)
                    if has(m):
                        un = 8 * m + u
                        pool.wait_ge(inv_done, un + 1)
                        if has(n):
                            pool.wait_ge(k_rotated, 2 * cn + 2)
                        pr = probs[:, u % 4, :].rearrange("p (h k) -> p h k", h=G)
                        pool.tensor_tensor(pr, pr, inv[:, u % 4, :].unsqueeze(2).to_broadcast([P, G, S]),
                                           ALU.mult).then_inc(normed, 1)
                if has(t):
                    wait_alone(pool, passed["pool"], ln_done, 2 * (t + 1))
                    if has(t - 1):
                        pool.wait_ge(k_rotated, 16 * t)
                    xs = v["x"][:, bass.ds(t * 2, 2), :]
                    pool.tensor_tensor(xs, xs, v["L1_attn_bo"][:].unsqueeze(1).to_broadcast([P, 2, D]),
                                       ALU.add).then_inc(x_pre, 1)
            run_steps(pool, step, 3)

        @block.scalar
        def _(act):
            ln_scale_act(act, v, ln)

            def step(t, p, has):
                q = 1 - p
                for k in range(8):
                    m, u = unit(t, k, 2)
                    if has(m):
                        un = 8 * m + u
                        act.wait_ge(turned, un + 1)
                        wait(act, pv_done, un - 1)
                        act.copy(pT[:, u % 2, :], turnb[u % 2][:]).then_inc(pT_ready, 1)
                    n = t - 2
                    if has(n):
                        un = 8 * n + k
                        act.wait_ge(max_done, un + 1)
                        wait(act, turned, un - 3)
                        wait(act, inv_done, un - 3)
                        for i in range(G):
                            act.activation(probs[:, k % 4, i * S:(i + 1) * S], scoreb[k % 2][:, i * S:(i + 1) * S],
                                           ACT.Exp, bias=negmax[:, k % 4, i:i + 1],
                                           accum_out=sums[:, k % 4, i:i + 1]).then_inc(exp_done, 1)
                    m, u = unit(t, k, 3)
                    if has(m) and u % 2:
                        act.wait_ge(pv_done, 8 * m + u + 1)
                        b, j0 = u // 4, (u % 4 - 1) * 2
                        if u % 4 == 1:
                            wait(act, y_ready, 2 * m + b - 1)
                        for i in range(4):
                            act.activation(oT[:, b, j0 + i, :], outb[:, i * S:(i + 1) * S], ACT.Identity,
                                           bias=v["L1_attn_bv"][:, j0 + i:j0 + i + 1]).then_inc(o_ready, 1)
                    n = t - 1
                    if has(n) and k < 4:
                        i = k
                        act.wait_ge(v_psum, 4 * n + i + 1)
                        act.copy(vals[:, q, i // 2, (i % 2) * 512:(i % 2 + 1) * 512], mixb[:]).then_inc(v_ready, 1)
                    if has(t) and k == 6:
                        act.wait_ge(xT_ready, t + 1)
                        act.copy(hT[:, p, 0, :], mixb[:, 0:W2]).then_inc(hT_high, 1)
            run_steps(act, step, 3)

        @block.vector
        def _(dve):
            ln_scale_dve(dve, v, ln)

            def add_y(n, b):
                k = 2 * n + b
                dve.wait_ge(y_ready, k + 1)
                dve.wait_ge(x_pre, n + 1)
                wait(dve, upd, 4 * k)
                xs = v["x"][:, bass.ds(n * 2 + b, 1), :]
                dve.tensor_tensor(xs, xs, mixb[:, 0:D].unsqueeze(1), ALU.add).then_inc(upd, 1)
                wait_alone(dve, passed["dve"], upd, 4 * k + 1)
                dve.bn_stats(stats[:], xs).then_inc(upd, 1)
                wait_alone(dve, passed["dve"], upd, 4 * k + 2)
                dve.bn_aggr(v["aggr"][:, 0, :], stats[:]).then_inc(upd, 1)
                dve.wait_ge(upd, 4 * k + 3)
                dve.tensor_copy(v["moments"][:, bass.ds(n * 2 + b, 1), :], v["aggr"][:, 0:1, :]).then_inc(upd, 1)

            def step(t, p, has):
                q = 1 - p
                for k in range(8):
                    n = t - 1
                    if has(n):
                        cn = 8 * n + k
                        dve.wait_ge(projected, cn + 1)
                        wait(dve, q_rotated, cn - 1)
                        wait(dve, k_rotated, 2 * (cn - 1))
                        for s, bk, bias in ((0, qb, "L1_attn_bq"), (1, kb, "L1_attn_bk")):
                            for dst, o, name, table in ((cosp, 0, bias, "rope_cos"), (sinp, W2, bias + "_swapped", "rope_sin")):
                                dve.scalar_tensor_tensor(
                                    dst[:, k % 2, s, :].rearrange("p (b t) -> p b t", b=2),
                                    bk[:, o:o + W2].rearrange("p (b t) -> p b t", b=2), v[name][:, k:k + 1],
                                    v[table][:].unsqueeze(1).to_broadcast([P, 2, S]), ALU.add, ALU.mult).then_inc(mixed, 1)
                    n = t - 2
                    if has(n):
                        un = 8 * n + k
                        dve.wait_ge(a_ready, un + 1)
                        dve.tensor_reduce(negmax[:, k % 4, :], scoreb[k % 2][:].rearrange("p (h k) -> p h k", h=G),
                                          AX.X, ALU.max, negate=True).then_inc(max_done, 1)
                    n = t - 1
                    if has(n):
                        cn = 8 * n + k
                        if k == 0:
                            wait(dve, a_ready, 8 * (n - 1))
                        dve.wait_ge(mixed, 4 * cn + 2)
                        dve.tensor_tensor(qT[:, q, k, :], cosp[:, k % 2, 0, :], sinp[:, k % 2, 0, :],
                                          ALU.add).then_inc(q_rotated, 1)
                    m, u = unit(t, k, 1)
                    if has(m):
                        un = 8 * m + u
                        dve.wait_ge(exp_done, 4 * un + 4)
                        wait(dve, normed, un - 3)
                        dve.reciprocal(inv[:, u % 4, :], sums[:, u % 4, :]).then_inc(inv_done, 1)
                    if k == 5 and has(t - 3):
                        add_y(t - 3, 1)
                    if k == 4 and has(t):
                        wait(dve, xT_ready, t - 1)
                        for b in range(2):
                            apply_ln(dve, v, xn[:, p, b:b + 1, :], t * 2 + b, ln_done)
                    if k == 7 and has(t):
                        dve.wait_ge(hT_high, t + 1)
                        dve.tensor_tensor(hT[:, p, 1, :], mixb[:, 0:W2], hT[:, p, 0, :].bitcast(F32), ALU.subtract).then_inc(hT_ready, 1)
                    if k == 7 and has(t - 2):
                        add_y(t - 2, 0)
            run_steps(dve, step, 3)

        @block.tensor
        def _(pe):
            ident, identb = v["ident"], v["ident_bf"]
            pe.wait_ge(kz_zero, 1)

            def out_projection(n, b):
                k = 2 * n + b
                pe.wait_ge(o_ready, 8 * (k + 1))
                for j in range(J1):
                    mm = pe.matmul(mixb[:, 0:D], oT[:, b, j, :], v["woT"][:, j, :], start=(j == 0), stop=(j == J1 - 1))
                mm.then_inc(y_ready, 1)

            def step(t, p, has):
                q = 1 - p
                m = t - 3
                n = t - 1
                for k in range(8):
                    if has(n):
                        cn = 8 * n + k
                        if k == 0:
                            pe.wait_ge(hT_ready, n + 1)
                        wait(pe, mixed, 4 * cn)
                        for bk, w in ((qb, "wqT"), (kb, "wkT")):
                            turned_x = [hT[:, q, i, :] for i in range(2)]
                            split_product(pe, bk[:, 0:W2], [v[w][:, i, k, :] for i in range(2)], turned_x)
                            mm = split_product(pe, bk[:, W2:2 * W2], [v[w + "_swapped"][:, i, k, :] for i in range(2)], turned_x)
                        mm.then_inc(projected, 1)
                    if has(t - 2):
                        un = 8 * (t - 2) + k
                        b, g = k // 4, k % 4
                        if k == 0:
                            pe.wait_ge(q_rotated, 8 * (t - 1))
                            pe.wait_ge(k_rotated, 16 * (t - 1))
                        wait(pe, exp_done, 4 * (un - 1))
                        out = scoreb[k % 2]
                        pe.matmul(out[:].rearrange("p (h k) -> p h k", h=G), identb[:],
                                  v["causal"][:].unsqueeze(1).to_broadcast([P, G, S]), start=True, stop=False)
                        for i in range(2):
                            j = 2 * g + i
                            mm = pe.matmul(out[:, i * W2:(i + 1) * W2], qT[:, p, j, b * S:(b + 1) * S],
                                           kz[:, p, j, b, :, :].rearrange("p h t -> p (h t)"), start=False, stop=(i == 1))
                        mm.then_inc(a_ready, 1)
                    l, u = unit(t, k, 2)
                    if has(l):
                        un = 8 * l + u
                        pe.wait_ge(normed, un + 1)
                        wait(pe, pT_ready, un - 1)
                        for i in range(G):
                            mm = pe.transpose(turnb[u % 2][:, i * S:(i + 1) * S], probs[:, u % 4, i * S:(i + 1) * S], ident[:])
                        mm.then_inc(turned, 1)
                    l, u = unit(t, k, 3)
                    if has(l):
                        un = 8 * l + u
                        r = p if k >= 3 else q
                        b, g = u // 4, u % 4
                        pe.wait_ge(pT_ready, un + 1)
                        if u == 0:
                            pe.wait_ge(v_ready, 4 * (l + 1))
                        if u % 2 == 0:
                            wait(pe, o_ready, 2 * un)
                        for i in range(G):
                            h = G * g + i
                            col = ((u % 2) * 2 + i // 2) * S
                            mm = pe.matmul(outb[64 * (i % 2):64 * (i % 2) + 64, col:col + S],
                                           vals[:, r, b, h * HD1:(h + 1) * HD1], pT[:, u % 2, i * S:(i + 1) * S],
                                           start=True, stop=True)
                        mm.then_inc(pv_done, 1)
                    if has(n) and k < 4:
                        i = k
                        if i == 0 and has(m):
                            pe.wait_ge(upd, 4 * (2 * m + 1))
                        if i:
                            pe.wait_ge(v_ready, 4 * n + i)
                        split_product(pe, mixb[:], [hT[:, q, c, (i // 2) * S:(i // 2 + 1) * S] for c in range(2)],
                                      [v["wvT"][:, c, (i % 2) * 4:(i % 2) * 4 + 4, :].rearrange("p j e -> p (j e)")
                                       for c in range(2)]).then_inc(v_psum, 1)
                    if k == 4 and has(m):
                        if has(n):
                            pe.wait_ge(v_ready, 4 * n + 4)
                        pe.wait_ge(upd, 4 * (2 * m + 1))
                        out_projection(m, 1)
                    if k == 6 and has(t):
                        if has(n):
                            pe.wait_ge(v_ready, 4 * n + 4)
                        if has(m):
                            pe.wait_ge(upd, 4 * (2 * m + 2))
                        pe.wait_ge(ln_done, 2 * (t + 1))
                        for b in range(2):
                            mm = pe.transpose(mixb[:, b * S:(b + 1) * S], xn[:, p, b, :], ident[:])
                        mm.then_inc(xT_ready, 1)
                    if k == 7 and has(t - 2):
                        if has(t):
                            pe.wait_ge(hT_ready, t + 1)
                        elif has(n):
                            pe.wait_ge(v_ready, 4 * n + 4)
                        if has(m):
                            pe.wait_ge(upd, 4 * (2 * m + 2))
                        out_projection(t - 2, 0)
            run_steps(pe, step, 3)


def router_phase(nc, a, v):
    E3 = [P, B, NE]
    with ExitStack() as c:
        sem = c.enter_context(phase_semaphores(nc, "rt_"))
        sb = lambda name, shape, dt=F32: c.enter_context(nc.sbuf_tensor("rt_" + name, shape, dt))
        bank = lambda name: c.enter_context(nc.psum_tensor("rt_" + name, [P, 512], F32))
        xn = sb("xn", [P, 2, 2, D])
        logits, score, sel = sb("logits", E3), sb("score", E3), sb("sel", E3)
        hit, key, rank, tmp = sb("hit", E3), sb("key", E3), sb("rank", E3), sb("tmp", E3)
        chosen = [sb("chosen0", E3), sb("chosen1", E3)]
        best, denom, big, inv = [sb(n, [P, B]) for n in ("best", "denom", "big", "inv")]
        turnb, logitb = [bank("turn0"), bank("turn1")], [bank("logit0"), bank("logit1")]
        ln = {k: sem(k) for k in ["var_ready", "root_ready", "chain"]}
        ln_done, xT_ready, hT_ready, logit_psum, logit_ready = (sem("ln_done"), sem("xT_ready"), sem("hT_ready"),
                                                                sem("logit_psum"), sem("logit_ready"))
        rank_ready, e_ready, g = sem("rank_ready"), sem("e_ready"), sem("gate")
        passed, low_done, high_ready = sem("passed"), sem("low_done"), sem("high_ready")
        two = sb("two", [P, 2, W2])
        split = ["L1_ffn_sw1", "L1_ffn_sw3", "L1_ffn_ew1"]
        block = c.enter_context(nc.Block())

        @block.gpsimd
        def _(pool):
            for e in range(NE):
                last = pool.memset(rank[:, :, e:e + 1], float(NE - e))
                last.then_inc(rank_ready, 1)

            def step(t, p, has):
                if has(t):
                    wait_alone(pool, passed, hT_ready, 2 * (t + 1))
                    high, low = [v["hT_all"][:, bass.ds(t, 1), k, :] for k in range(2)]
                    pool.tensor_tensor(low, two[:, p, :].unsqueeze(1), high.bitcast(F32), ALU.subtract).then_inc(low_done, 1)
            run_steps(pool, step, 0)
            for i, name in enumerate(split):
                pool.wait_ge(high_ready, i + 1)
                pool.tensor_tensor(v[name + "_halves"][:, 1], v[name][:], v[name + "_halves"][:, 0].bitcast(F32), ALU.subtract)

        @block.scalar
        def _(act):
            ln_scale_act(act, v, ln)

            def step(t, p, has):
                if has(t):
                    act.wait_ge(xT_ready, t + 1)
                    wait(act, low_done, t - 1)
                    act.copy(two[:, p, :], turnb[p][:, 0:W2]).then_inc(hT_ready, 1)
                    act.copy(v["hT_all"][:, bass.ds(t, 1), 0, :],
                             turnb[p][:, 0:W2].unsqueeze(1)).then_inc(hT_ready, 1)
            run_steps(act, step, 0)
            for name in split:
                act.copy(v[name + "_halves"][:, 0], v[name][:]).then_inc(high_ready, 1)
            act.wait_ge(logit_ready, NP)
            act.activation(score[:], logits[:], ACT.Exp, scale=-1.0).then_inc(e_ready, 1)

        @block.tensor
        def _(pe):
            def step(t, p, has):
                q = 1 - p
                if has(t):
                    pe.wait_ge(ln_done, 2 * (t + 1))
                    wait(pe, hT_ready, 2 * (t - 1))
                    for b in range(2):
                        mm = pe.transpose(turnb[p][:, b * S:(b + 1) * S], xn[:, p, b, :], v["ident"][:])
                    mm.then_inc(xT_ready, 1)
                n = t - 1
                if has(n):
                    pe.wait_ge(hT_ready, 2 * (n + 1))
                    wait(pe, logit_ready, n - 1)
                    for b in range(2):
                        mm = pe.matmul(logitb[q][:, b * NE:(b + 1) * NE], two[:, q, b * S:(b + 1) * S],
                                       v["router_t"][:], start=True, stop=True)
                    mm.then_inc(logit_psum, 1)
            run_steps(pe, step, 1)

        @block.vector
        def _(dve):
            ln_scale_dve(dve, v, ln)

            def step(t, p, has):
                q = 1 - p
                if has(t):
                    wait(dve, xT_ready, t - 1)
                    for b in range(2):
                        apply_ln(dve, v, xn[:, p, b:b + 1, :], t * 2 + b, ln_done)
                n = t - 2
                if has(n):
                    dve.wait_ge(logit_psum, n + 1)
                    dve.tensor_copy(logits[:, bass.ds(n * 2, 2), :],
                                    logitb[p][:, 0:2 * NE].rearrange("p (b e) -> p b e", b=2)).then_inc(logit_ready, 1)
            run_steps(dve, step, 2)
            dve.wait_ge(rank_ready, NE)
            dve.wait_ge(e_ready, 1)
            wide = lambda t: t[:].unsqueeze(2).to_broadcast(E3)
            dve.tensor_scalar(tmp[:], score[:], 1.0, None, ALU.add).then_inc(g, 1)
            dve.wait_ge(g, 1)
            dve.reciprocal(score[:], tmp[:]).then_inc(g, 1)
            dve.wait_ge(g, 2)
            dve.tensor_tensor(sel[:], score[:], v["L1_ffn_router_bias"][:].unsqueeze(1).to_broadcast(E3), ALU.add).then_inc(g, 1)
            n = 3
            for i in range(2):
                dve.wait_ge(g, n)
                dve.tensor_reduce(best[:], sel[:], AX.X, ALU.max).then_inc(g, 1)
                dve.wait_ge(g, n + 1)
                dve.tensor_tensor(hit[:], sel[:], wide(best), ALU.is_equal).then_inc(g, 1)
                dve.wait_ge(g, n + 2)
                dve.tensor_tensor(key[:], hit[:], rank[:], ALU.mult).then_inc(g, 1)
                dve.wait_ge(g, n + 3)
                dve.tensor_reduce(best[:], key[:], AX.X, ALU.max).then_inc(g, 1)
                dve.wait_ge(g, n + 4)
                dve.tensor_tensor(chosen[i][:], key[:], wide(best), ALU.is_equal).then_inc(g, 1)
                dve.wait_ge(g, n + 5)
                n += 5
                if i == 0:
                    dve.scalar_tensor_tensor(sel[:], chosen[0][:], MASKED, sel[:], ALU.mult, ALU.add).then_inc(g, 1)
                    n += 1
            dve.tensor_tensor(chosen[0][:], chosen[0][:], chosen[1][:], ALU.add).then_inc(g, 1)
            dve.wait_ge(g, n + 1)
            dve.tensor_tensor(tmp[:], score[:], chosen[0][:], ALU.mult).then_inc(g, 1)
            dve.wait_ge(g, n + 2)
            dve.tensor_reduce(denom[:], tmp[:], AX.X, ALU.add).then_inc(g, 1)
            dve.wait_ge(g, n + 3)
            dve.tensor_scalar(big[:], denom[:], 1e-9, None, ALU.is_gt).then_inc(g, 1)
            dve.tensor_scalar(denom[:], denom[:], 1e-9, None, ALU.add).then_inc(g, 1)
            dve.wait_ge(g, n + 5)
            dve.reciprocal(inv[:], denom[:]).then_inc(g, 1)
            dve.wait_ge(g, n + 6)
            dve.tensor_tensor(inv[:], inv[:], big[:], ALU.mult).then_inc(g, 1)
            dve.tensor_scalar(big[:], big[:], -0.5, 0.5, ALU.mult, ALU.add).then_inc(g, 1)
            dve.wait_ge(g, n + 8)
            dve.tensor_tensor(tmp[:], tmp[:], wide(inv), ALU.mult).then_inc(g, 1)
            dve.tensor_tensor(chosen[0][:], chosen[0][:], wide(big), ALU.mult).then_inc(g, 1)
            dve.wait_ge(g, n + 10)
            dve.tensor_tensor(v["gates"][:], tmp[:], chosen[0][:], ALU.add)


def experts_phase(nc, a, v):
    with ExitStack() as c:
        sem = c.enter_context(phase_semaphores(nc, "ex_"))
        passed = {eng: sem("passed_" + eng) for eng in ("dve", "pool", "sp")}
        sb = lambda name, shape, dt=F32: c.enter_context(nc.sbuf_tensor("ex_" + name, shape, dt))
        bank = lambda name: c.enter_context(nc.psum_tensor("ex_" + name, [P, 512], F32))
        th, up, act_in = sb("th", [P, 512]), sb("up", [P, 512]), sb("act_in", [P, 2, 512])
        g = sb("g", [P, 2, NE, W2])
        gateb, linb, hidb = bank("gate"), bank("lin"), [bank("hid0"), bank("hid1")]
        yb, sharedb = [bank("y0"), bank("y1")], bank("shared")
        shared_psum, tanh_done, silu_mid, act_ready = sem("shared_psum"), sem("tanh_done"), sem("silu_mid"), sem("act_ready")
        hid_psum, g_ready, y_psum, shared_y, upd, stored = (sem("hid_psum"), sem("g_ready"), sem("y_psum"),
                                                            sem("shared_y"), sem("upd"), sem("stored"))
        out = a["out"].rearrange("b t d -> t b d")
        UP = NE * 2 + 1
        block = c.enter_context(nc.Block())

        @block.sync
        def _(sp):
            def step(t, p, has):
                n = t - 1
                if has(n):
                    sp.wait_ge(upd, UP * (n + 1))
                    sp.dma_start(out[:, bass.ds(n * 2, 2), :], v["x"][:, bass.ds(n * 2, 2), :]).then_inc(stored, 16)
            run_steps(sp, step, 1)
            sp.wait_ge(stored, 16 * NP)

        @block.scalar
        def _(act):
            def step(t, p, has):
                if has(t):
                    act.wait_ge(shared_psum, t + 1)
                    wait(act, silu_mid, t)
                    act.activation(th[:], gateb[:], ACT.Tanh, scale=0.5).then_inc(tanh_done, 1)
                    wait(act, y_psum, 4 * (t - 1))
                    for i in range(NE // 2):
                        act.wait_ge(hid_psum, 4 * t + i + 1)
                        act.activation(g[:, p, 2 * i:2 * i + 2, :].rearrange("p e t -> p (e t)"), hidb[i % 2][:],
                                       ACT.Gelu).then_inc(g_ready, 1)
            run_steps(act, step, 0)

        @block.vector
        def _(dve):
            def step(t, p, has):
                q = 1 - p
                if has(t):
                    dve.wait_ge(tanh_done, t + 1)
                    wait(dve, act_ready, t)
                    dve.scalar_tensor_tensor(up[:], th[:], 1.0, gateb[:], ALU.add, ALU.mult).then_inc(silu_mid, 1)
                    dve.wait_ge(silu_mid, t + 1)
                    wait(dve, shared_y, t - 1)
                    dve.scalar_tensor_tensor(act_in[:, p, :], up[:], 0.5, linb[:], ALU.mult, ALU.mult).then_inc(act_ready, 1)
                n = t - 1
                if has(n):
                    k = UP * n
                    xs = v["x"][:, bass.ds(n * 2, 2), :]
                    dve.wait_ge(shared_y, n + 1)
                    wait(dve, upd, k)
                    dve.tensor_tensor(xs, xs, sharedb[:, 0:W2].rearrange("p (b d) -> p b d", b=2), ALU.add).then_inc(upd, 1)
                    for i in range(4):
                        dve.wait_ge(y_psum, 4 * n + i + 1)
                        for e in range(2):
                            for b in range(2):
                                if b == 0:
                                    dve.wait_ge(upd, k + 1 + 4 * i + 2 * e)
                                x1 = v["x"][:, bass.ds(n * 2 + b, 1), :]
                                gate = v["gates"][:, bass.ds(n * 2 + b, 1), 2 * i + e:2 * i + e + 1]
                                dve.scalar_tensor_tensor(
                                    x1, yb[i % 2][:, (2 * e + b) * D:(2 * e + b + 1) * D].unsqueeze(1),
                                    gate.rearrange("p a b -> p (a b)"), x1, ALU.mult, ALU.add).then_inc(upd, 1)
            run_steps(dve, step, 1)

        @block.tensor
        def _(pe):
            def step(t, p, has):
                q = 1 - p
                n = t - 1
                if has(t):
                    h = [v["hT_all"][:, bass.ds(t, 1), k, :].rearrange("p a t -> p (a t)") for k in range(2)]
                    halves = lambda name, at: [v[name + "_halves"][:, k][at] for k in range(2)]
                    wait(pe, act_ready, t)
                    for j in range(2):
                        split_product(pe, gateb[:, j * W2:(j + 1) * W2], halves("L1_ffn_sw1", (slice(None), slice(j * P, (j + 1) * P))), h)
                    for j in range(2):
                        mm = split_product(pe, linb[:, j * W2:(j + 1) * W2], halves("L1_ffn_sw3", (slice(None), slice(j * P, (j + 1) * P))), h)
                    mm.then_inc(shared_psum, 1)
                for i in range(4):
                    if has(t):
                        wait(pe, g_ready, 4 * t + i - 1)
                        for e in range(2):
                            mm = split_product(pe, hidb[i % 2][:, e * W2:(e + 1) * W2], halves("L1_ffn_ew1", (slice(None), 2 * i + e)), h)
                        mm.then_inc(hid_psum, 1)
                    if has(n):
                        if i == 0:
                            pe.wait_ge(act_ready, n + 1)
                            wait(pe, upd, UP * (n - 1) + 1)
                            for b in range(2):
                                for j in range(2):
                                    mm = pe.matmul(sharedb[:, b * D:(b + 1) * D], act_in[:, q, j * W2 + b * S:j * W2 + (b + 1) * S],
                                                   v["L1_ffn_sw2"][:, j, :], start=(j == 0), stop=(j == 1))
                            mm.then_inc(shared_y, 1)
                        pe.wait_ge(g_ready, 4 * n + i + 1)
                        wait(pe, upd, UP * n + 1 + 4 * (i - 1) if i >= 2 else UP * (n - 1) + 1 + 4 * (i + 3))
                        for e in range(2):
                            for b in range(2):
                                mm = pe.matmul(yb[i % 2][:, (2 * e + b) * D:(2 * e + b + 1) * D],
                                               g[:, q, 2 * i + e, b * S:(b + 1) * S], v["L1_ffn_ew2"][:, 2 * i + e, :],
                                               start=True, stop=True)
                        mm.then_inc(y_psum, 1)
            run_steps(pe, step, 1)


def rope_tables():
    theta = np.float32(10000.0) ** (np.arange(0, HD1, 2, dtype=np.float32) / np.float32(HD1))
    freqs = np.arange(S, dtype=np.float32)[:, None] * (np.float32(1.0) / theta)[None, :]
    emb = np.concatenate([freqs, freqs], axis=-1).astype(np.float64).T
    sign = np.where(np.arange(HD1) % 2 == 0, -1.0, 1.0)[:, None]
    return (np.tile(np.cos(emb), (2, 1)).astype(np.float32), np.tile(np.sin(emb) * sign, (2, 1)).astype(np.float32))


def laid_out(x):
    by_place = np.arange(D).reshape(H, DH).T.reshape(-1)
    partner = np.arange(H * HD1).reshape(-1, 2)[:, ::-1].reshape(-1)
    given = {name: x[name] for name in [
        "x", "ctx_1024", "mask_Bx1xSxS2_ff0", "mask_Bx1x1xS2_ff0", "L0_attn_Wf", "L0_attn_bf",
        "L0_ffn_W_exp", "L0_ffn_b_exp", "L0_ffn_up_weights", "L0_ffn_down_weights", "L0_ffn_b_con",
        "L0_ffn_down_bias", "L1_attn_bo", "L1_xattn_Wv", "L1_xattn_bv", "L1_ffn_router_bias", "L1_ffn_sw1",
        "L1_ffn_sw3", "L1_ffn_sw2", "L1_ffn_ew1", "L1_ffn_ew2"]}
    given["L0_attn_Wk"] = x["L0_attn_Wk"][by_place][:, by_place]
    given["L0_attn_Wv"] = x["L0_attn_Wv"][by_place]
    for name in ["L1_xattn_Wq", "L1_xattn_Wk"]:
        given[name] = x[name][:, by_place]
    for name in ["L0_xattn_wq", "L0_xattn_wk"]:
        given[name] = x[name].reshape(D, D)[:, by_place]
    given["L0_xattn_wv"] = x["L0_xattn_wv"].reshape(D, D)
    given["L0_xattn_wo"] = x["L0_xattn_wo"].reshape(D, D)
    for name in ["L0_attn_bk", "L1_xattn_bq", "L1_xattn_bk"]:
        given[name] = x[name][by_place].reshape(D, 1)
    for name in ["L0_attn_bv", "L0_ffn_up_bias"]:
        given[name] = x[name].reshape(NJ, P).T
    for name in ["L1_attn_bq", "L1_attn_bk", "L1_attn_bv"]:
        given[name] = x[name].reshape(J1, P).T
    for name in ["L1_attn_bq", "L1_attn_bk"]:
        given[name + "_swapped"] = x[name][partner].reshape(J1, P).T
    for name in ["wq", "wk", "wv"]:
        given[name + "T"] = x["L1_attn_" + name].T.reshape(D, J1, P)
    for name in ["wq", "wk"]:
        given[name + "T_swapped"] = x["L1_attn_" + name][partner].T.reshape(D, J1, P)
    given["woT"] = x["L1_attn_wo"].T.reshape(J1, P, D).transpose(1, 0, 2)
    given["con_t"] = x["L0_ffn_W_con"].T
    given["router_t"] = x["L1_ffn_router_w"].T
    given["rope_cos"], given["rope_sin"] = rope_tables()
    return {name: np.ascontiguousarray(value) for name, value in given.items()}


def build_program(nc, a):
    a = dict(a)
    a["query_scratch"] = nc.dram_tensor("query_scratch", [2, 6, 2, DH, H, S], BF16, kind="Internal").ap()
    a["key_scratch"] = nc.dram_tensor("key_scratch", [2, 3, 2, DH, H, S], BF16, kind="Internal").ap()
    a["mask_scratch"] = nc.dram_tensor("mask_scratch", [3, B, S], BF16, kind="Internal").ap()
    with ExitStack() as c:
        v = {}

        def keep(name, shape, dt=F32):
            v[name] = c.enter_context(nc.sbuf_tensor("v_" + name, shape, dt))
        keep("x", [P, B, D])
        for name in ["vareps", "root", "rstd0", "newton", "rstd", "shift"]:
            keep(name, [P, B])
        keep("moments", [P, B, 2])
        keep("aggr", [P, 2, 2])
        keep("ident", [P, P])
        keep("ident_bf", [P, P], BF16)
        keep("ident_r", [P, P], F32R)
        keep("causal", [P, S], BF16)
        keep("causal_t", [P, S], BF16)
        keep("ones", [P, SLOT])
        keep("ones_bf", [P, W2], BF16)
        for name in ["L0_attn_Wk", "L1_xattn_Wq", "L1_xattn_Wk", "L1_xattn_Wv", "L0_xattn_wq", "L0_xattn_wk",
                     "L0_xattn_wv", "L0_xattn_wo", "L0_attn_bf", "L1_xattn_bv", "L1_attn_bo", "L0_ffn_b_con",
                     "L0_ffn_down_bias", "ffn_bias", "rope_cos", "rope_sin"]:
            keep(name, [P, D])
        for name in ["L0_attn_Wv", "L0_ffn_W_exp", "W_up"]:
            keep(name, [P, FH])
        for name in ["L0_attn_Wf", "W_down"]:
            keep(name, [P, NJ, D])
        keep("L1_ffn_sw1", [P, SH])
        keep("L1_ffn_sw3", [P, SH])
        keep("L1_ffn_sw2", [P, SH // P, D])
        keep("router_t", [P, NE])
        keep("L1_ffn_router_bias", [P, NE])
        keep("gates", [P, B, NE])
        for name in ["L0_attn_bk", "L1_xattn_bq", "L1_xattn_bk"]:
            keep(name, [P, 1])
        for name in ["L0_attn_bv", "L0_ffn_up_bias", "up_bias", "up_bias_row"]:
            keep(name, [P, NJ])
        setup_phase(nc, a, v)
        with ExitStack() as own:
            v["o_all"] = own.enter_context(nc.sbuf_tensor("v_o_all", [P, NP, NJ, W2], F32))
            narrow_attention(nc, a, v, "self")
            gelu_projection(nc, a, v)
        narrow_attention(nc, a, v, "cross0")
        keep("L1_ffn_ew1", [P, NE, P])
        keep("L1_ffn_ew2", [P, NE, D])
        for name in ["wqT", "wkT", "wvT", "wqT_swapped", "wkT_swapped"]:
            keep(name, [P, 2, J1, P], F32R)
        keep("woT", [P, J1, P])
        for name in ["L1_attn_bq", "L1_attn_bk", "L1_attn_bv", "L1_attn_bq_swapped", "L1_attn_bk_swapped"]:
            keep(name, [P, J1])
        weights_phase(nc, a, v)
        ffn_phase(nc, a, v)
        rotary_attention(nc, a, v)
        narrow_attention(nc, a, v, "cross1")
        keep("hT_all", [P, NP, 2, W2], F32R)
        keep("L1_ffn_sw1_halves", [P, 2, SH], F32R)
        keep("L1_ffn_sw3_halves", [P, 2, SH], F32R)
        keep("L1_ffn_ew1_halves", [P, 2, NE, P], F32R)
        router_phase(nc, a, v)
        experts_phase(nc, a, v)


def kernel(**inputs):
    import concourse.bacc as bacc
    from concourse.bass_utils import run_bass_kernel_spmd

    nc = bacc.Bacc("TRN2", target_bir_lowering=False, num_devices=1)
    arrays, aps = {}, {}
    for name, value in laid_out(inputs).items():
        arrays["in_" + name] = value
        aps[name] = nc.dram_tensor("in_" + name, value.shape, mybir.dt.from_np(value.dtype), kind="ExternalInput").ap()
    aps["out"] = nc.dram_tensor("out_x", [B, S, D], F32, kind="ExternalOutput").ap()
    build_program(nc, aps)
    result = run_bass_kernel_spmd(nc, [arrays], core_ids=[0])
    return result.results[0]["out_x"]
```
